# Optimizing a Trainium2 kernel written in Bass

```python
import numpy as np
import jax
import jax.numpy as jnp

def _softmax(x, axis=-1):
    return jax.nn.softmax(x, axis=axis)

def _gelu(x):
    return jax.nn.gelu(x, approximate=True)

def _silu(x):
    return jax.nn.silu(x)

def _sigmoid(x):
    return jax.nn.sigmoid(x)

def _layernorm(x, axis=-1, eps=1e-05):
    m = jnp.mean(x, axis=axis, keepdims=True)
    v = jnp.var(x, axis=axis, keepdims=True)
    return (x - m) / jnp.sqrt(v + eps)

def _scatter_add(tgt, idx, src, axis=0):
    return tgt.at[idx].add(src)

def _segment_sum(src, seg, n):
    return jax.ops.segment_sum(src, seg, n)
kernel_name = 'mk_recurrent_d2_jaxref_r8_3aef9d'

def setup_inputs(seed: int=0):
    np.random.seed(seed)
    _w = jnp.asarray

    def _L0_attn_setup():
        import jax, jax.numpy as jnp
        import numpy as np
        B, L, D = (4, 256, 128)
        H, DK, DV = (4, 32, 32)
        CHUNK = 32
        MIN_FLOOR, MAX_FLOOR = (0.01, 0.1)
        EPS = 1e-05

        def _l2norm(x):
            return x * jax.lax.rsqrt(jnp.sum(x * x, -1, keepdims=True) + 1e-06)

        def _causal_dwconv(x, w):
            b, l, c = x.shape
            k = w.shape[-1]
            xt = jnp.transpose(x, (0, 2, 1))
            y = jax.lax.conv_general_dilated(xt, w[:, None, :], (1,), [(k - 1, 0)], dimension_numbers=('NCH', 'OIH', 'NCH'), feature_group_count=c)
            return jnp.transpose(y, (0, 2, 1))

        def _delta_rule_chunkwise(q, k, v, beta, chunk=CHUNK):
            b, h, l, dk = q.shape
            dv = v.shape[-1]
            q = _l2norm(q)
            k = _l2norm(k)
            v = v * beta[..., None]
            kb = k * beta[..., None]
            n = l // chunk
            resh = lambda t: t.reshape(b, h, n, chunk, t.shape[-1])
            q, k, v, kb = (resh(q), resh(k), resh(v), resh(kb))
            tri = jnp.triu(jnp.ones((chunk, chunk), bool))
            strict = jnp.triu(jnp.ones((chunk, chunk), bool), 1)
            att = jnp.where(tri, 0.0, -(kb @ jnp.swapaxes(k, -1, -2)))
            for i in range(1, chunk):
                upd = jnp.einsum('bhnj,bhnjk->bhnk', att[..., i, :], att)
                att = att.at[..., i, :i].add(upd[..., :i])
            att = att + jnp.eye(chunk, dtype=att.dtype)
            u = att @ v
            w = att @ kb

            def step(S, xs):
                q_i, k_i, u_i, w_i = xs
                local = jnp.where(strict, 0.0, q_i @ jnp.swapaxes(k_i, -1, -2))
                u_adj = u_i - w_i @ S
                o_i = q_i @ S + local @ u_adj
                return (S + jnp.swapaxes(k_i, -1, -2) @ u_adj, o_i)
            xs = tuple((jnp.moveaxis(t, 2, 0) for t in (q, k, u, w)))
            S0 = jnp.zeros((b, h, dk, dv), q.dtype)
            S, o = jax.lax.scan(step, S0, xs)
            return (jnp.moveaxis(o, 0, 2).reshape(b, h, l, dv), S)

        def _rmsnorm(x, w):
            return x * jax.lax.rsqrt(jnp.mean(x * x, -1, keepdims=True) + EPS) * w
        key = jax.random.key(seed)
        ks = jax.random.split(key, 16)
        s = 0.02
        return {'hidden_states': jax.random.normal(ks[0], (B, L, D), jnp.float32), 'W_q': jax.random.normal(ks[1], (D, H * DK), jnp.float32) * s, 'W_k': jax.random.normal(ks[2], (D, H * DK), jnp.float32) * s, 'W_v': jax.random.normal(ks[3], (D, H * DV), jnp.float32) * s, 'W_b': jax.random.normal(ks[4], (D, H), jnp.float32) * s, 'conv_w_q': jax.random.normal(ks[5], (H * DK, 4), jnp.float32) * 0.3, 'conv_w_k': jax.random.normal(ks[6], (H * DK, 4), jnp.float32) * 0.3, 'conv_w_v': jax.random.normal(ks[7], (H * DV, 4), jnp.float32) * 0.3, 'fir_short_w': jax.random.normal(ks[8], (H, DV, 3), jnp.float32) * 0.1, 'fir_long_w': jax.random.normal(ks[9], (H, DV, 31), jnp.float32) * 0.1, 'W_fuse1': jax.random.normal(ks[10], (D + 3 * H * DV, 2 * D), jnp.float32) * s, 'b_fuse1': jnp.zeros((2 * D,), jnp.float32), 'W_fuse2': jax.random.normal(ks[11], (2 * D, H * 4), jnp.float32) * s, 'b_fuse2': jnp.zeros((H * 4,), jnp.float32).at[3::4].set(4.0), 'others_log_tau': jnp.zeros((H,), jnp.float32), 'norm_w': jnp.ones((DV,), jnp.float32), 'W_o': jax.random.normal(ks[12], (H * DV, D), jnp.float32) * s}
    _L0_attn_in = _L0_attn_setup()

    def _L0_ffn_setup():
        import jax, jax.numpy as jnp
        import numpy as np
        B, S, DIM = (4, 256, 128)
        E, K, HID = (8, 2, 512)
        key = jax.random.key(seed)
        ks = jax.random.split(key, 8)
        init = lambda k, sh: jax.random.normal(k, sh, jnp.float32) * 0.02
        return {'x': jax.random.normal(ks[0], (B, S, DIM), jnp.float32), 'gate_w': init(ks[1], (DIM, E)), 'gate_b': jnp.zeros((E,), jnp.float32), 'w1': init(ks[2], (E, DIM, HID)), 'b1': jnp.zeros((E, HID), jnp.float32), 'w2': init(ks[3], (E, HID, DIM)), 'b2': jnp.zeros((E, DIM), jnp.float32), 'ws1': init(ks[4], (DIM, HID)), 'bs1': jnp.zeros((HID,), jnp.float32), 'ws2': init(ks[5], (HID, DIM)), 'bs2': jnp.zeros((DIM,), jnp.float32)}
    _L0_ffn_in = _L0_ffn_setup()

    def _L1_attn_setup():
        import jax, jax.numpy as jnp
        import numpy as np
        D_MODEL = 128
        B, S = (4, 256)
        key = jax.random.key(seed)
        k1, k2, k3 = jax.random.split(key, 3)
        scale = 1.0 / np.sqrt(D_MODEL)
        x = jax.random.normal(k1, (B, S, D_MODEL), dtype=jnp.float32)
        Wq = jax.random.normal(k2, (D_MODEL, D_MODEL), dtype=jnp.float32) * scale
        bq = jnp.zeros((D_MODEL,), dtype=jnp.float32)
        Wk = jax.random.normal(k3, (D_MODEL, D_MODEL), dtype=jnp.float32) * scale
        bk = jnp.zeros((D_MODEL,), dtype=jnp.float32)
        return {'x': x, 'Wq': Wq, 'bq': bq, 'Wk': Wk, 'bk': bk}
    _L1_attn_in = _L1_attn_setup()

    def _L1_ffn_setup():
        import jax, jax.numpy as jnp
        import numpy as np
        B, S, H = (2, 128, 128)
        KD, NH, K = (128, 8, 8)
        NE = 8192
        NK = 32
        EPS = 1e-05
        key = jax.random.key(seed)
        ks = jax.random.split(key, 5)
        inputs = jax.random.normal(ks[0], (B, S, H), jnp.float32)
        bn_gamma = jnp.ones((H,), jnp.float32)
        bn_beta = jnp.zeros((H,), jnp.float32)
        w_q = jax.random.normal(ks[1], (2 * NH * KD, H), jnp.float32) * (1.0 / np.sqrt(H))
        keys_p = jax.random.normal(ks[2], (NH, NK, 2, KD), jnp.float32) * 0.02
        lim = float(np.sqrt(6.0 / (NE + H)))
        down = jax.random.uniform(ks[3], (NE, H), jnp.float32, -lim, lim)
        up = jax.random.uniform(ks[4], (NE, H), jnp.float32, -lim, lim)
        return {'inputs': inputs, 'bn_gamma': bn_gamma, 'bn_beta': bn_beta, 'w_q': w_q, 'keys_p': keys_p, 'down': down, 'up': up}
    _L1_ffn_in = _L1_ffn_setup()
    _d = {'L0_attn_hidden_states': _L0_attn_in['hidden_states'], 'L0_attn_W_q': _L0_attn_in['W_q'], 'L0_attn_W_k': _L0_attn_in['W_k'], 'L0_attn_W_v': _L0_attn_in['W_v'], 'L0_attn_W_b': _L0_attn_in['W_b'], 'L0_attn_conv_w_q': _L0_attn_in['conv_w_q'], 'L0_attn_conv_w_k': _L0_attn_in['conv_w_k'], 'L0_attn_conv_w_v': _L0_attn_in['conv_w_v'], 'L0_attn_fir_short_w': _L0_attn_in['fir_short_w'], 'L0_attn_fir_long_w': _L0_attn_in['fir_long_w'], 'L0_attn_W_fuse1': _L0_attn_in['W_fuse1'], 'L0_attn_b_fuse1': _L0_attn_in['b_fuse1'], 'L0_attn_W_fuse2': _L0_attn_in['W_fuse2'], 'L0_attn_b_fuse2': _L0_attn_in['b_fuse2'], 'L0_attn_others_log_tau': _L0_attn_in['others_log_tau'], 'L0_attn_norm_w': _L0_attn_in['norm_w'], 'L0_attn_W_o': _L0_attn_in['W_o'], 'L0_ffn_gate_w': _L0_ffn_in['gate_w'], 'L0_ffn_gate_b': _L0_ffn_in['gate_b'], 'L0_ffn_w1': _L0_ffn_in['w1'], 'L0_ffn_b1': _L0_ffn_in['b1'], 'L0_ffn_w2': _L0_ffn_in['w2'], 'L0_ffn_b2': _L0_ffn_in['b2'], 'L0_ffn_ws1': _L0_ffn_in['ws1'], 'L0_ffn_bs1': _L0_ffn_in['bs1'], 'L0_ffn_ws2': _L0_ffn_in['ws2'], 'L0_ffn_bs2': _L0_ffn_in['bs2'], 'L1_attn_Wq': _L1_attn_in['Wq'], 'L1_attn_bq': _L1_attn_in['bq'], 'L1_attn_Wk': _L1_attn_in['Wk'], 'L1_attn_bk': _L1_attn_in['bk'], 'L1_ffn_bn_gamma': _L1_ffn_in['bn_gamma'], 'L1_ffn_bn_beta': _L1_ffn_in['bn_beta'], 'L1_ffn_w_q': _L1_ffn_in['w_q'], 'L1_ffn_keys_p': _L1_ffn_in['keys_p'], 'L1_ffn_down': _L1_ffn_in['down'], 'L1_ffn_up': _L1_ffn_in['up']}
    _x0 = _d['L0_attn_hidden_states']
    _d['L0_attn_hidden_states'] = jax.random.normal(jax.random.fold_in(jax.random.key(seed), 1), (8, 512, 128), dtype=_x0.dtype)
    del _x0
    return _d

def reference(L0_attn_hidden_states, L0_attn_W_q, L0_attn_W_k, L0_attn_W_v, L0_attn_W_b, L0_attn_conv_w_q, L0_attn_conv_w_k, L0_attn_conv_w_v, L0_attn_fir_short_w, L0_attn_fir_long_w, L0_attn_W_fuse1, L0_attn_b_fuse1, L0_attn_W_fuse2, L0_attn_b_fuse2, L0_attn_others_log_tau, L0_attn_norm_w, L0_attn_W_o, L0_ffn_gate_w, L0_ffn_gate_b, L0_ffn_w1, L0_ffn_b1, L0_ffn_w2, L0_ffn_b2, L0_ffn_ws1, L0_ffn_bs1, L0_ffn_ws2, L0_ffn_bs2, L1_attn_Wq, L1_attn_bq, L1_attn_Wk, L1_attn_bk, L1_ffn_bn_gamma, L1_ffn_bn_beta, L1_ffn_w_q, L1_ffn_keys_p, L1_ffn_down, L1_ffn_up):

    def _L0_attn_ref(hidden_states, W_q, W_k, W_v, W_b, conv_w_q, conv_w_k, conv_w_v, fir_short_w, fir_long_w, W_fuse1, b_fuse1, W_fuse2, b_fuse2, others_log_tau, norm_w, W_o):
        import jax, jax.numpy as jnp
        import numpy as np
        B, L, D = (4, 256, 128)
        H, DK, DV = (4, 32, 32)
        CHUNK = 32
        MIN_FLOOR, MAX_FLOOR = (0.01, 0.1)
        EPS = 1e-05

        def _l2norm(x):
            return x * jax.lax.rsqrt(jnp.sum(x * x, -1, keepdims=True) + 1e-06)

        def _causal_dwconv(x, w):
            b, l, c = x.shape
            k = w.shape[-1]
            xt = jnp.transpose(x, (0, 2, 1))
            y = jax.lax.conv_general_dilated(xt, w[:, None, :], (1,), [(k - 1, 0)], dimension_numbers=('NCH', 'OIH', 'NCH'), feature_group_count=c)
            return jnp.transpose(y, (0, 2, 1))

        def _delta_rule_chunkwise(q, k, v, beta, chunk=CHUNK):
            b, h, l, dk = q.shape
            dv = v.shape[-1]
            q = _l2norm(q)
            k = _l2norm(k)
            v = v * beta[..., None]
            kb = k * beta[..., None]
            n = l // chunk
            resh = lambda t: t.reshape(b, h, n, chunk, t.shape[-1])
            q, k, v, kb = (resh(q), resh(k), resh(v), resh(kb))
            tri = jnp.triu(jnp.ones((chunk, chunk), bool))
            strict = jnp.triu(jnp.ones((chunk, chunk), bool), 1)
            att = jnp.where(tri, 0.0, -(kb @ jnp.swapaxes(k, -1, -2)))
            for i in range(1, chunk):
                upd = jnp.einsum('bhnj,bhnjk->bhnk', att[..., i, :], att)
                att = att.at[..., i, :i].add(upd[..., :i])
            att = att + jnp.eye(chunk, dtype=att.dtype)
            u = att @ v
            w = att @ kb

            def step(S, xs):
                q_i, k_i, u_i, w_i = xs
                local = jnp.where(strict, 0.0, q_i @ jnp.swapaxes(k_i, -1, -2))
                u_adj = u_i - w_i @ S
                o_i = q_i @ S + local @ u_adj
                return (S + jnp.swapaxes(k_i, -1, -2) @ u_adj, o_i)
            xs = tuple((jnp.moveaxis(t, 2, 0) for t in (q, k, u, w)))
            S0 = jnp.zeros((b, h, dk, dv), q.dtype)
            S, o = jax.lax.scan(step, S0, xs)
            return (jnp.moveaxis(o, 0, 2).reshape(b, h, l, dv), S)

        def _rmsnorm(x, w):
            return x * jax.lax.rsqrt(jnp.mean(x * x, -1, keepdims=True) + EPS) * w
        b, l, d = hidden_states.shape
        q = jax.nn.silu(_causal_dwconv(hidden_states @ W_q, conv_w_q))
        k = jax.nn.silu(_causal_dwconv(hidden_states @ W_k, conv_w_k))
        v = jax.nn.silu(_causal_dwconv(hidden_states @ W_v, conv_w_v))
        q = q.reshape(b, l, H, DK)
        k = k.reshape(b, l, H, DK)
        v = v.reshape(b, l, H, DV)
        beta = jax.nn.sigmoid(hidden_states @ W_b)
        delta_out, _ = _delta_rule_chunkwise(jnp.transpose(q, (0, 2, 1, 3)), jnp.transpose(k, (0, 2, 1, 3)), jnp.transpose(v, (0, 2, 1, 3)), jnp.transpose(beta, (0, 2, 1)))
        delta_out = jnp.transpose(delta_out, (0, 2, 1, 3))
        vc = v.reshape(b, l, H * DV)
        fir_s = _causal_dwconv(vc, fir_short_w.reshape(H * DV, -1)).reshape(b, l, H, DV)
        fir_l = _causal_dwconv(vc, fir_long_w.reshape(H * DV, -1)).reshape(b, l, H, DV)
        gate_in = jnp.concatenate([hidden_states, fir_s.reshape(b, l, -1), fir_l.reshape(b, l, -1), delta_out.reshape(b, l, -1)], -1)
        hid = jax.nn.gelu(gate_in @ W_fuse1 + b_fuse1, approximate=False)
        logits = (hid @ W_fuse2 + b_fuse2).reshape(b, l, H, 4)
        p_raw = jax.nn.sigmoid(logits[..., 3])
        floor = MIN_FLOOR + (MAX_FLOOR - MIN_FLOOR) * (1.0 - p_raw)
        p_val = (1.0 - floor) * p_raw
        tau = jnp.exp(others_log_tau)
        others = jax.nn.softmax(logits[..., :3] / tau[None, None, :, None], -1)
        p_ctx = (1.0 - p_val)[..., None] * others
        o = p_ctx[..., 0:1] * fir_s + p_ctx[..., 1:2] * fir_l + p_ctx[..., 2:3] * delta_out + p_val[..., None] * v
        o = _rmsnorm(o, norm_w)
        return o.reshape(b, l, H * DV) @ W_o

    def _L0_ffn_ref(x, gate_w, gate_b, w1, b1, w2, b2, ws1, bs1, ws2, bs2):
        import jax, jax.numpy as jnp
        import numpy as np
        B, S, DIM = (4, 256, 128)
        E, K, HID = (8, 2, 512)
        orig_shape = x.shape
        xf = x.reshape(-1, DIM)
        logits = xf @ gate_w + gate_b
        top_w, top_i = jax.lax.top_k(logits, K)
        gw = jax.nn.softmax(top_w, axis=-1).astype(xf.dtype)
        combine = (gw[:, :, None] * jax.nn.one_hot(top_i, E, dtype=xf.dtype)).sum(axis=1)
        out = jnp.zeros_like(xf)
        for e in range(E):
            h = jax.nn.gelu(xf @ w1[e] + b1[e], approximate=False)
            out = out + combine[:, e:e + 1] * (h @ w2[e] + b2[e])
        shared = jax.nn.gelu(xf @ ws1 + bs1, approximate=False) @ ws2 + bs2
        return (out + shared).reshape(orig_shape)

    def _L1_attn_ref(x, Wq, bq, Wk, bk):
        import jax, jax.numpy as jnp
        import numpy as np
        D_MODEL = 128
        B, S = (4, 256)
        gamma_1 = 1.0
        gamma_2 = 1.0
        d_model = x.shape[-1]
        q = jnp.einsum('bsd,ed->bse', x, Wq) + bq
        k = jnp.einsum('bsd,ed->bse', x, Wk) + bk
        attn = jnp.einsum('bse,bte->bst', q, k) / np.sqrt(d_model)
        attn = jax.nn.softmax(attn, axis=-1)
        S_len = x.shape[1]
        eye = jnp.eye(S_len, dtype=x.dtype)
        attn = gamma_1 * eye[None, :, :] + attn
        mean = jnp.mean(attn, axis=-1, keepdims=True)
        attn = attn - gamma_2 * mean
        return jnp.einsum('bst,btd->bsd', attn, x)

    def _L1_ffn_ref(inputs, bn_gamma, bn_beta, w_q, keys_p, down, up):
        import jax, jax.numpy as jnp
        import numpy as np
        B, S, H = (2, 128, 128)
        KD, NH, K = (128, 8, 8)
        NE = 8192
        NK = 32
        EPS = 1e-05
        b, s, d = inputs.shape
        x = inputs.reshape(b * s, d)
        mean = x.mean(axis=0)
        var = x.var(axis=0)
        xn = (x - mean) * jax.lax.rsqrt(var + EPS) * bn_gamma + bn_beta
        xn = xn.reshape(b, s, d)
        q = (xn @ w_q.T).reshape(b, s, 2, NH, KD).transpose(2, 0, 1, 3, 4)
        sim = jnp.einsum('pbnhd,hkpd->pbnhk', q, keys_p)
        scores, idx = jax.lax.top_k(sim, K)
        all_scores = (scores[0][..., :, None] + scores[1][..., None, :]).reshape(b, s, NH, K * K)
        all_idx = (idx[0][..., :, None] * NK + idx[1][..., None, :]).reshape(b, s, NH, K * K)
        sc, pk = jax.lax.top_k(all_scores, K)
        indices = jnp.take_along_axis(all_idx, pk, axis=-1)
        wd = down[indices]
        hmid = jnp.einsum('bnd,bnhkd->bnhk', inputs, wd)
        hmid = jax.nn.sigmoid(sc) * jax.nn.gelu(hmid, approximate=False)
        wu = up[indices]
        return jnp.einsum('bnhk,bnhkd->bnd', hmid, wu)
    x = L0_attn_hidden_states
    xn = _layernorm(x, axis=-1)
    s = _L0_attn_ref(xn, L0_attn_W_q, L0_attn_W_k, L0_attn_W_v, L0_attn_W_b, L0_attn_conv_w_q, L0_attn_conv_w_k, L0_attn_conv_w_v, L0_attn_fir_short_w, L0_attn_fir_long_w, L0_attn_W_fuse1, L0_attn_b_fuse1, L0_attn_W_fuse2, L0_attn_b_fuse2, L0_attn_others_log_tau, L0_attn_norm_w, L0_attn_W_o)
    g = _silu(_L0_ffn_ref(xn, L0_ffn_gate_w, L0_ffn_gate_b, L0_ffn_w1, L0_ffn_b1, L0_ffn_w2, L0_ffn_b2, L0_ffn_ws1, L0_ffn_bs1, L0_ffn_ws2, L0_ffn_bs2))
    x = x + s * g
    xn = _layernorm(x, axis=-1)
    s = _L1_attn_ref(xn, L1_attn_Wq, L1_attn_bq, L1_attn_Wk, L1_attn_bk)
    g = _silu(_L1_ffn_ref(xn, L1_ffn_bn_gamma, L1_ffn_bn_beta, L1_ffn_w_q, L1_ffn_keys_p, L1_ffn_down, L1_ffn_up))
    x = x + s * g
    return x

_drawn_inputs = setup_inputs


def setup_inputs(seed=0):
    import zlib

    import numpy as np

    out = dict(_drawn_inputs(seed))
    spreads = {'L0_attn_b_fuse1': (0.0, 0.8),
     'L0_attn_others_log_tau': (0.0, 2.0),
     'L0_attn_norm_w': (1.0, 0.6),
     'L0_ffn_gate_b': (0.0, 0.8),
     'L0_ffn_b1': (0.0, 0.8),
     'L0_ffn_b2': (0.0, 0.8),
     'L0_ffn_bs1': (0.0, 0.8),
     'L0_ffn_bs2': (0.0, 0.71),
     'L1_attn_bq': (0.0, 0.8),
     'L1_attn_bk': (0.0, 2.0),
     'L1_ffn_bn_gamma': (1.0, 0.6),
     'L1_ffn_bn_beta': (0.0, 0.8)}
    factors = {'L0_attn_W_q': 8.0,
     'L0_attn_W_k': 8.0,
     'L0_attn_W_v': 3.503,
     'L0_attn_W_b': 8.0,
     'L0_attn_conv_w_q': 8.0,
     'L0_attn_conv_w_k': 8.0,
     'L0_attn_conv_w_v': 3.494,
     'L0_attn_fir_short_w': 8.0,
     'L0_attn_fir_long_w': 8.0,
     'L0_attn_W_fuse1': 8.0,
     'L0_attn_W_fuse2': 8.0,
     'L0_attn_b_fuse2': 8.0,
     'L0_attn_W_o': 3.454,
     'L0_ffn_gate_w': 7.038,
     'L0_ffn_w1': 8.0,
     'L0_ffn_w2': 8.0,
     'L0_ffn_ws1': 8.0,
     'L0_ffn_ws2': 8.0,
     'L1_attn_Wq': 8.0,
     'L1_attn_Wk': 8.0,
     'L1_ffn_w_q': 8.0,
     'L1_ffn_keys_p': 8.0,
     'L1_ffn_down': 8.0,
     'L1_ffn_up': 8.0}
    for name, (base, spread) in spreads.items():
        noise = np.random.default_rng([zlib.crc32(name.encode()), seed]).standard_normal(out[name].shape)
        drawn = base * np.exp(spread * noise) if base else spread * noise
        out[name] = jnp.asarray(drawn.astype(out[name].dtype))
    for name, factor in factors.items():
        out[name] = (out[name] * factor).astype(out[name].dtype)
    return out
```

```python
from contextlib import ExitStack

import numpy as np

import concourse.bass as bass
from concourse import mybir

F32 = mybir.dt.float32
ALU = mybir.AluOpType
ACT = mybir.ActivationFunctionType
AX = mybir.AxisListType

NB, L, D = 8, 512, 128
TOK = NB * L
P = 128
TPB = L // P
NT = TOK // P
H, DK = 4, 32
C = 32
NCH = L // C
ITEMS = NB * NCH
PADV = 30
VW = PADV + L
E, HID = 8, 512
NX = E + 1
MB = HID // P
PH, NK, PK = 8, 32, 8
NE = NK * NK
EB = NE // P
EPS = 1e-5
MIN_FLOOR, MAX_FLOOR = 0.01, 0.1
CREDIT = 2


def shape_constants():
    p = np.arange(P)[:, None]
    c = np.arange(P)[None, :]
    i = np.arange(C)[None, :]
    parts = [
        p == c,
        p // C == c // C,
        np.ones((P, P)),
        p % C == i,
        -1.0 * (i > p % C),
        i >= p % C,
        np.broadcast_to(np.arange(E)[None, :] - E, (P, E)),
        np.full((P, 1), 1e-6), np.full((P, 1), EPS),
    ]
    return np.ascontiguousarray(np.concatenate([np.asarray(x, np.float32) for x in parts], 1))


O_ID, O_BLK, O_ONE, O_STK, O_GRAM, O_LOC, O_IOTA, O_E6, O_E5 = 0, 128, 256, 384, 416, 448, 480, 488, 489
NCONST = 490

SMALLS, SMALL = {}, 0
for _n, _w in (("cw", 12), ("fs", 3), ("fl", 31), ("bf1", 2), ("nw", 1), ("b1", NX * MB), ("bq", 1), ("bk", 1),
               ("gamma", 1), ("bbeta", 1)):
    SMALLS[_n] = (SMALL, _w)
    SMALL += _w


def gated_two_layer_kernel(nc, a, out, debug=None):
    ctx = ExitStack()
    with ctx:
        def sb(name, shape):
            return ctx.enter_context(nc.sbuf_tensor(name, shape, F32))

        def sem(name):
            return ctx.enter_context(nc.semaphore(name))

        con = sb("con", [P, NCONST])
        small = sb("small", [P, SMALL])
        rows = sb("rows", [P, 16 + H + E])
        xT = sb("xT", [P, TOK])
        stats = sb("stats", [P, NT, 6])
        mean = sb("mean", [P, NT])
        rstd = sb("rstd", [P, NT])
        lntmp = sb("lntmp", [P, 3, NT])
        wproj = sb("wproj", [P, 3, D])
        wo = sb("wo", [P, D])
        wb = sb("wb", [P, H])
        wf1 = sb("wf1", [P, 4, 2 * D])
        wf2 = sb("wf2", [P, 2, 16])
        gatew = sb("gatew", [P, E])
        b2 = sb("b2", [NX, D])
        acc = sb("acc", [P, NT, D])
        bnc_t = sb("bnc", [P, 4])
        scal = sb("scal", [P, 4 * NT + TPB * NX + H])
        ctT = sb("ctT", [NX, L])
        RA = sb("RA", [P, NT * D])
        RK = sb("RK", [P, ITEMS * 2 * C])
        RV = sb("RV", [P, NB * VW])
        RF = sb("RF", [P, 2 * TOK])
        RW = sb("RW", [P, 2 * NX * HID])
        RH = sb("RH", [P, 2 * MB * L])
        RP = sb("RP", [P, H * 16 * 16])
        beta_it = sb("beta_it", [P, H, C])
        gl = sb("gl", [P, NT, E])
        comb = sb("comb", [P, NT, NX])

        pb = [ctx.enter_context(nc.psum_tensor(f"bank{i}", [P, 512], F32)) for i in range(8)]

        ident = con[:, O_ID:O_ID + P]
        blocks = con[:, O_BLK:O_BLK + P]
        ones = con[:, O_ONE:O_ONE + P]
        stack = con[:, O_STK:O_STK + C]
        gl_mask = con[:, O_GRAM:O_GRAM + C]
        loc_mask = con[:, O_LOC:O_LOC + C]
        iota_e = con[:, O_IOTA:O_IOTA + E]
        eps6 = con[:, O_E6:O_E6 + 1]
        eps5 = con[:, O_E5:O_E5 + 1]

        def col(name, n=None):
            o, w = SMALLS[name]
            return small[:, o:o + w] if n is None else small[:, o + n:o + n + 1]

        x_in = RA[:, :].rearrange("p (t d) -> p t d", d=D)
        att = RA[:, :].rearrange("p (h j i) -> p h j i", h=H, j=C)
        dT = RA[:, :].rearrange("p (b l) -> p b l", b=NB)
        kq = RK[:, :].rearrange("p (n s c) -> p n s c", s=2, c=C)
        vT = RV[:, :].rearrange("p (b l) -> p b l", b=NB)
        firs = RF[:, 0:TOK].rearrange("p (b l) -> p b l", b=NB)
        firl = RF[:, TOK:2 * TOK].rearrange("p (b l) -> p b l", b=NB)
        w1 = RW[:, 0:NX * HID].rearrange("p (e n) -> p e n", e=NX)
        w2 = RW[:, NX * HID:].rearrange("p (e m d) -> p e m d", e=NX, m=MB)
        hT = RH[:, :].rearrange("p (r m l) -> p r m l", r=2, m=MB)

        beta_d = nc.dram_tensor("beta_d", (H, ITEMS, C), F32, kind="Internal").ap()
        gram_d = nc.dram_tensor("gram_d", (ITEMS, H, C, C), F32, kind="Internal").ap()
        inv_d = nc.dram_tensor("inv_d", (ITEMS, H, C, C), F32, kind="Internal").ap()
        lv_d = nc.dram_tensor("lv_d", (P, ITEMS, 2, C), F32, kind="Internal").ap()

        s = {}

        def S(name):
            if name not in s:
                s[name] = sem(name)
            return s[name]

        block = ctx.enter_context(nc.Block())
        x_d = a["x"].rearrange("(b q p) d -> b p q d", p=P, q=TPB)
        out_d = out.rearrange("(b q p) d -> b p q d", p=P, q=TPB)

        def seq(b, n=L):
            return bass.ds(b * n, n)

        def staggered(eng, lead, follow):
            lead(0, 0)
            with eng.Fori(0, (NB - 2) // 2) as pair:
                b = pair * 2
                for r in range(2):
                    lead(b + (r + 1), 1 - r)
                    follow(b + r, r)
            lead(NB - 1, 1)
            follow(NB - 2, 0)
            follow(NB - 1, 1)

        xst = RH[:, 0:2 * L].rearrange("p (r q d) -> p r q d", r=2, q=TPB)
        xs = RH[:, 2 * L:4 * L].rearrange("p (r l) -> p r l", r=2)
        top = RH[:, 4 * L:8 * L].rearrange("p (n x) -> p n x", n=8)
        beta_sb = acc[0:H, :, :].rearrange("p t d -> p (t d)")
        CW = 3 + L
        pads = RF[:, 0:6 * CW].rearrange("p (r s l) -> p r s l", r=2, s=3)
        cacc = RF[:, 6 * CW:6 * CW + 2 * 2 * L]
        cv0 = RF[:, 6 * CW:6 * CW + 3 * L].rearrange("p (s l) -> p s l", s=3)
        cv1 = RH[:, 5 * L:8 * L].rearrange("p (s l) -> p s l", s=3)
        cacc = [cv0, cv1]
        sq = RH[:, 0:4 * L].rearrange("p (r l) -> p r l", r=2)
        rn = RW[:, 0:4 * L].rearrange("p (r l) -> p r l", r=2)
        KX = RH[:, 0:2 * L].rearrange("p (r n c) -> p r n c", r=2, n=4)
        kv_in = RH[:, 2 * L:6 * L].rearrange("p (r s n c) -> p r s n c", r=2, s=2, n=NCH)
        kt = RH[:, 6 * L:8 * L].rearrange("p (r n c) -> p r n c", r=2, n=NCH)
        cst = RF[:, 0:2 * NCH * 3 * C].rearrange("p (r n s c) -> p r n s c", r=2, n=NCH, s=3)
        blocks4 = blocks.rearrange("p (h c) -> p h c", h=H)
        vtok = vT[:, :, PADV:VW]
        tw = scal[:, 0:4 * NT].rearrange("p (n t) -> p n t", n=4)
        cs = scal[:, 4 * NT:4 * NT + TPB * NX].rearrange("p (q e) -> p q e", q=TPB)
        itau = scal[:, 4 * NT + TPB * NX:4 * NT + TPB * NX + H]
        cT = ctT[:, :]
        SW = NB * P
        Kb = RW[:, 0:2 * SW].rearrange("p (r b c) -> p r b c", r=2, b=NB)
        Gb = RW[:, 2 * SW:4 * SW].rearrange("p (r b c) -> p r b c", r=2, b=NB)
        Wn = RW[:, 4 * SW:6 * SW].rearrange("p (r b c) -> p r b c", r=2, b=NB)
        Ub = RW[:, 6 * SW:7 * SW].rearrange("p (b c) -> p b c", b=NB)
        Sb = RW[:, 7 * SW:8 * SW].rearrange("p (b c) -> p b c", b=NB)
        U4 = RH[:, 0:NB * C].rearrange("p (b c) -> p b c", b=NB)
        S4 = RH[:, NB * C:2 * NB * C].rearrange("p (b c) -> p b c", b=NB)
        lv = RW[:, 8 * SW:8 * SW + 4 * NB * C].rearrange("p (r b s c) -> p r b s c", r=2, b=NB, s=2)
        kq5 = RK[:, :].rearrange("p (b n s c) -> p b n s c", b=NB, n=NCH, s=2)
        zero = RP[:, 0:NB * C]
        hidT = RH[:, 0:4 * L].rearrange("p (r m l) -> p r m l", r=2, m=2)
        lg = RH[:, 4 * L:5 * L].rearrange("p (t h c) -> p t h c", t=NT, h=H)
        PG = RH[:, 5 * L:6 * L].rearrange("p (t c h) -> p t c h", t=NT, c=4)
        ft = RH[:, 6 * L:8 * L].rearrange("p (n x) -> p n x", n=8)

        def ftx(k):
            return ft[:, k, :].rearrange("p (t h) -> p t h", h=H)

        def ft3(k):
            return RH[:, 6 * L + k * P:6 * L + (k + 3) * P].rearrange("p (t h c) -> p t h c", h=H, c=3)
        Pst = RW[:, 0:8 * L].rearrange("p (r q c d) -> p r q c d", r=2, q=TPB, c=4)
        mC = RW[:, 8 * L:12 * L].rearrange("p (c l) -> p c l", c=4)
        oT = RW[:, 12 * L:14 * L].rearrange("p (r l) -> p r l", r=2)
        sqo = RW[:, 14 * L:15 * L]
        rr = RW[:, 15 * L:16 * L]
        oN = RW[:, 16 * L:17 * L]
        xr = RW[:, 17 * L:18 * L].rearrange("p (q d) -> p q d", q=TPB)
        sgt = RP[:, 0:L].rearrange("p (q d) -> p q d", q=TPB)

        CONVC = 24
        ACCC = 8
        FIRS = [("s", 0), ("l", 0), ("s", 1), ("l", 1), ("s", 2)] + [("l", k) for k in range(2, 31)]

        def moments(dve, x, sems, loaded):
            v, var, std, done = sems
            if loaded:
                dve.wait_ge(S(loaded), 16)
            with dve.Fori(0, NB) as b:
                for q in range(TPB):
                    op = dve.bn_stats(stats[:, bass.ds(b * TPB + q, 1), :].squeeze(1),
                                      x[:, bass.ds(b * TPB + q, 1), :].squeeze(1))
                op.then_inc(S(v), 1)
            dve.wait_ge(S(v), NB)
            me, mo, se, so = (stats[:, :, k] for k in (1, 4, 2, 5))
            t0, t1, t2 = (lntmp[:, k, :] for k in range(3))
            dve.tensor_tensor(t0, me, mo, ALU.add).then_inc(S(v), 1)
            dve.tensor_tensor(t1, me, mo, ALU.subtract).then_inc(S(v), 1)
            dve.tensor_tensor(t2, se, so, ALU.add).then_inc(S(v), 1)
            dve.wait_ge(S(v), NB + 3)
            dve.tensor_scalar(mean[:, :], t0, 0.5, None, ALU.mult).then_inc(S(v), 1)
            dve.scalar_tensor_tensor(t1, t1, 0.25, t1, ALU.mult, ALU.mult).then_inc(S(v), 1)
            dve.wait_ge(S(v), NB + 5)
            dve.scalar_tensor_tensor(t1, t2, 1.0 / D, t1, ALU.mult, ALU.add).then_inc(S(var), 1)
            dve.wait_ge(S(std), 1)
            dve.reciprocal(rstd[:, :], rstd[:, :]).then_inc(S(done), 1)
            dve.wait_ge(S(done), 1)

        def normed(dve, dst, x, t):
            return dve.tensor_scalar(dst, x[:, bass.ds(t, 1), :].squeeze(1), mean[:, bass.ds(t, 1)],
                                     rstd[:, bass.ds(t, 1)], ALU.subtract, ALU.mult)


        xn2 = RA[:, :].rearrange("p (t d) -> p t d", d=D)
        s1 = RF[:, 0:TOK].rearrange("p (t d) -> p t d", d=D)
        o2 = RF[:, TOK:2 * TOK].rearrange("p (t d) -> p t d", d=D)
        wqk = RK[:, 0:2048].rearrange("p (n d) -> p n d", n=2 * PH)
        Wt = RK[:, 0:2048].rearrange("p (r e n) -> p r e n", r=2, e=EB)
        keys = RK[:, 2048:2560].rearrange("p (n k) -> p n k", n=2 * PH)
        down = RK[:, 2560:3584]
        up = RK[:, 3584:4608].rearrange("p (e d) -> p e d", e=EB)
        aWq = RK[:, 4608:4736]
        aWk = RK[:, 4736:4864]
        WK = RK[:, 5120:5632]
        xb = RK[:, 6144:7168].rearrange("p (r l) -> p r l", r=2)
        qk = RW[:, 0:2048].rearrange("p (r s l) -> p r s l", r=2, s=2)
        Pr = RW[:, 2048:3072].rearrange("p (r l) -> p r l", r=2)
        PT = RW[:, 3072:4096].rearrange("p (r n s) -> p r n s", r=2, n=TPB)
        xsum = RW[:, 4096:4352].rearrange("p (r d) -> p r d", r=2)
        atmp = RW[:, 4352:4608].rearrange("p (r d) -> p r d", r=2)
        ac = RW[:, 4608:4624].rearrange("p (r n) -> p r n", r=2)
        bqs = lntmp[:, 0, 0:1]
        bnst = lntmp[:, 1:3, :].rearrange("p a b -> p (a b)")[:, 0:6 * NB]
        bnc = bnc_t[:, :]
        RING = 4
        Z = RW[:, 0:4096].rearrange("p (k e) -> p k e", k=RING)
        SG = RW[:, 4096:8192].rearrange("p (k e) -> p k e", k=RING)
        MK = RV[:, 0:4096].rearrange("p (k e) -> p k e", k=RING)
        sim = RW[:, 8192:9216].rearrange("p (r h s k) -> p r h s k", r=2, h=PH, s=2)
        cand = RP[:, 0:512].rearrange("p (h a b) -> p h a b", h=PH, a=PK)
        tv = RP[:, 512:768].rearrange("p (r h s k) -> p r h s k", r=2, h=PH, s=2)
        t8 = RP[:, 768:896].rearrange("p (r h k) -> p r h k", r=2, h=PH)
        AB = [RH[:, :].rearrange("p (e l) -> p e l", e=EB), RA[:, :].rearrange("p (e l) -> p e l", e=EB)]
        ZP = 7
        SCALE = float(D) ** -0.5

        def following(b, q, r):
            return (b, q + 1, r) if q + 1 < TPB else (b + 1, 0, 1 - r)

        def preceding(b, q, r):
            return (b, q - 1, r) if q > 0 else (b - 1, TPB - 1, 1 - r)

        def over_tiles(eng, tile):
            tile(0, 0, 0, "first")
            with eng.Fori(0, NB // 2 - 1) as pair:
                for r in range(2):
                    b = pair * 2 + r
                    for q in range(1, TPB):
                        tile(b, q, r, "")
                    tile(b + 1, 0, 1 - r, "")
            for b in (NB - 2, NB - 1):
                for q in range(1, TPB):
                    tile(b, q, b % 2, "last" if (b, q) == (NB - 1, TPB - 1) else "")
                if b == NB - 2:
                    tile(b + 1, 0, 1 - b % 2, "")

        def final(b):
            return isinstance(b, int) and b == NB - 1

        def sync_layer1(sp):
            with sp.Fori(0, NB) as b:
                sp.wait_ge(S("y_done"), b + 1)
                sp.dma_start(out_d[bass.ds(b, 1)].squeeze(0), acc[:, bass.ds(b * TPB, TPB), :]).then_inc(S("out_done"), 16)
            sp.wait_ge(S("out_done"), 16 * NB)

        def pool_layer1(pool):
            pool.sem_inc(S("z_pool"), 1)

            def tile(b, q, r, last):
                t = b * TPB + q
                pool.wait_ge(S("sm_ready"), t + 2)
                for h in range(ZP):
                    pool.wait_ge(S("mk_done"), t * PH + (h + 1))
                    pool.tensor_tensor(Z[:, h % RING].rearrange("p (i j) -> p i j", i=NK),
                                       sim[:, q % 2, h, 0, :].unsqueeze(2).to_broadcast([P, NK, NK]),
                                       sim[:, q % 2, h, 1, :].unsqueeze(1).to_broadcast([P, NK, NK]),
                                       ALU.add).then_inc(S("z_pool"), 1)
            with pool.Fori(0, NB) as b:
                for q in range(TPB):
                    tile(b, q, 0, False)

        def tensor_layer1(pe):
            pe.sem_inc(S("at_s"), CREDIT)
            pe.sem_inc(S("at_t"), CREDIT)
            pe.sem_inc(S("at_v"), CREDIT)
            pe.sem_inc(S("tc"), RING)
            pe.sem_inc(S("pr_mm"), CREDIT)
            pe.sem_inc(S("o2_mm"), CREDIT)
            pe.wait_ge(S("ld2"), 96)
            pe.wait_ge(S("x1_done"), NB + 1)
            for n in range(2 * PH):
                s_, h = n // PH, n % PH
                mm = pe.matmul(pb[7][:, (2 * h + s_) * NK:(2 * h + s_ + 1) * NK], wqk[:, n, :], keys[:, n, :],
                               start=True, stop=True)
            mm.then_inc(S("wk_mm"), 1)
            with pe.Fori(0, NB // 2) as pair:
                for r in range(2):
                    pe.wait_ge(S("x2_ready"), pair * 2 + (r + 1))
                    pe.wait_ge(S("x2_copied"), pair * 2 + (r + 1))
                    for q in range(TPB):
                        mm = pe.transpose(pb[r][:, q * P:(q + 1) * P], xst[:, r, q, :], ident)
                    mm.then_inc(S("x2_turned"), 1)
            pe.wait_ge(S("x2_copied"), NB + CREDIT)

            def attend(b, r):
                def scores(q):
                    pe.wait_ge(S("at_p"), b * TPB + (q + 1))
                    pe.matmul(pb[2 + q % 2][:, :], qk[:, r, 0, q * P:(q + 1) * P], qk[:, r, 1, :],
                              start=True, stop=True).then_inc(S("at_s"), 1)

                def turn(q):
                    pe.wait_ge(S("at_p"), b * TPB + (q + 1 + CREDIT))
                    pe.wait_ge(S("at_c"), b * TPB + (q + 1))
                    for n in range(TPB):
                        mm = pe.transpose(pb[4 + q % 2][:, n * P:(n + 1) * P], Pr[:, q % 2, n * P:(n + 1) * P], ident)
                    mm.then_inc(S("at_t"), 1)

                def values(q):
                    pe.wait_ge(S("at_c"), b * TPB + (q + 1 + CREDIT))
                    pe.wait_ge(S("at_o"), b * TPB + (q + 1))
                    if q == 0:
                        pe.wait_ge(S("xsum_ready"), b + 1)
                    for n in range(TPB):
                        mm = pe.matmul(pb[6 + q % 2][:, 0:D], PT[:, q % 2, n, :],
                                       xn2[:, bass.ds(b * TPB + n, 1), :].squeeze(1),
                                       start=(n == 0), stop=(n == TPB - 1))
                    mm.then_inc(S("at_v"), 1)

                pe.wait_ge(S("qk_ready"), 2 * b + 1)
                for k, wgt in enumerate((aWq, aWk)):
                    mm = pe.matmul(pb[k][:, :], wgt, xT[:, seq(b)], start=True, stop=True)
                mm.then_inc(S("pr_mm"), 1)
                pe.wait_ge(S("at_o"), b * TPB + 1)
                for n in range(TPB):
                    mm = pe.matmul(pb[6][:, 0:D], ones, xn2[:, bass.ds(b * TPB + n, 1), :].squeeze(1),
                                   start=(n == 0), stop=(n == TPB - 1))
                mm.then_inc(S("xsum_mm"), 1)
                pe.wait_ge(S("qk_ready"), 2 * b + 3)
                scores(0)
                scores(1)
                for q in range(TPB):
                    turn(q)
                    if q + 2 < TPB:
                        scores(q + 2)
                    if q >= 1:
                        values(q - 1)
                values(TPB - 1)
            with pe.Fori(0, NB // 2) as pair:
                attend(pair * 2, 0)
                attend(pair * 2 + 1, 1)

            pe.wait_ge(S("at_o"), NT + CREDIT)

            def scores_of(b, q, r):
                t = b * TPB + q
                pe.wait_ge(S("xb_ready"), b + 1)
                pe.wait_ge(S("sm_ready"), t + 1)
                pe.matmul(pb[0][:, :], xb[:, r, q * P:(q + 1) * P], WK, start=True, stop=True).then_inc(S("sm_mm"), 1)

            def hidden_of(b, es):
                for e in es:
                    pe.wait_ge(S("a_ready"), b * EB + (e + 1))
                    pe.matmul(pb[2 + e % 2][:, :], down[:, e * P:(e + 1) * P], xT[:, seq(b)],
                              start=True, stop=True).then_inc(S("a_mm"), 1)

            def output_of(b, q, r):
                t = b * TPB + q
                pe.wait_ge(S("wt_done"), 2 * t + 3)
                pe.wait_ge(S("o2_done"), t + 1)
                for e in range(EB):
                    mm = pe.matmul(pb[1][:, 0:D], Wt[:, q % 2, e, :], up[:, e, :],
                                   start=(e == 0), stop=(e == EB - 1))
                mm.then_inc(S("o2_mm"), 1)

            def tile(b, q, r, where):
                t = b * TPB + q
                if where != "last":
                    scores_of(*following(b, q, r))
                for h in range(PH):
                    pe.wait_ge(S("mk_done"), t * PH + (h + 1 + RING))
                    if h == 0 and where != "first":
                        pe.wait_ge(S("wt_done"), 2 * t - 1)
                    for e in range(EB):
                        mm = pe.matmul(pb[4 + 2 * (q % 2) + e // 4][:, (e % 4) * P:(e % 4 + 1) * P],
                                       MK[:, h % RING, e * P:(e + 1) * P],
                                       ident, start=(h == 0 and e % 4 == 0), stop=(h == PH - 1 and e % 4 == 3),
                                       is_transpose=True, skip_group_check=True)
                    mm.then_inc(S("tc"), 1)
                    if h == 2 and where != "first":
                        output_of(*preceding(b, q, r))
                    if h == 1 and not final(b):
                        hidden_of(b + 1, (2 * q, 2 * q + 1))
                if where == "last":
                    output_of(b, q, r)
            scores_of(0, 0, 0)
            hidden_of(0, range(EB))
            over_tiles(pe, tile)

        def scalar_layer1(act):
            act.sem_inc(S("x2_copied"), CREDIT)
            act.sem_inc(S("at_p"), CREDIT)
            act.sem_inc(S("qk_ready"), 1)
            act.sem_inc(S("sm_ready"), 1)
            act.sem_inc(S("at_c"), CREDIT)
            act.sem_inc(S("a_ready"), 2)
            act.sem_inc(S("o2_done"), 1)
            act.sem_inc(S("sg_done"), RING)
            act.wait_ge(S("sc_o"), NCH + CREDIT)
            for dst, src in ((wqk, a["wqk"].rearrange("p s h d -> p (s h) d")), (keys, a["keys"].rearrange("p s h k -> p (s h) k")),
                             (down, a["down"]), (up, a["up"].rearrange("(e p) d -> p e d", p=P)),
                             (aWq, a["aWq"]), (aWk, a["aWk"])):
                act.dma_start(dst, src).then_inc(S("ld2"), 16)
            act.wait_ge(S("ln2_var"), 1)
            act.activation(rstd[:, :], lntmp[:, 1, :], ACT.Sqrt, bias=eps5).then_inc(S("ln2_std"), 1)
            act.wait_ge(S("wk_mm"), 1)
            act.activation(WK, pb[7][:, :], ACT.Copy).then_inc(S("wk_ready"), 1)
            with act.Fori(0, NB // 2) as pair:
                for r in range(2):
                    b = pair * 2 + r
                    act.wait_ge(S("x2_turned"), b + 1)
                    act.activation(xT[:, seq(b)], pb[r][:, :], ACT.Copy)
                    act.activation(xn2[:, bass.ds(b * TPB, TPB), :], xst[:, r], ACT.Copy).then_inc(S("x2_copied"), 1)
            act.wait_ge(S("bn_var"), 1)
            act.activation(bnc[:, 2:3], bnc[:, 1:2], ACT.Sqrt, bias=eps5).then_inc(S("bn_std"), 1)
            act.wait_ge(S("bq_ready"), 1)

            def attend(b, r):
                act.wait_ge(S("pr_mm"), b + 1 + CREDIT)
                act.wait_ge(S("at_t"), b * TPB + 1)
                act.activation(qk[:, r, 0, :], pb[0][:, :], ACT.Identity, scale=SCALE, bias=bqs).then_inc(S("qk_ready"), 1)
                act.activation(qk[:, r, 1, :], pb[1][:, :], ACT.Identity, bias=col("bk")).then_inc(S("qk_ready"), 1)
                act.wait_ge(S("xsum_mm"), b + 1)
                act.wait_ge(S("at_o"), b * TPB + 1)
                act.activation(xsum[:, r, :], pb[6][:, 0:D], ACT.Copy).then_inc(S("xsum_ready"), 1)

                def soft(q):
                    t = b * TPB + q
                    act.wait_ge(S("at_m"), t + 1)
                    act.wait_ge(S("at_t"), t + 1)
                    act.activation(Pr[:, q % 2, :], pb[2 + q % 2][:, :], ACT.Exp, bias=ac[:, q % 2, 0:1],
                                   accum_out=ac[:, q % 2, 1:2]).then_inc(S("at_p"), 1)

                def turned(q):
                    t = b * TPB + q
                    act.wait_ge(S("at_t"), t + 1 + CREDIT)
                    act.wait_ge(S("at_v"), t + 1)
                    act.activation(PT[:, q % 2].rearrange("p n s -> p (n s)"), pb[4 + q % 2][:, :],
                                   ACT.Copy).then_inc(S("at_c"), 1)
                soft(0)
                for q in range(1, TPB):
                    soft(q)
                    turned(q - 1)
                turned(TPB - 1)
            with act.Fori(0, NB // 2) as pair:
                attend(pair * 2, 0)
                attend(pair * 2 + 1, 1)

            act.wait_ge(S("at_o"), NT + CREDIT)

            def scores_in(b, q, r):
                t = b * TPB + q
                if not (isinstance(b, int) and t < 2):
                    act.wait_ge(S("z_pool"), t * ZP - (ZP - 1))
                    act.wait_ge(S("z_dve"), t * (PH - ZP) - (PH - ZP))
                act.wait_ge(S("sm_mm"), t + 1)
                act.activation(sim[:, q % 2].rearrange("p h s k -> p (h s k)"), pb[0][:, :],
                               ACT.Copy).then_inc(S("sm_ready"), 1)

            def hidden_in(b, r, es):
                for e in es:
                    act.wait_ge(S("a_mm"), b * EB + (e + 1))
                    act.activation(AB[r][:, e, :], pb[2 + e % 2][:, :], ACT.Gelu).then_inc(S("a_ready"), 1)

            def output(b, q, r):
                t = b * TPB + q
                act.wait_ge(S("o2_mm"), t + 3)
                act.activation(o2[:, bass.ds(t, 1), :].squeeze(1), pb[1][:, 0:D], ACT.Copy).then_inc(S("o2_done"), 1)

            def tile(b, q, r, where):
                t = b * TPB + q
                for h in range(PH):
                    if h < ZP:
                        act.wait_ge(S("z_pool"), t * ZP + (h + 2))
                    else:
                        act.wait_ge(S("z_dve"), t * (PH - ZP) + (h - ZP + 1))
                    act.wait_ge(S("mk_done"), t * PH + (h + 1))
                    act.activation(SG[:, h % RING, :], Z[:, h % RING, :], ACT.Sigmoid).then_inc(S("sg_done"), 1)
                    if h == 1 and where != "last":
                        scores_in(*following(b, q, r))
                    if h == 5 and where != "first":
                        output(*preceding(b, q, r))
                if not final(b):
                    if q == 0 and where != "first":
                        act.wait_ge(S("wt_done"), 2 * TPB * b + 1)
                    hidden_in(b + 1, 1 - r, (2 * q, 2 * q + 1))
                if where == "last":
                    output(b, q, r)
            scores_in(0, 0, 0)
            hidden_in(0, 0, range(EB))
            over_tiles(act, tile)
            act.wait_ge(S("o2_done"), NT + 1)
            with act.Fori(0, NB) as b:
                ob = o2[:, bass.ds(b * TPB, TPB), :]
                act.activation(ob, ob, ACT.Silu).then_inc(S("g2_ready"), 1)

        def vector_layer1(dve):
            dve.sem_inc(S("at_o"), CREDIT)
            dve.sem_inc(S("mk_done"), RING)
            dve.sem_inc(S("wt_done"), 1)
            dve.wait_ge(S("x1_done"), NB + 1)
            moments(dve, acc, ("ln2_v", "ln2_var", "ln2_std", "ln2_done"), None)
            with dve.Fori(0, NB // 2) as pair:
                for r in range(2):
                    b = pair * 2 + r
                    dve.wait_ge(S("x2_copied"), b + 1)
                    for q in range(TPB):
                        op = normed(dve, xst[:, r, q, :], acc, b * TPB + q)
                    op.then_inc(S("x2_ready"), 1)
            dve.wait_ge(S("x2_copied"), NB + CREDIT)
            with dve.Fori(0, NB) as b:
                dve.bn_stats(bnst[:, bass.ds(b * 6, 6)], xT[:, seq(b)]).then_inc(S("bn_v"), 1)
            dve.wait_ge(S("bn_v"), NB)
            dve.bn_aggr(bnc[:, 0:2], bnst).then_inc(S("bn_var"), 1)
            dve.wait_ge(S("bn_std"), 1)
            dve.reciprocal(bnc[:, 2:3], bnc[:, 2:3]).then_inc(S("bn_v"), 1)
            dve.tensor_scalar(bqs, col("bq"), SCALE, None, ALU.mult).then_inc(S("bq_ready"), 1)
            dve.wait_ge(S("bn_v"), NB + 1)
            dve.tensor_tensor(bnc[:, 2:3], bnc[:, 2:3], col("gamma"), ALU.mult).then_inc(S("bn_v"), 1)
            dve.wait_ge(S("bn_v"), NB + 2)
            dve.tensor_tensor(bnc[:, 3:4], bnc[:, 2:3], bnc[:, 0:1], ALU.mult).then_inc(S("bn_v"), 1)
            dve.wait_ge(S("bn_v"), NB + 3)
            dve.tensor_tensor(bnc[:, 3:4], col("bbeta"), bnc[:, 3:4], ALU.subtract).then_inc(S("bn_v"), 1)
            dve.wait_ge(S("bn_v"), NB + 4)

            def attend(b, r):
                def top(q):
                    t = b * TPB + q
                    dve.wait_ge(S("at_s"), t + 1 + CREDIT)
                    dve.wait_ge(S("at_o"), t + 1)
                    dve.tensor_reduce(ac[:, q % 2, 0:1], pb[2 + q % 2][:, :], AX.X, ALU.max,
                                      negate=True).then_inc(S("at_m"), 1)

                def rest(q):
                    t = b * TPB + q
                    z, rz, mz = (ac[:, q % 2, k:k + 1] for k in (1, 2, 3))
                    dve.wait_ge(S("at_p"), t + 1 + CREDIT)
                    dve.reciprocal(rz, z).then_inc(S("at_z"), 1)
                    dve.wait_ge(S("at_z"), 3 * t + 1)
                    dve.tensor_tensor(mz, z, rz, ALU.mult).then_inc(S("at_z"), 1)
                    dve.wait_ge(S("at_z"), 3 * t + 2)
                    dve.tensor_scalar(mz, mz, -1.0 / L, -1.0 / L, ALU.mult, ALU.add).then_inc(S("at_z"), 1)
                    dve.wait_ge(S("at_v"), t + 1 + CREDIT)
                    dve.scalar_tensor_tensor(atmp[:, q % 2, :], pb[6 + q % 2][:, 0:D], rz,
                                             xn2[:, bass.ds(t, 1), :].squeeze(1), ALU.mult, ALU.add).then_inc(S("at_x"), 1)
                    dve.wait_ge(S("at_z"), 3 * t + 3)
                    dve.wait_ge(S("at_x"), t + 1)
                    dve.wait_ge(S("xsum_ready"), b + 1)
                    dve.scalar_tensor_tensor(s1[:, bass.ds(t, 1), :].squeeze(1), xsum[:, r, :], mz,
                                             atmp[:, q % 2, :], ALU.mult, ALU.add).then_inc(S("at_o"), 1)
                top(0)
                top(1)
                for q in range(TPB):
                    rest(q)
                    if q + 2 < TPB:
                        top(q + 2)
            with dve.Fori(0, NB // 2) as pair:
                attend(pair * 2, 0)
                attend(pair * 2 + 1, 1)

            def bn_apply(b, r):
                dve.tensor_scalar(xb[:, r, :], xT[:, seq(b)], bnc[:, 2:3], bnc[:, 3:4], ALU.mult,
                                  ALU.add).then_inc(S("xb_ready"), 1)

            def picks(b, q):
                t = b * TPB + q
                dve.wait_ge(S("sm_ready"), t + 2)
                dve.sem_inc(S("picks_at"), 1)
                for h in range(PH):
                    for s_ in range(2):
                        op = dve.max(tv[:, q % 2, h, s_, :], sim[:, q % 2, h, s_, :])
                op.then_inc(S("tk_v"), 1)
                dve.wait_ge(S("tk_v"), 2 * t + 1)
                dve.tensor_tensor(cand, tv[:, q % 2, :, 0, :].unsqueeze(3).to_broadcast([P, PH, PK, PK]),
                                  tv[:, q % 2, :, 1, :].unsqueeze(2).to_broadcast([P, PH, PK, PK]),
                                  ALU.add).then_inc(S("tk_v"), 1)
                dve.wait_ge(S("tk_v"), 2 * t + 2)
                dve.sem_inc(S("picks_at"), 1)
                for h in range(PH):
                    op = dve.max(t8[:, q % 2, h, :], cand[:, h].rearrange("p a b -> p (a b)"))
                op.then_inc(S("tk_done"), 1)

            def weigh_hidden(b, q, r):
                t = b * TPB + q
                dve.wait_ge(S("tc"), (t + 1) * PH + RING)
                dve.wait_ge(S("a_ready"), (b + 1) * EB + 2)
                dve.wait_ge(S("o2_mm"), t + 1)
                for k in range(2):
                    dve.tensor_tensor(Wt[:, q % 2, 4 * k:4 * k + 4, :],
                                      pb[4 + 2 * (q % 2) + k][:, :].rearrange("p (e n) -> p e n", e=4),
                                      AB[r][:, 4 * k:4 * k + 4, q * P:(q + 1) * P], ALU.mult).then_inc(S("wt_done"), 1)

            def tile(b, q, r, where):
                t = b * TPB + q
                if q == 1 and not final(b):
                    bn_apply(b + 1, 1 - r)
                dve.wait_ge(S("tk_done"), t + 1)
                for h in range(PH):
                    k = t * PH + (h + 1)
                    dve.wait_ge(S("sg_done"), k + RING)
                    dve.wait_ge(S("tc"), k)
                    dve.scalar_tensor_tensor(MK[:, h % RING, :], Z[:, h % RING, :], t8[:, q % 2, h, 7:8],
                                             SG[:, h % RING, :], ALU.is_ge, ALU.mult).then_inc(S("mk_done"), 1)
                    if h == 1 and where != "first":
                        weigh_hidden(*preceding(b, q, r))
                    if h == 3:
                        for hz in range(ZP, PH):
                            dve.wait_ge(S("mk_done"), t * PH + (hz + 1))
                            dve.tensor_tensor(Z[:, hz % RING].rearrange("p (i j) -> p i j", i=NK),
                                              sim[:, q % 2, hz, 0, :].unsqueeze(2).to_broadcast([P, NK, NK]),
                                              sim[:, q % 2, hz, 1, :].unsqueeze(1).to_broadcast([P, NK, NK]),
                                              ALU.add).then_inc(S("z_dve"), 1)
                        if where != "last":
                            picks(*following(b, q, r)[0:2])
                if where == "last":
                    weigh_hidden(b, q, r)
            bn_apply(0, 0)
            picks(0, 0)
            over_tiles(dve, tile)
            with dve.Fori(0, NB) as b:
                bt = bass.ds(b * TPB, TPB)
                dve.wait_ge(S("g2_ready"), b + 1)
                dve.tensor_tensor(s1[:, bt, :], s1[:, bt, :], o2[:, bt, :], ALU.mult).then_inc(S("y_mul"), 1)
                dve.wait_ge(S("y_mul"), b + 1)
                dve.tensor_tensor(acc[:, bt, :], acc[:, bt, :], s1[:, bt, :], ALU.add).then_inc(S("y_done"), 1)

        @block.sync
        def _(sp):
            for dst, src in ((con[:, :], a["con"]), (small[:, :], a["small"]),
                             (rows[:, 0:16], a["bf2"].partition_broadcast(P)),
                             (rows[:, 16:20], a["tau"].partition_broadcast(P)),
                             (rows[:, 20:28], a["gb"].partition_broadcast(P))):
                sp.dma_start(dst, src).then_inc(S("ld_const"), 16)
            sp.dma_start(x_in, a["x"].rearrange("(t p) d -> p t d", p=P)).then_inc(S("ld_x"), 16)
            for dst, src in ((wproj[:, 0, :], a["Wq"]), (wproj[:, 1, :], a["Wk"]), (wproj[:, 2, :], a["Wv"]),
                             (wb[:, :], a["Wb"]), (gatew[:, :], a["gw"]), (wo[:, :], a["Wo"]),
                             (wf1[:, :, :], a["Wf1"].rearrange("(k p) n -> p k n", p=P)),
                             (wf2[:, :, :], a["Wf2"].rearrange("(k p) n -> p k n", p=P)),
                             (b2[0:E, :], a["b2"]), (b2[E:NX, :], a["bs2"])):
                sp.dma_start(dst, src).then_inc(S("ld_w"), 16)
            sp.wait_ge(S("beta_done"), NB + CREDIT)
            sp.dma_start(beta_d, beta_sb.rearrange("h (n c) -> h n c", c=C)).then_inc(S("beta_out"), 16)
            sp.wait_ge(S("beta_out"), 16)
            sp.dma_start(beta_it[:, :, :], beta_d.rearrange("h n c -> n h c")).then_inc(S("beta_in"), 16)
            sp.wait_ge(S("nrm_done"), NB + CREDIT)
            for dst, src in ((w1[:, 0:E, :], a["w1"].rearrange("e p n -> p e n")), (w1[:, E, :], a["ws1"]),
                             (w2[:, 0:E], a["w2"].rearrange("e (m p) d -> p e m d", p=P)),
                             (w2[:, E], a["ws2"].rearrange("(m p) d -> p m d", p=P))):
                sp.dma_start(dst, src).then_inc(S("ld_e"), 16)
            with sp.Fori(0, NB // 2) as pair:
                b0 = pair * 2
                for r in range(2):
                    sp.wait_ge(S("gram_v"), (b0 + (r + 1)) * TPB + TPB)
                    sp.wait_ge(S("v_turned"), (b0 + (r + 1)) * TPB + TPB)
                    sp.dma_start(gram_d[bass.ds((b0 + r) * NCH, NCH)].rearrange("n h j i -> (h j) n i"),
                                 cst[:, r, :, 0, :]).then_inc(S(f"cst_out{r}"), 16)
                    sp.dma_start(lv_d[:, bass.ds((b0 + r) * NCH, NCH)], cst[:, r, :, 1:3, :]).then_inc(S(f"cst_out{r}"), 16)
            for r in range(2):
                sp.wait_ge(S(f"cst_out{r}"), 16 * NB + 32)
            sp.dma_start(att[:, :, :, :], gram_d).then_inc(S("ld_att"), 16)
            sp.wait_ge(S("inv_ready"), 1)
            sp.dma_start(inv_d, att[:, :, :, :]).then_inc(S("inv_out"), 16)
            sp.wait_ge(S("inv_out"), 16)
            sp.wait_ge(S("scan_zero"), 2)

            def scan_load(n, r):
                sp.wait_ge(S("sc_o"), n + 1)
                for h in range(H):
                    sp.dma_start(Gb[h * C:(h + 1) * C, r, :, h * C:(h + 1) * C],
                                 inv_n[bass.ds(n, 1), h].squeeze(0)).then_inc(S(f"ld_g{r}"), 16)
                sp.dma_start(lv[:, r], lv_n[:, :, bass.ds(n, 1)].squeeze(2)).then_inc(S(f"ld_g{r}"), 16)

            inv_n = inv_d.rearrange("(b n) h j i -> n h j b i", b=NB)
            lv_n = lv_d.rearrange("p (b n) s c -> p b n s c", b=NB)
            with sp.Fori(0, NCH // 2) as pair:
                n0 = pair * 2
                for r in range(2):
                    scan_load(n0 + r, r)
            sp.wait_ge(S("sc_o"), NCH + CREDIT)
            with sp.Fori(0, NB) as b:
                sp.wait_ge(S("x1_done"), b + 1)
                sp.dma_start(xr, x_d[bass.ds(b, 1)].squeeze(0)).then_inc(S("ld_xr"), 16)
            sync_layer1(sp)

        @block.gpsimd
        def _(pool):
            pool.memset(pads[:, 0, :, 0:3], 0.0).then_inc(S("zeros"), 1)
            pool.memset(pads[:, 1, :, 0:3], 0.0).then_inc(S("zeros"), 1)
            pool.memset(vT[:, :, 0:PADV], 0.0).then_inc(S("zeros"), 1)
            pool.memset(comb[:, :, E:NX], 1.0).then_inc(S("zeros"), 1)
            pool.wait_ge(S("ld_const"), 80)
            with pool.Fori(0, NB) as b:
                for q in range(TPB):
                    pool.wait_ge(S("nrm_done"), b + 1 + CREDIT)
                    if q == 0:
                        pool.wait_ge(S("sq_free"), 1)
                    pool.wait_ge(S("gram_mm"), b * TPB + (q + 1))
                    pool.tensor_tensor(
                        KX[:, q % 2].rearrange("p n (h c) -> p n h c", h=H),
                        kq[:, bass.ds(b * NCH + q * 4, 4), 0, :].unsqueeze(2).to_broadcast([P, 4, H, C]),
                        blocks4.unsqueeze(1).to_broadcast([P, 4, H, C]), ALU.mult).then_inc(S("kx_ready"), 1)
            pool.wait_ge(S("ld_att"), 16)
            pool.wait_ge(S("beta_in"), 16)
            pool.tensor_tensor(att, att, beta_it[:, :, :].unsqueeze(2).to_broadcast([P, H, C, C]),
                               ALU.mult).then_inc(S("subst"), 1)
            for j in range(1, C - 1):
                n = C - 1 - j
                prod = RP[:, 0:H * j * n].rearrange("p (h k i) -> p h k i", h=H, k=j)
                pool.wait_ge(S("subst"), 2 * j - 1)
                pool.tensor_tensor(prod, att[:, :, j, j + 1:C].unsqueeze(2).to_broadcast([P, H, j, n]),
                                   att[:, :, 0:j, j].unsqueeze(3).to_broadcast([P, H, j, n]),
                                   ALU.mult).then_inc(S("subst"), 1)
                pool.wait_ge(S("subst"), 2 * j)
                pool.tensor_tensor(att[:, :, 0:j, j + 1:C], att[:, :, 0:j, j + 1:C], prod,
                                   ALU.add).then_inc(S("subst"), 1)
            pool.wait_ge(S("subst"), 2 * C - 3)
            diag = RA[:, :].rearrange("p (h x) -> p h x", h=H)[:, :, 0:C * C:C + 1]
            pool.tensor_scalar(diag, diag, 1.0, None, ALU.add).then_inc(S("subst"), 1)
            pool.wait_ge(S("subst"), 2 * C - 2)
            pool.tensor_tensor(att, att, beta_it[:, :, :].unsqueeze(3).to_broadcast([P, H, C, C]),
                               ALU.mult).then_inc(S("inv_ready"), 1)
            pool.wait_ge(S("gram_a"), NB + CREDIT)
            pool.wait_ge(S("inv_ready"), 1)
            pool.wait_ge(S("y_mm"), 10 * NB + CREDIT)
            pool.memset(RW[:, 2 * SW:4 * SW], 0.0).then_inc(S("scan_zero"), 1)
            pool.memset(zero, 0.0).then_inc(S("scan_zero"), 1)
            with pool.Fori(0, NCH // 2) as pair:
                n0 = pair * 2
                for r in range(2):
                    n = n0 + r
                    pool.wait_ge(S("sc_s"), n + 1)
                    pool.tensor_tensor(
                        Kb[:, r].rearrange("p b (h c) -> p b h c", h=H),
                        kq5[:, :, bass.ds(n, 1), 0, :].to_broadcast([P, NB, H, C]),
                        blocks4.unsqueeze(1).to_broadcast([P, NB, H, C]), ALU.mult).then_inc(S("sc_k"), 1)
            def fuse_sum(b, r):
                pool.wait_ge(S("fz_mul"), 4 * (b + 1) + 1)
                pool.wait_ge(S("fz_n"), b + 1)
                pool.tensor_tensor(mC[:, 0], mC[:, 0], mC[:, 1], ALU.add).then_inc(S("fz_add"), 1)
                pool.tensor_tensor(mC[:, 2], mC[:, 2], mC[:, 3], ALU.add).then_inc(S("fz_add"), 1)
                pool.wait_ge(S("fz_add"), 3 * b + 2 + 3)
                pool.tensor_tensor(oT[:, r], mC[:, 0], mC[:, 2], ALU.add).then_inc(S("fz_add"), 1)
            with pool.Fori(0, NB // 2) as pair:
                b0 = pair * 2
                for r in range(2):
                    fuse_sum(b0 + r, r)
            pool_layer1(pool)

        @block.tensor
        def _(pe):
            for n in ("xn_turned", "nrm_mm", "gram_mm", "y_mm", "sc_u", "sc_s", "sc_o", "fl_mm", "fp_mm"):
                pe.sem_inc(S(n), CREDIT)
            for n in ("gate_mm", "fz_ms", "cs_turned", "fz_wo"):
                pe.sem_inc(S(n), 1)
            pe.wait_ge(S("ld_const"), 80)
            with pe.Fori(0, NB // 2) as pair:
                b0 = pair * 2
                for r in range(2):
                    pe.wait_ge(S("xn_ready"), b0 + (r + 1))
                    pe.wait_ge(S("xT_ready"), b0 + (r + 1))
                    for q in range(TPB):
                        mm = pe.transpose(pb[r][:, q * P:(q + 1) * P], xst[:, r, q, :], ident)
                    mm.then_inc(S("xn_turned"), 1)
            pe.wait_ge(S("ld_w"), 160)
            with pe.Fori(0, NB // 2) as pair:
                b0 = pair * 2
                for r in range(2):
                    b = b0 + r
                    pe.wait_ge(S("xs_ready"), b + 1)
                    pe.wait_ge(S("beta_done"), b + 1)
                    pe.wait_ge(S("gl_done"), b + 1)
                    pe.matmul(pb[2 + r][0:H, :], wb[:, :], xs[:, r, :], start=True, stop=True)
                    for q in range(TPB):
                        mm = pe.matmul(pb[4 + r][:, q * E:(q + 1) * E], xs[:, r, q * P:(q + 1) * P], gatew[:, :],
                                       start=True, stop=True)
                    mm.then_inc(S("gate_mm"), 1)
            pe.wait_ge(S("beta_done"), NB + CREDIT)
            pe.wait_ge(S("gl_done"), NB + CREDIT)
            with pe.Fori(0, NB // 2) as pair:
                b0 = pair * 2
                for r in range(2):
                    pe.wait_ge(S("conv_evac"), b0 + (r + 1))
                    for k in range(3):
                        mm = pe.matmul(pb[2 + 3 * r + k][:, :], wproj[:, k, :], xT[:, seq(b0 + r)],
                                       start=True, stop=True)
                    mm.then_inc(S("conv_mm"), 1)
            pe.wait_ge(S("xT_ready"), NB + CREDIT)
            pe.wait_ge(S("conv_evac"), NB + CREDIT)
            with pe.Fori(0, NB // 2) as pair:
                b0 = pair * 2
                for r in range(2):
                    b = b0 + r
                    pe.wait_ge(S("nrm_sq"), b + 1)
                    pe.wait_ge(S("nrm_rt"), b + 1)
                    for k in range(2):
                        mm = pe.matmul(pb[2 * r + k][:, :], blocks, sq[:, r, k * L:(k + 1) * L], start=True, stop=True)
                    mm.then_inc(S("nrm_mm"), 1)
            with pe.Fori(0, NB) as b:
                for q in range(TPB):
                    g1 = b * TPB + (q + 1)
                    pe.wait_ge(S("kx_ready"), g1)
                    pe.wait_ge(S("gram_v"), g1)
                    bank = pb[4 + q][:, 0:8 * C].rearrange("p (n c) -> p n c", n=4)
                    for i in range(4):
                        mm = pe.matmul(bank[:, i, 0:2 * C], KX[:, q % 2, i, :],
                                  kq[:, bass.ds(b * NCH + (q * 4 + i), 1), :, :].rearrange("p n s c -> p (n s c)"),
                                  start=True, stop=True)
                    mm.then_inc(S("gram_mm"), 1)
            pe.wait_ge(S("ld_e"), 64)
            pe.wait_ge(S("gram_v"), NB * TPB + TPB)
            with pe.Fori(0, NB) as b:
                def hidden(e):
                    for m in range(MB):
                        pe.wait_ge(S("h_ready"), (b * NX + e) * MB + (m + 1))
                        pe.matmul(pb[m][:, :], w1[:, e, m * P:(m + 1) * P], xT[:, seq(b)],
                                  start=True, stop=True).then_inc(S("h_mm"), 1)

                hidden(0)
                for e in range(NX):
                    if e + 1 < NX:
                        hidden(e + 1)
                    pe.wait_ge(S("h_ready"), (b * NX + (e + 1)) * MB + MB)
                    pe.wait_ge(S("y_added"), 4 * (b * 10 + (e + 1)))
                    for q in range(TPB):
                        for m in range(MB):
                            mm = pe.matmul(pb[4 + e % 2][:, q * P:(q + 1) * P], hT[:, e % 2, m, q * P:(q + 1) * P],
                                           w2[:, e, m, :], start=(m == 0), stop=(m == MB - 1))
                    mm.then_inc(S("y_mm"), 1)
                    if e == 3:
                        pe.wait_ge(S("cs_ready"), b + 1)
                        pe.wait_ge(S("ct_ready"), b + 1)
                        for q in range(TPB):
                            mm = pe.transpose(pb[6][0:NX, q * P:(q + 1) * P], cs[:, q, :], ident)
                        mm.then_inc(S("cs_turned"), 1)
                pe.wait_ge(S("ct_ready"), b + 2)
                pe.wait_ge(S("y_added"), 4 * (b * 10 + 10))
                for q in range(TPB):
                    mm = pe.matmul(pb[5][:, q * P:(q + 1) * P], cT[:, q * P:(q + 1) * P], b2[:, :],
                                   start=True, stop=True)
                mm.then_inc(S("y_mm"), 1)
            psW = [pb[0], pb[1]]

            def w_mm(n, r):
                pe.wait_ge(S("sc_k"), n + 1)
                pe.wait_ge(S(f"ld_g{r}"), 40 * n + (80 - 40 * r))
                pe.wait_ge(S("sc_wn"), n + 1)
                for b in range(NB):
                    mm = pe.matmul(psW[b // 4][:, (b % 4) * P:(b % 4 + 1) * P], Kb[:, r, b, :], Gb[:, r, b, :],
                                   start=True, stop=True)
                mm.then_inc(S("sc_w"), 1)

            def scan_step(n, r, last):
                pe.wait_ge(S("sc_wn"), n + 2)
                pe.wait_ge(S("sc_s4"), n + 1)
                pe.wait_ge(S("sc_u4"), n + 1)
                for b in range(NB):
                    o = pb[2 + r][:, b * C:(b + 1) * C]
                    pe.matmul(o, Gb[:, r, b, :], lv[:, r, b, 1, :], start=True, stop=False)
                    mm = pe.matmul(o, Wn[:, r, b, :], S4[:, b, :], start=False, stop=True)
                mm.then_inc(S("sc_u"), 1)
                if not last:
                    w_mm(n + 1, 1 - r)
                pe.wait_ge(S("sc_u4"), n + 1 + CREDIT)
                pe.wait_ge(S("sc_sb"), n + 1)
                for b in range(NB):
                    mm = pe.matmul(pb[6][:, b * C:(b + 1) * C], Kb[:, r, b, :], U4[:, b, :],
                                   start=False, stop=False, skip_group_check=True)
                mm.then_inc(S("sc_s"), 1)
                pe.wait_ge(S("sc_ub"), n + 1 + CREDIT)
                pe.wait_ge(S("sc_oe"), n + 1)
                for b in range(NB):
                    o = pb[4 + r][:, b * C:(b + 1) * C]
                    pe.matmul(o, Sb[:, b, :], kq5[:, b, bass.ds(n, 1), 1, :].rearrange("p n c -> p (n c)"),
                              start=True, stop=False)
                    mm = pe.matmul(o, Ub[:, b, :], lv[:, r, b, 0, :], start=False, stop=True)
                mm.then_inc(S("sc_o"), 1)

            pe.wait_ge(S("scan_zero"), 2)
            pe.wait_ge(S("y_added"), 40 * NB + ACCC)
            pe.wait_ge(S("ct_ready"), NB + 1)
            pe.matmul(pb[6][:, 0:NB * C], blocks, zero, start=True, stop=False, skip_group_check=True)
            w_mm(0, 0)
            with pe.Fori(0, (NCH - 2) // 2) as pair:
                n0 = pair * 2
                scan_step(n0, 0, False)
                scan_step(n0 + 1, 1, False)
            scan_step(NCH - 2, 0, False)
            scan_step(NCH - 1, 1, True)
            pe.wait_ge(S("sc_oe"), NCH + CREDIT)

            def fuse_hidden(b, r):
                pe.wait_ge(S("fh_ready"), 2 * b + 2)
                srcs = [xT[:, seq(b)], firs[:, bass.ds(b, 1), :].squeeze(1), firl[:, bass.ds(b, 1), :].squeeze(1),
                        dT[:, bass.ds(b, 1), :].squeeze(1)]
                for m in range(2):
                    for k in range(4):
                        mm = pe.matmul(pb[2 * r + m][:, :], wf1[:, k, m * P:(m + 1) * P], srcs[k],
                                       start=(k == 0), stop=(k == 3))
                    mm.then_inc(S("fh_mm"), 1)

            def fuse_logits(b, r):
                pe.wait_ge(S("fh_ready"), 2 * b + 2 + 4)
                pe.wait_ge(S("fl_done"), b + 1)
                for q in range(TPB):
                    for m in range(2):
                        mm = pe.matmul(pb[4 + r][:, q * 16:(q + 1) * 16], hidT[:, r, m, q * P:(q + 1) * P],
                                       wf2[:, m, :], start=(m == 0), stop=(m == 1))
                mm.then_inc(S("fl_mm"), 1)
            staggered(pe, fuse_hidden, fuse_logits)

            def path_weights(b, r):
                pe.wait_ge(S("fp_ready"), b + 1)
                pe.wait_ge(S("fz_mul"), 4 * b + 1)
                for c in range(4):
                    for q in range(TPB):
                        mm = pe.transpose(pb[c][:, q * P:(q + 1) * P], Pst[:, r, q, c, :], ident)
                mm.then_inc(S("fp_mm"), 1)

            def project(b, r):
                pe.wait_ge(S("fz_sq"), b + 1)
                pe.wait_ge(S("fz_rt"), b + 1)
                pe.matmul(pb[4][:, :], blocks, sqo, start=True, stop=True).then_inc(S("fz_ms"), 1)
                pe.wait_ge(S("fz_n"), b + 1 + CREDIT)
                pe.wait_ge(S("fz_sg"), b + 1)
                for q in range(TPB):
                    mm = pe.matmul(pb[5][:, q * P:(q + 1) * P], oN[:, q * P:(q + 1) * P], wo[:, :],
                                   start=True, stop=True)
                mm.then_inc(S("fz_wo"), 1)
            pe.wait_ge(S("fl_done"), NB + CREDIT)
            pe.wait_ge(S("fh_ready"), 2 * NB + 4)
            staggered(pe, path_weights, project)
            tensor_layer1(pe)

        @block.scalar
        def _(act):
            act.sem_inc(S("xT_ready"), CREDIT)
            act.sem_inc(S("beta_done"), CREDIT)
            act.sem_inc(S("conv_evac"), CREDIT)
            act.sem_inc(S("silu_done"), CREDIT)
            act.sem_inc(S("nrm_rt"), CREDIT)
            act.sem_inc(S("gram_a"), CREDIT)
            act.sem_inc(S("h_ready"), MB)
            act.sem_inc(S("ct_ready"), 1)
            act.sem_inc(S("sc_wn"), 1)
            act.sem_inc(S("sc_u4"), CREDIT)
            act.sem_inc(S("sc_oe"), CREDIT)
            act.sem_inc(S("fh_ready"), 4)
            act.sem_inc(S("fz_rt"), 1)
            act.wait_ge(S("ld_const"), 80)
            act.wait_ge(S("ln_var"), 1)
            act.activation(rstd[:, :], lntmp[:, 1, :], ACT.Sqrt, bias=eps5).then_inc(S("ln_std"), 1)
            with act.Fori(0, NB // 2) as pair:
                b0 = pair * 2
                for r in range(2):
                    act.wait_ge(S("xn_turned"), b0 + (r + 1 + CREDIT))
                    act.activation(xT[:, seq(b0 + r)], pb[r][:, :], ACT.Copy).then_inc(S("xT_ready"), 1)

            def gate_in(b, r):
                act.wait_ge(S("xT_ready"), b + 1 + CREDIT)
                act.wait_ge(S("gate_mm"), b + 1)
                act.activation(xs[:, r, :], xT[:, seq(b)], ACT.Copy).then_inc(S("xs_ready"), 1)

            def gate_beta(b, r):
                act.wait_ge(S("gate_mm"), b + 2)
                act.activation(beta_sb[:, seq(b)], pb[2 + r][0:H, :], ACT.Sigmoid).then_inc(S("beta_done"), 1)
            with act.Fori(0, NB // 2) as pair:
                b0 = pair * 2
                for r in range(2):
                    gate_in(b0 + r, r)
                    gate_beta(b0 + r, r)

            def conv_in(b, r):
                act.wait_ge(S("conv_mm"), b + 1)
                act.wait_ge(S("conv_tap"), 12 * (b + 1))
                for k in range(3):
                    op = act.activation(pads[:, r, k, 3:CW], pb[2 + 3 * r + k][:, :], ACT.Copy)
                op.then_inc(S("conv_evac"), 1)

            def conv_out(b, r):
                act.wait_ge(S("conv_tap"), 12 * (b + 1) + CONVC)
                items = bass.ds(b * NCH, NCH)
                v3 = [cacc[r][:, k, :].rearrange("p (n c) -> p n c", n=NCH) for k in range(2)]
                act.activation(kq[:, items, 1, :], v3[0], ACT.Silu)
                act.activation(kq[:, items, 0, :], v3[1], ACT.Silu)
                act.activation(vtok[:, bass.ds(b, 1), :].squeeze(1), cacc[r][:, 2, :],
                               ACT.Silu).then_inc(S("silu_done"), 1)
            act.wait_ge(S("zeros"), 4)
            staggered(act, conv_in, conv_out)

            def nrm_square(b, r):
                act.wait_ge(S("nrm_mm"), b + 1)
                act.activation(sq[:, r, :], RK[:, seq(b, 2 * L)], ACT.Square).then_inc(S("nrm_sq"), 1)

            def nrm_root(b, r):
                act.wait_ge(S("nrm_mm"), b + 1 + CREDIT)
                act.wait_ge(S("nrm_done"), b + 1)
                for k in range(2):
                    op = act.activation(rn[:, r, k * L:(k + 1) * L], pb[2 * r + k][:, :], ACT.Sqrt, bias=eps6)
                op.then_inc(S("nrm_rt"), 1)
            act.wait_ge(S("silu_done"), NB + CREDIT)
            staggered(act, nrm_square, nrm_root)
            act.wait_ge(S("nrm_mm"), NB + CREDIT)
            act.sem_inc(S("sq_free"), 1)
            def kv_copy(b, r):
                act.wait_ge(S("k_turned"), b + 1)
                act.activation(kv_in[:, r, 0], kq[:, bass.ds(b * NCH, NCH), 0, :], ACT.Copy)
                act.activation(kv_in[:, r, 1].rearrange("p n c -> p (n c)"), vtok[:, bass.ds(b, 1), :].squeeze(1),
                               ACT.Copy).then_inc(S("kv_in"), 1)

            def keys_back(b, r):
                act.wait_ge(S("gram_mm"), (b + 1) * TPB + CREDIT)
                act.wait_ge(S("k_turned"), b + 1 + CREDIT)
                act.sem_inc(S("keys_at"), 1)
                act.activation(kq[:, bass.ds(b * NCH, NCH), 0, :], kt[:, r], ACT.Copy).then_inc(S("gram_a"), 1)
            act.wait_ge(S("nrm_done"), NB + CREDIT)
            staggered(act, kv_copy, keys_back)
            act.wait_ge(S("topk"), 10)
            act.activation(tw[:, 2, :], tw[:, 2, :], ACT.Exp).then_inc(S("top_e"), 1)
            act.wait_ge(S("top_all"), 1)
            with act.Fori(0, NB) as b:
                for e in range(NX):
                    for m in range(MB):
                        act.wait_ge(S("h_mm"), (b * NX + e) * MB + (m + 1))
                        if m == 0:
                            act.wait_ge(S("y_mm"), b * 10 + (e + 1 if e >= 2 else 1))
                        act.activation(hT[:, e % 2, m, :], pb[m][:, :], ACT.Gelu,
                                       bias=col("b1", e * MB + m)).then_inc(S("h_ready"), 1)
                    if e == 5:
                        act.wait_ge(S("cs_turned"), b + 2)
                        act.wait_ge(S("y_mm"), b * 10 + CREDIT)
                        act.activation(cT, pb[6][0:NX, :], ACT.Copy).then_inc(S("ct_ready"), 1)
            act.wait_ge(S("y_added"), 40 * NB + ACCC)
            act.activation(acc[:, :, :], acc[:, :, :], ACT.Silu).then_inc(S("g_ready"), 1)

            def w_out(n, r):
                act.wait_ge(S("sc_w"), n + 1)
                act.wait_ge(S("sc_u"), n + 1)
                for k in range(2):
                    op = act.activation(Wn[:, r, 4 * k:4 * k + 4, :].rearrange("p b c -> p (b c)"), pb[k][:, :],
                                        ACT.Copy, scale=-1.0)
                op.then_inc(S("sc_wn"), 1)

            def scan_step(n, r, last):
                act.wait_ge(S("sc_u"), n + 1 + CREDIT)
                act.wait_ge(S("sc_s"), n + 2)
                act.wait_ge(S("sc_ub"), n + CREDIT)
                act.activation(U4.rearrange("p b c -> p (b c)"), pb[2 + r][:, 0:NB * C], ACT.Copy).then_inc(S("sc_u4"), 1)
                if not last:
                    w_out(n + 1, 1 - r)
                act.wait_ge(S("sc_s"), n + 1 + CREDIT)
                act.wait_ge(S("sc_sb"), n + 1)
                act.activation(S4.rearrange("p b c -> p (b c)"), pb[6][:, 0:NB * C], ACT.Copy).then_inc(S("sc_s4"), 1)
                act.wait_ge(S("sc_o"), n + 1 + CREDIT)
                act.activation(dT[:, :, bass.ds(n * C, C)], pb[4 + r][:, 0:NB * C].rearrange("p (b c) -> p b c", b=NB),
                               ACT.Copy).then_inc(S("sc_oe"), 1)
            act.wait_ge(S("inv_out"), 16)
            w_out(0, 0)
            with act.Fori(0, (NCH - 2) // 2) as pair:
                n0 = pair * 2
                scan_step(n0, 0, False)
                scan_step(n0 + 1, 1, False)
            scan_step(NCH - 2, 0, False)
            scan_step(NCH - 1, 1, True)
            act.wait_ge(S("sc_sb"), NCH + 1)
            with act.Fori(0, NB // 2) as pair:
                b0 = pair * 2
                for r in range(2):
                    b = b0 + r
                    for m in range(2):
                        act.wait_ge(S("fh_mm"), 2 * b + (m + 1))
                        if m == 0:
                            act.wait_ge(S("fl_mm"), b + 1)
                        act.activation(hidT[:, r, m, :], pb[2 * r + m][:, :], ACT.Gelu,
                                       bias=col("bf1", m)).then_inc(S("fh_ready"), 1)
            act.activation(itau, rows[:, 16:20], ACT.Exp, scale=-1.0).then_inc(S("itau"), 1)
            act.wait_ge(S("fg"), 3)
            act.activation(ft3(2), ft3(2), ACT.Exp).then_inc(S("fg_e"), 1)
            act.activation(ftx(1), lg[:, :, :, 3], ACT.Exp, scale=-1.0).then_inc(S("fg_e"), 1)
            act.wait_ge(S("pg_ready"), 2)

            def path_spread(b, r):
                act.wait_ge(S("fp_mm"), b + 1)
                act.activation(
                    Pst[:, r].rearrange("p q c (h d) -> p (q c h) d", h=H),
                    PG[:, bass.ds(b * TPB, TPB)].rearrange("p t c h -> p (t c h)").unsqueeze(2).to_broadcast([P, 64, DK]),
                    ACT.Copy).then_inc(S("fp_ready"), 1)

            def rms(b, r):
                act.wait_ge(S("fz_add"), 3 * (b + 1) + 3)
                act.wait_ge(S("fz_ms"), b + 1)
                act.activation(sqo, oT[:, r], ACT.Square).then_inc(S("fz_sq"), 1)
                act.wait_ge(S("fz_ms"), b + 2)
                act.wait_ge(S("fz_n"), b + 2)
                act.activation(rr, pb[4][:, :], ACT.Sqrt, scale=1.0 / DK, bias=eps5).then_inc(S("fz_rt"), 1)
            staggered(act, path_spread, rms)
            scalar_layer1(act)

        @block.vector
        def _(dve):
            dve.sem_inc(S("gl_done"), CREDIT)
            dve.sem_inc(S("conv_tap"), CONVC)
            dve.sem_inc(S("nrm_done"), CREDIT)
            dve.sem_inc(S("gram_v"), TPB)
            dve.sem_inc(S("v_turned"), TPB)
            dve.sem_inc(S("k_turned"), CREDIT)
            dve.sem_inc(S("cst_out0"), 32)
            dve.sem_inc(S("cst_out1"), 32)
            dve.sem_inc(S("y_added"), ACCC)
            dve.sem_inc(S("sc_ub"), CREDIT)
            dve.sem_inc(S("fl_done"), CREDIT)
            dve.sem_inc(S("fz_n"), CREDIT)
            dve.sem_inc(S("fz_add"), 3)
            dve.sem_inc(S("fz_sg"), 1)
            dve.sem_inc(S("x1_done"), 1)
            dve.sem_inc(S("fz_mul"), 1)

            moments(dve, x_in, ("ln_v", "ln_var", "ln_std", "ln_done"), "ld_x")
            with dve.Fori(0, NB // 2) as pair:
                b0 = pair * 2
                for r in range(2):
                    dve.wait_ge(S("xn_turned"), b0 + (r + 1))
                    for q in range(TPB):
                        op = normed(dve, xst[:, r, q, :], x_in, (b0 + r) * TPB + q)
                    op.then_inc(S("xn_ready"), 1)
            gate_b = rows[:, 20:28]
            with dve.Fori(0, NB // 2) as pair:
                b0 = pair * 2
                for r in range(2):
                    dve.wait_ge(S("gate_mm"), b0 + (r + 2))
                    dve.tensor_tensor(gl[:, bass.ds((b0 + r) * TPB, TPB), :],
                                      pb[4 + r][:, 0:TPB * E].rearrange("p (q e) -> p q e", q=TPB),
                                      gate_b.unsqueeze(1).to_broadcast([P, TPB, E]), ALU.add).then_inc(S("gl_done"), 1)
            with dve.Fori(0, NB // 2) as pair:
                b0 = pair * 2
                for r in range(2):
                    b = b0 + r
                    dve.wait_ge(S("conv_evac"), b + 1 + CREDIT)
                    dve.wait_ge(S("silu_done"), b + 1)
                    for k in range(4):
                        for c3 in range(3):
                            tap, src, dst = col("cw", c3 * 4 + k), pads[:, r, c3, k:k + L], cacc[r][:, c3, :]
                            if k == 0:
                                op = dve.tensor_scalar(dst, src, tap, None, ALU.mult)
                            else:
                                dve.wait_ge(S("conv_tap"), 12 * b + (3 * (k - 1) + c3 + 1 + CONVC))
                                op = dve.scalar_tensor_tensor(dst, src, tap, dst, ALU.mult, ALU.add)
                            op.then_inc(S("conv_tap"), 1)
            with dve.Fori(0, NB // 2) as pair:
                b0 = pair * 2
                for r in range(2):
                    b = b0 + r
                    dve.wait_ge(S("nrm_rt"), b + 1 + CREDIT)
                    dve.reciprocal(rn[:, r, :], rn[:, r, :]).then_inc(S("nrm_rec"), 1)
                    dve.wait_ge(S("nrm_rec"), b + 1)
                    dve.tensor_tensor(RK[:, seq(b, 2 * L)], RK[:, seq(b, 2 * L)], rn[:, r, :],
                                      ALU.mult).then_inc(S("nrm_done"), 1)
            masks = con[:, O_GRAM:O_GRAM + 2 * C]

            def products(b, r):
                dve.wait_ge(S(f"cst_out{r}"), 16 * b + (32 - 16 * r))
                dve.wait_ge(S("kv_in"), b + 1)
                dve.transpose(cst[:, r, :, 2, :], kv_in[:, r, 1]).then_inc(S("v_turned"), TPB)
                dve.wait_ge(S("gram_a"), b + 1)
                dve.transpose(kt[:, r], kv_in[:, r, 0]).then_inc(S("k_turned"), 1)
                for q in range(TPB):
                    dve.wait_ge(S("gram_mm"), b * TPB + (q + 1 + CREDIT))
                    bank = pb[4 + q][:, 0:8 * C].rearrange("p (n c) -> p n c", n=4)
                    dve.tensor_tensor(cst[:, r, q * 4:q * 4 + 4, 0:2, :].rearrange("p n s c -> p n (s c)"),
                                      bank[:, :, 0:2 * C], masks.unsqueeze(1).to_broadcast([P, 4, 2 * C]),
                                      ALU.mult).then_inc(S("gram_v"), 1)
            with dve.Fori(0, NB // 2) as pair:
                b0 = pair * 2
                for r in range(2):
                    products(b0 + r, r)
            n_top = 0

            def t_inc(op):
                op.then_inc(S("topk"), 1)

            bc = [P, NT, E]
            io = iota_e.unsqueeze(1).to_broadcast(bc)
            t8 = [top[:, k, 0:NT * E].rearrange("p (t e) -> p t e", e=E) for k in range(4)]
            m1, m2, df, i1 = (tw[:, k, :] for k in range(4))
            dve.wait_ge(S("gl_done"), NB + CREDIT)

            def best(src, m, oh, k0):
                dve.tensor_reduce(m, src, AX.X, ALU.max).then_inc(S("topk"), 1)
                dve.wait_ge(S("topk"), k0 + 1)
                dve.tensor_tensor(oh, src, m.unsqueeze(2).to_broadcast(bc), ALU.is_equal).then_inc(S("topk"), 1)
                dve.wait_ge(S("topk"), k0 + 2)
                dve.tensor_tensor(oh, oh, io, ALU.mult).then_inc(S("topk"), 1)
                dve.wait_ge(S("topk"), k0 + 3)
                dve.tensor_reduce(i1, oh, AX.X, ALU.min).then_inc(S("topk"), 1)
                dve.wait_ge(S("topk"), k0 + 4)
                dve.tensor_tensor(oh, io, i1.unsqueeze(2).to_broadcast(bc), ALU.is_equal).then_inc(S("topk"), 1)
                dve.wait_ge(S("topk"), k0 + 5)
            dve.wait_ge(S("silu_done"), NB + CREDIT)
            best(gl[:, :, :], m1, t8[0], 0)
            dve.scalar_tensor_tensor(t8[1].rearrange("p t e -> p (t e)"), t8[0].rearrange("p t e -> p (t e)"), -3e38,
                                     gl[:, :, :].rearrange("p t e -> p (t e)"), ALU.mult, ALU.add).then_inc(S("top_x"), 1)
            dve.wait_ge(S("top_x"), 1)
            dve.tensor_reduce(m2, t8[1], AX.X, ALU.max).then_inc(S("topk"), 1)
            dve.wait_ge(S("topk"), 6)
            dve.tensor_tensor(df, m2, m1, ALU.subtract).then_inc(S("topk"), 1)
            dve.tensor_tensor(t8[2], t8[1], m2.unsqueeze(2).to_broadcast(bc), ALU.is_equal).then_inc(S("topk"), 1)
            dve.wait_ge(S("topk"), 8)
            dve.tensor_tensor(t8[2], t8[2], io, ALU.mult).then_inc(S("topk"), 1)
            dve.wait_ge(S("topk"), 9)
            dve.tensor_reduce(i1, t8[2], AX.X, ALU.min).then_inc(S("topk"), 1)
            dve.wait_ge(S("topk"), 10)
            dve.tensor_tensor(t8[2], io, i1.unsqueeze(2).to_broadcast(bc), ALU.is_equal).then_inc(S("topk"), 1)
            dve.wait_ge(S("top_e"), 1)
            dve.wait_ge(S("topk"), 11)
            dve.tensor_scalar(m1, df, 1.0, None, ALU.add).then_inc(S("topk"), 1)
            dve.wait_ge(S("topk"), 12)
            dve.reciprocal(m1, m1).then_inc(S("topk"), 1)
            dve.wait_ge(S("topk"), 13)
            dve.tensor_tensor(m2, df, m1, ALU.mult).then_inc(S("topk"), 1)
            dve.tensor_tensor(t8[0], t8[0], m1.unsqueeze(2).to_broadcast(bc), ALU.mult).then_inc(S("topk"), 1)
            dve.wait_ge(S("topk"), 15)
            dve.tensor_tensor(t8[2], t8[2], m2.unsqueeze(2).to_broadcast(bc), ALU.mult).then_inc(S("topk"), 1)
            dve.wait_ge(S("topk"), 16)
            dve.wait_ge(S("zeros"), 4)
            dve.tensor_tensor(comb[:, :, 0:E], t8[0], t8[2], ALU.add).then_inc(S("top_all"), 1)
            dve.wait_ge(S("top_all"), 1)
            for r in range(2):
                dve.wait_ge(S(f"cst_out{r}"), 16 * NB + 32)
            dve.wait_ge(S("beta_out"), 16)
            with dve.Fori(0, NB) as b:
                done = 0
                at = {}

                def filters(n):
                    nonlocal done
                    for _ in range(n):
                        if done == len(FIRS):
                            return
                        kind, k = FIRS[done]
                        dst = (firs if kind == "s" else firl)[:, bass.ds(b, 1), :].squeeze(1)
                        off = PADV - 2 + k if kind == "s" else k
                        src = vT[:, bass.ds(b, 1), off:off + L].squeeze(1)
                        tap = col("fs" if kind == "s" else "fl", k)
                        if k == 0:
                            op = dve.tensor_scalar(dst, src, tap, None, ALU.mult)
                        else:
                            dve.wait_ge(S("fir"), b * len(FIRS) + (at[kind] + 1))
                            op = dve.scalar_tensor_tensor(dst, src, tap, dst, ALU.mult, ALU.add)
                        op.then_inc(S("fir"), 1)
                        at[kind] = done
                        done += 1
                dve.wait_ge(S("cs_turned"), b + 1)
                dve.tensor_copy(cs, comb[:, bass.ds(b * TPB, TPB), :]).then_inc(S("cs_ready"), 1)
                for e in range(NX):
                    dve.wait_ge(S("y_mm"), b * 10 + (e + 1 + CREDIT))
                    for q in range(TPB):
                        y = pb[4 + e % 2][:, q * P:(q + 1) * P]
                        t = b * TPB + q
                        dst = acc[:, bass.ds(t, 1), :].squeeze(1)
                        weight = comb[:, bass.ds(t, 1), e:e + 1].squeeze(1)
                        if e == 0:
                            op = dve.tensor_scalar(dst, y, weight, None, ALU.mult)
                        else:
                            dve.wait_ge(S("y_added"), b * 40 + (4 * (e - 1) + q + 1 + ACCC))
                            op = dve.scalar_tensor_tensor(dst, y, weight, dst, ALU.mult, ALU.add)
                        op.then_inc(S("y_added"), 1)
                        filters(1)
                dve.wait_ge(S("y_mm"), b * 10 + (10 + CREDIT))
                dve.wait_ge(S("y_added"), b * 40 + (36 + ACCC))
                dst = acc[:, bass.ds(b * TPB, TPB), :]
                dve.tensor_tensor(dst, dst, pb[5][:, :].rearrange("p (q d) -> p q d", q=TPB),
                                  ALU.add).then_inc(S("y_added"), 4)
                assert done == len(FIRS)
            dve.wait_ge(S("y_mm"), 10 * NB + CREDIT)
            dve.memset(S4, 0.0).then_inc(S("sc_s4"), 1)
            dve.memset(Sb, 0.0).then_inc(S("sc_sb"), 1)

            def spread(dst, src):
                return dve.tensor_tensor(dst.rearrange("p b (h c) -> p b h c", h=H),
                                         src.unsqueeze(2).to_broadcast([P, NB, H, C]),
                                         blocks4.unsqueeze(1).to_broadcast([P, NB, H, C]), ALU.mult)
            with dve.Fori(0, NCH // 2) as pair:
                n0 = pair * 2
                for r in range(2):
                    n = n0 + r
                    dve.wait_ge(S("sc_u4"), n + 1 + CREDIT)
                    dve.wait_ge(S("sc_o"), n + CREDIT)
                    spread(Ub, U4).then_inc(S("sc_ub"), 1)
                    dve.wait_ge(S("sc_s4"), n + 2)
                    dve.wait_ge(S("sc_o"), n + 1 + CREDIT)
                    spread(Sb, S4).then_inc(S("sc_sb"), 1)
            with dve.Fori(0, NB // 2) as pair:
                b0 = pair * 2
                for r in range(2):
                    b = b0 + r
                    dve.wait_ge(S("fl_mm"), b + 1 + CREDIT)
                    dve.tensor_tensor(lg[:, bass.ds(b * TPB, TPB)].rearrange("p t h c -> p t (h c)"),
                                      pb[4 + r][:, 0:64].rearrange("p (q n) -> p q n", q=TPB),
                                      rows[:, 0:16].unsqueeze(1).to_broadcast([P, TPB, 16]),
                                      ALU.add).then_inc(S("fl_done"), 1)
            dve.wait_ge(S("fl_done"), NB + CREDIT)
            dve.wait_ge(S("itau"), 1)
            b3 = [P, NT, H, 3]
            dve.tensor_tensor(ft3(2), lg[:, :, :, 0:3],
                              itau.unsqueeze(1).unsqueeze(3).to_broadcast(b3), ALU.mult).then_inc(S("fg"), 1)
            dve.wait_ge(S("fg"), 1)
            dve.tensor_reduce(ftx(0), ft3(2), AX.X, ALU.max).then_inc(S("fg"), 1)
            dve.wait_ge(S("fg"), 2)
            dve.tensor_tensor(ft3(2), ft3(2), ftx(0).unsqueeze(3).to_broadcast(b3), ALU.subtract).then_inc(S("fg"), 1)
            dve.wait_ge(S("fg_e"), 2)
            dve.tensor_reduce(ftx(0), ft3(2), AX.X, ALU.add).then_inc(S("fg"), 1)
            dve.tensor_scalar(ftx(1), ftx(1), 1.0, None, ALU.add).then_inc(S("fg"), 1)
            dve.wait_ge(S("fg"), 5)
            dve.reciprocal(ftx(0), ftx(0)).then_inc(S("fg"), 1)
            dve.reciprocal(ftx(1), ftx(1)).then_inc(S("fg"), 1)
            dve.wait_ge(S("fg"), 7)
            dve.tensor_scalar(ftx(5), ftx(1), MAX_FLOOR - MIN_FLOOR, 1.0 - MAX_FLOOR, ALU.mult, ALU.add).then_inc(S("fg"), 1)
            dve.wait_ge(S("fg"), 8)
            pv = PG[:, :, 3, :]
            dve.tensor_tensor(pv, ftx(5), ftx(1), ALU.mult).then_inc(S("fg"), 1)
            dve.wait_ge(S("fg"), 9)
            dve.tensor_scalar(ftx(5), pv, -1.0, 1.0, ALU.mult, ALU.add).then_inc(S("fg"), 1)
            dve.wait_ge(S("fg"), 10)
            dve.tensor_tensor(ftx(5), ftx(5), ftx(0), ALU.mult).then_inc(S("pg_ready"), 1)
            dve.wait_ge(S("pg_ready"), 1)
            dve.tensor_tensor(PG[:, :, 0:3, :], ft3(2).rearrange("p t h c -> p t c h"),
                              ftx(5).unsqueeze(2).to_broadcast([P, NT, 3, H]), ALU.mult).then_inc(S("pg_ready"), 1)
            paths = [firs, firl, dT, vtok]

            def weigh(b, r):
                dve.wait_ge(S("fp_mm"), b + 1 + CREDIT)
                dve.wait_ge(S("fz_add"), 3 * (b + 1))
                for c in range(4):
                    dve.tensor_tensor(mC[:, c], pb[c][:, :], paths[c][:, bass.ds(b, 1), :].squeeze(1),
                                      ALU.mult).then_inc(S("fz_mul"), 1)

            def gated(b, r):
                dve.wait_ge(S("fz_rt"), b + 2)
                dve.reciprocal(rr, rr).then_inc(S("fz_rec"), 1)
                dve.wait_ge(S("fz_rec"), b + 1)
                dve.wait_ge(S("fz_wo"), b + 1)
                dve.scalar_tensor_tensor(oN, oT[:, r], col("nw"), rr, ALU.mult, ALU.mult).then_inc(S("fz_n"), 1)
                dve.wait_ge(S("fz_wo"), b + 2)
                dve.wait_ge(S("x1_done"), b + 1)
                ga = acc[:, bass.ds(b * TPB, TPB), :]
                dve.tensor_tensor(sgt, pb[5][:, :].rearrange("p (q d) -> p q d", q=TPB), ga,
                                  ALU.mult).then_inc(S("fz_sg"), 1)
                dve.wait_ge(S("fz_sg"), b + 2)
                dve.wait_ge(S("ld_xr"), (b + 1) * 16)
                dve.tensor_tensor(ga, sgt, xr, ALU.add).then_inc(S("x1_done"), 1)
            dve.wait_ge(S("g_ready"), 1)
            staggered(dve, weigh, gated)
            vector_layer1(dve)


def kernel(**inputs):
    import concourse.bacc as bacc
    from concourse.bass_utils import run_bass_kernel_spmd

    g = {k: np.asarray(v) for k, v in inputs.items()}
    A, F, A1, F1 = "L0_attn_", "L0_ffn_", "L1_attn_", "L1_ffn_"
    b1 = np.concatenate([g[F + "b1"], g[F + "bs1"][None]], 0)
    small = np.concatenate([
        g[A + "conv_w_q"], g[A + "conv_w_k"], g[A + "conv_w_v"],
        g[A + "fir_short_w"].reshape(P, 3), g[A + "fir_long_w"].reshape(P, 31),
        g[A + "b_fuse1"].reshape(2, P).T, np.tile(g[A + "norm_w"], H)[:, None],
        b1.reshape(NX * MB, P).T, g[A1 + "bq"][:, None], g[A1 + "bk"][:, None],
        g[F1 + "bn_gamma"][:, None], g[F1 + "bn_beta"][:, None]], 1)
    laid = {
        "x": g[A + "hidden_states"].reshape(TOK, D), "con": shape_constants(), "small": small,
        "bf2": g[A + "b_fuse2"], "tau": g[A + "others_log_tau"], "gb": g[F + "gate_b"],
        "Wq": g[A + "W_q"], "Wk": g[A + "W_k"], "Wv": g[A + "W_v"], "Wb": g[A + "W_b"], "gw": g[F + "gate_w"],
        "Wo": g[A + "W_o"], "Wf1": g[A + "W_fuse1"], "Wf2": g[A + "W_fuse2"],
        "b2": g[F + "b2"], "bs2": g[F + "bs2"][None], "w1": g[F + "w1"], "ws1": g[F + "ws1"],
        "w2": g[F + "w2"], "ws2": g[F + "ws2"],
        "aWq": g[A1 + "Wq"].T, "aWk": g[A1 + "Wk"].T,
        "wqk": g[F1 + "w_q"].reshape(2, PH, P, D).transpose(2, 0, 1, 3),
        "keys": g[F1 + "keys_p"].transpose(3, 2, 0, 1),
        "down": g[F1 + "down"][:NE].T, "up": g[F1 + "up"][:NE],
    }
    laid = {"in_" + k: np.ascontiguousarray(v) for k, v in laid.items()}
    nc = bacc.Bacc("TRN2", target_bir_lowering=False, num_devices=1)
    aps = {k[3:]: nc.dram_tensor(k, v.shape, F32, kind="ExternalInput").ap() for k, v in laid.items()}
    out = nc.dram_tensor("out", (TOK, D), F32, kind="ExternalOutput").ap()
    gated_two_layer_kernel(nc, aps, out)
    r = run_bass_kernel_spmd(nc, [laid], core_ids=[0])
    return r.results[0]["out"].reshape(NB, L, D)
```

```python
from contextlib import ExitStack

import numpy as np

import concourse.bass as bass
from concourse import mybir

F32 = mybir.dt.float32
ALU = mybir.AluOpType
ACT = mybir.ActivationFunctionType
AX = mybir.AxisListType

NB, L, D = 8, 512, 128
TOK = NB * L
P = 128
TPB = L // P
NT = TOK // P
H, DK = 4, 32
C = 32
NCH = L // C
ITEMS = NB * NCH
PADV = 30
VW = PADV + L
E, HID = 8, 512
NX = E + 1
MB = HID // P
EA = 5
YA = EA + 1
SPE = NB // 2
PH, NK, PK = 8, 32, 8
NE = NK * NK
EB = NE // P
EPS = 1e-5
MIN_FLOOR, MAX_FLOOR = 0.01, 0.1
CREDIT = 2


def shape_constants():
    p = np.arange(P)[:, None]
    c = np.arange(P)[None, :]
    i = np.arange(C)[None, :]
    parts = [
        p == c,
        p // C == c // C,
        np.ones((P, P)),
        p % C == i,
        -1.0 * (i > p % C),
        i >= p % C,
        np.broadcast_to(np.arange(E)[None, :] - E, (P, E)),
        np.full((P, 1), 1e-6), np.full((P, 1), EPS),
    ]
    return np.ascontiguousarray(np.concatenate([np.asarray(x, np.float32) for x in parts], 1))


O_ID, O_BLK, O_ONE, O_STK, O_GRAM, O_LOC, O_IOTA, O_E6, O_E5 = 0, 128, 256, 384, 416, 448, 480, 488, 489
NCONST = 490

SMALLS, SMALL = {}, 0
for _n, _w in (("cw", 12), ("fs", 3), ("fl", 31), ("bf1", 2), ("nw", 1), ("b1", NX * MB), ("bq", 1), ("bk", 1),
               ("gamma", 1), ("bbeta", 1)):
    SMALLS[_n] = (SMALL, _w)
    SMALL += _w


def gated_two_layer_kernel(nc, a, out, debug=None):
    ctx = ExitStack()
    with ctx:
        def sb(name, shape):
            return ctx.enter_context(nc.sbuf_tensor(name, shape, F32))

        def sem(name):
            return ctx.enter_context(nc.semaphore(name))

        con = sb("con", [P, NCONST])
        small = sb("small", [P, SMALL])
        rows = sb("rows", [P, 16 + H + E])
        xT = sb("xT", [P, TOK])
        stats = sb("stats", [P, NT, 6])
        mean = sb("mean", [P, NT])
        rstd = sb("rstd", [P, NT])
        lntmp = sb("lntmp", [P, 3, NT])
        wproj = sb("wproj", [P, 3, D])
        wo = sb("wo", [P, D])
        wb = sb("wb", [P, H])
        wf1 = sb("wf1", [P, 4, 2 * D])
        wf2 = sb("wf2", [P, 2, 16])
        gatew = sb("gatew", [P, E])
        b2 = sb("b2", [NX, D])
        acc = sb("acc", [P, NT, D])
        bnc_t = sb("bnc", [P, 4])
        scal = sb("scal", [P, 4 * NT + TPB * NX + H])
        ctT = sb("ctT", [NX, L])
        RA = sb("RA", [P, NT * D])
        RK = sb("RK", [P, ITEMS * 2 * C])
        RV = sb("RV", [P, NB * VW])
        RF = sb("RF", [P, 2 * TOK])
        RW = sb("RW", [P, 2 * NX * HID])
        RH = sb("RH", [P, 2 * MB * L])
        RP = sb("RP", [P, H * 16 * 16])
        RS = sb("RS", [P, 3 * NB * C])
        beta_it = sb("beta_it", [P, H, C])
        gl = sb("gl", [P, NT, E])
        comb = sb("comb", [P, NT, NX])

        pb = [ctx.enter_context(nc.psum_tensor(f"bank{i}", [P, 512], F32)) for i in range(8)]

        ident = con[:, O_ID:O_ID + P]
        blocks = con[:, O_BLK:O_BLK + P]
        ones = con[:, O_ONE:O_ONE + P]
        stack = con[:, O_STK:O_STK + C]
        gl_mask = con[:, O_GRAM:O_GRAM + C]
        loc_mask = con[:, O_LOC:O_LOC + C]
        iota_e = con[:, O_IOTA:O_IOTA + E]
        eps6 = con[:, O_E6:O_E6 + 1]
        eps5 = con[:, O_E5:O_E5 + 1]

        def col(name, n=None):
            o, w = SMALLS[name]
            return small[:, o:o + w] if n is None else small[:, o + n:o + n + 1]

        x_in = RA[:, :].rearrange("p (t d) -> p t d", d=D)
        att = RA[:, :].rearrange("p (h j i) -> p h j i", h=H, j=C)
        dT = RA[:, :].rearrange("p (b l) -> p b l", b=NB)
        kq = RK[:, :].rearrange("p (n s c) -> p n s c", s=2, c=C)
        vT = RV[:, :].rearrange("p (b l) -> p b l", b=NB)
        firs = RF[:, 0:TOK].rearrange("p (b l) -> p b l", b=NB)
        firl = RF[:, TOK:2 * TOK].rearrange("p (b l) -> p b l", b=NB)
        w1 = RW[:, 0:NX * HID].rearrange("p (e n) -> p e n", e=NX)
        w2 = RW[:, NX * HID:].rearrange("p (e m d) -> p e m d", e=NX, m=MB)
        hT = RH[:, :].rearrange("p (r m l) -> p r m l", r=2, m=MB)

        beta_d = nc.dram_tensor("beta_d", (H, ITEMS, C), F32, kind="Internal").ap()
        gram_d = nc.dram_tensor("gram_d", (ITEMS, H, C, C), F32, kind="Internal").ap()
        inv_d = nc.dram_tensor("inv_d", (ITEMS, H, C, C), F32, kind="Internal").ap()
        lv_d = nc.dram_tensor("lv_d", (P, ITEMS, 2, C), F32, kind="Internal").ap()

        s = {}

        def S(name):
            if name not in s:
                s[name] = sem(name)
            return s[name]

        block = ctx.enter_context(nc.Block())
        x_d = a["x"].rearrange("(b q p) d -> b p q d", p=P, q=TPB)
        out_d = out.rearrange("(b q p) d -> b p q d", p=P, q=TPB)

        def seq(b, n=L):
            return bass.ds(b * n, n)

        def staggered(eng, lead, follow):
            lead(0, 0)
            with eng.Fori(0, (NB - 2) // 2) as pair:
                b = pair * 2
                for r in range(2):
                    lead(b + (r + 1), 1 - r)
                    follow(b + r, r)
            lead(NB - 1, 1)
            follow(NB - 2, 0)
            follow(NB - 1, 1)

        xst = RH[:, 0:2 * L].rearrange("p (r q d) -> p r q d", r=2, q=TPB)
        xs = RH[:, 2 * L:4 * L].rearrange("p (r l) -> p r l", r=2)
        top = RH[:, 4 * L:8 * L].rearrange("p (n x) -> p n x", n=8)
        beta_sb = acc[0:H, :, :].rearrange("p t d -> p (t d)")
        CW = 3 + L
        pads = RF[:, 0:6 * CW].rearrange("p (r s l) -> p r s l", r=2, s=3)
        cacc = RF[:, 6 * CW:6 * CW + 2 * 2 * L]
        cv0 = RF[:, 6 * CW:6 * CW + 3 * L].rearrange("p (s l) -> p s l", s=3)
        cv1 = RH[:, 5 * L:8 * L].rearrange("p (s l) -> p s l", s=3)
        cacc = [cv0, cv1]
        sq = RH[:, 0:4 * L].rearrange("p (r l) -> p r l", r=2)
        rn = RW[:, 0:4 * L].rearrange("p (r l) -> p r l", r=2)
        KX = RH[:, 0:2 * L].rearrange("p (r n c) -> p r n c", r=2, n=4)
        kv_in = RH[:, 2 * L:6 * L].rearrange("p (r s n c) -> p r s n c", r=2, s=2, n=NCH)
        kt = RH[:, 6 * L:8 * L].rearrange("p (r n c) -> p r n c", r=2, n=NCH)
        cst = RF[:, 0:2 * NCH * 3 * C].rearrange("p (r n s c) -> p r n s c", r=2, n=NCH, s=3)
        blocks4 = blocks.rearrange("p (h c) -> p h c", h=H)
        vtok = vT[:, :, PADV:VW]
        tw = scal[:, 0:4 * NT].rearrange("p (n t) -> p n t", n=4)
        cs = scal[:, 4 * NT:4 * NT + TPB * NX].rearrange("p (q e) -> p q e", q=TPB)
        itau = scal[:, 4 * NT + TPB * NX:4 * NT + TPB * NX + H]
        cT = ctT[:, :]
        SW = NB * P
        assert 2 * SW + 2 * NB * C <= EA * HID and 2 * SW <= EA * HID
        Kb = RW[:, 0:SW].rearrange("p (b c) -> p b c", b=NB)
        Gb = RW[:, SW:2 * SW].rearrange("p (b c) -> p b c", b=NB)
        lv = RW[:, 2 * SW:2 * SW + 2 * NB * C].rearrange("p (b s c) -> p b s c", b=NB, s=2)
        Wn = RW[:, NX * HID:NX * HID + SW].rearrange("p (b c) -> p b c", b=NB)
        Ub = RW[:, NX * HID + SW:NX * HID + 2 * SW].rearrange("p (b c) -> p b c", b=NB)
        Sb = RP[:, 0:SW].rearrange("p (b c) -> p b c", b=NB)
        U4 = RS[:, 0:NB * C].rearrange("p (b c) -> p b c", b=NB)
        S4 = RS[:, NB * C:2 * NB * C].rearrange("p (b c) -> p b c", b=NB)
        kq5 = RK[:, :].rearrange("p (b n s c) -> p b n s c", b=NB, n=NCH, s=2)
        zero = RS[:, 2 * NB * C:]
        hidT = RH[:, 0:4 * L].rearrange("p (r m l) -> p r m l", r=2, m=2)
        lg = RH[:, 4 * L:5 * L].rearrange("p (t h c) -> p t h c", t=NT, h=H)
        PG = RH[:, 5 * L:6 * L].rearrange("p (t c h) -> p t c h", t=NT, c=4)
        ft = RH[:, 6 * L:8 * L].rearrange("p (n x) -> p n x", n=8)

        def ftx(k):
            return ft[:, k, :].rearrange("p (t h) -> p t h", h=H)

        def ft3(k):
            return RH[:, 6 * L + k * P:6 * L + (k + 3) * P].rearrange("p (t h c) -> p t h c", h=H, c=3)
        Pst = RW[:, 0:8 * L].rearrange("p (r q c d) -> p r q c d", r=2, q=TPB, c=4)
        mC = RW[:, 8 * L:12 * L].rearrange("p (c l) -> p c l", c=4)
        oT = RW[:, 12 * L:14 * L].rearrange("p (r l) -> p r l", r=2)
        sqo = RW[:, 14 * L:15 * L]
        rr = RW[:, 15 * L:16 * L]
        oN = RW[:, 16 * L:17 * L]
        xr = RW[:, 17 * L:18 * L].rearrange("p (q d) -> p q d", q=TPB)
        sgt = RP[:, 0:L].rearrange("p (q d) -> p q d", q=TPB)

        CONVC = 24
        ACCC = 8
        FIRS = [("s", 0), ("l", 0), ("s", 1), ("l", 1), ("s", 2)] + [("l", k) for k in range(2, 31)]
        FB = 4
        FA = len(FIRS) - FB * (NX - EA)

        def over_steps(eng, step):
            for e in range(EA, NX):
                with eng.Fori(0, SPE) as i:
                    n = i + (e - EA) * SPE
                    step(n, 2 * n, i, e)

        def moments(dve, x, sems, loaded):
            v, var, std, done = sems
            if loaded:
                dve.wait_ge(S(loaded), 16)
            with dve.Fori(0, NB) as b:
                for q in range(TPB):
                    op = dve.bn_stats(stats[:, bass.ds(b * TPB + q, 1), :].squeeze(1),
                                      x[:, bass.ds(b * TPB + q, 1), :].squeeze(1))
                op.then_inc(S(v), 1)
            dve.wait_ge(S(v), NB)
            me, mo, se, so = (stats[:, :, k] for k in (1, 4, 2, 5))
            t0, t1, t2 = (lntmp[:, k, :] for k in range(3))
            dve.tensor_tensor(t0, me, mo, ALU.add).then_inc(S(v), 1)
            dve.tensor_tensor(t1, me, mo, ALU.subtract).then_inc(S(v), 1)
            dve.tensor_tensor(t2, se, so, ALU.add).then_inc(S(v), 1)
            dve.wait_ge(S(v), NB + 3)
            dve.tensor_scalar(mean[:, :], t0, 0.5, None, ALU.mult).then_inc(S(v), 1)
            dve.scalar_tensor_tensor(t1, t1, 0.25, t1, ALU.mult, ALU.mult).then_inc(S(v), 1)
            dve.wait_ge(S(v), NB + 5)
            dve.scalar_tensor_tensor(t1, t2, 1.0 / D, t1, ALU.mult, ALU.add).then_inc(S(var), 1)
            dve.wait_ge(S(std), 1)
            dve.reciprocal(rstd[:, :], rstd[:, :]).then_inc(S(done), 1)
            dve.wait_ge(S(done), 1)

        def normed(dve, dst, x, t):
            return dve.tensor_scalar(dst, x[:, bass.ds(t, 1), :].squeeze(1), mean[:, bass.ds(t, 1)],
                                     rstd[:, bass.ds(t, 1)], ALU.subtract, ALU.mult)


        xn2 = RA[:, :].rearrange("p (t d) -> p t d", d=D)
        s1 = RF[:, 0:TOK].rearrange("p (t d) -> p t d", d=D)
        o2 = RF[:, TOK:2 * TOK].rearrange("p (t d) -> p t d", d=D)
        wqk = RK[:, 0:2048].rearrange("p (n d) -> p n d", n=2 * PH)
        Wt = RK[:, 0:2048].rearrange("p (r e n) -> p r e n", r=2, e=EB)
        keys = RK[:, 2048:2560].rearrange("p (n k) -> p n k", n=2 * PH)
        down = RK[:, 2560:3584]
        up = RK[:, 3584:4608].rearrange("p (e d) -> p e d", e=EB)
        aWq = RK[:, 4608:4736]
        aWk = RK[:, 4736:4864]
        WK = RK[:, 5120:5632]
        xb = RK[:, 6144:7168].rearrange("p (r l) -> p r l", r=2)
        qk = RW[:, 0:2048].rearrange("p (r s l) -> p r s l", r=2, s=2)
        Pr = RW[:, 2048:3072].rearrange("p (r l) -> p r l", r=2)
        PT = RW[:, 3072:4096].rearrange("p (r n s) -> p r n s", r=2, n=TPB)
        xsum = RW[:, 4096:4352].rearrange("p (r d) -> p r d", r=2)
        atmp = RW[:, 4352:4608].rearrange("p (r d) -> p r d", r=2)
        ac = RW[:, 4608:4624].rearrange("p (r n) -> p r n", r=2)
        bqs = lntmp[:, 0, 0:1]
        bnst = lntmp[:, 1:3, :].rearrange("p a b -> p (a b)")[:, 0:6 * NB]
        bnc = bnc_t[:, :]
        RING = 4
        Z = RW[:, 0:4096].rearrange("p (k e) -> p k e", k=RING)
        SG = RW[:, 4096:8192].rearrange("p (k e) -> p k e", k=RING)
        MK = RV[:, 0:4096].rearrange("p (k e) -> p k e", k=RING)
        sim = RW[:, 8192:9216].rearrange("p (r h s k) -> p r h s k", r=2, h=PH, s=2)
        cand = RP[:, 0:512].rearrange("p (h a b) -> p h a b", h=PH, a=PK)
        tv = RP[:, 512:768].rearrange("p (r h s k) -> p r h s k", r=2, h=PH, s=2)
        t8 = RP[:, 768:896].rearrange("p (r h k) -> p r h k", r=2, h=PH)
        AB = [RH[:, :].rearrange("p (e l) -> p e l", e=EB), RA[:, :].rearrange("p (e l) -> p e l", e=EB)]
        ZP = 7
        SCALE = float(D) ** -0.5

        def following(b, q, r):
            return (b, q + 1, r) if q + 1 < TPB else (b + 1, 0, 1 - r)

        def preceding(b, q, r):
            return (b, q - 1, r) if q > 0 else (b - 1, TPB - 1, 1 - r)

        def over_tiles(eng, tile):
            tile(0, 0, 0, "first")
            with eng.Fori(0, NB // 2 - 1) as pair:
                for r in range(2):
                    b = pair * 2 + r
                    for q in range(1, TPB):
                        tile(b, q, r, "")
                    tile(b + 1, 0, 1 - r, "")
            for b in (NB - 2, NB - 1):
                for q in range(1, TPB):
                    tile(b, q, b % 2, "last" if (b, q) == (NB - 1, TPB - 1) else "")
                if b == NB - 2:
                    tile(b + 1, 0, 1 - b % 2, "")

        def final(b):
            return isinstance(b, int) and b == NB - 1

        def sync_layer1(sp):
            with sp.Fori(0, NB) as b:
                sp.wait_ge(S("y_done"), b + 1)
                sp.dma_start(out_d[bass.ds(b, 1)].squeeze(0), acc[:, bass.ds(b * TPB, TPB), :]).then_inc(S("out_done"), 16)
            sp.wait_ge(S("out_done"), 16 * NB)

        def pool_layer1(pool):
            pool.sem_inc(S("z_pool"), 1)

            def tile(b, q, r, last):
                t = b * TPB + q
                pool.wait_ge(S("sm_ready"), t + 2)
                for h in range(ZP):
                    pool.wait_ge(S("mk_done"), t * PH + (h + 1))
                    pool.tensor_tensor(Z[:, h % RING].rearrange("p (i j) -> p i j", i=NK),
                                       sim[:, q % 2, h, 0, :].unsqueeze(2).to_broadcast([P, NK, NK]),
                                       sim[:, q % 2, h, 1, :].unsqueeze(1).to_broadcast([P, NK, NK]),
                                       ALU.add).then_inc(S("z_pool"), 1)
            with pool.Fori(0, NB) as b:
                for q in range(TPB):
                    tile(b, q, 0, False)

        def tensor_layer1(pe):
            pe.sem_inc(S("at_s"), CREDIT)
            pe.sem_inc(S("at_t"), CREDIT)
            pe.sem_inc(S("at_v"), CREDIT)
            pe.sem_inc(S("tc"), RING)
            pe.sem_inc(S("pr_mm"), CREDIT)
            pe.sem_inc(S("o2_mm"), CREDIT)
            pe.wait_ge(S("ld2"), 96)
            pe.wait_ge(S("x1_done"), NB + 1)
            for n in range(2 * PH):
                s_, h = n // PH, n % PH
                mm = pe.matmul(pb[7][:, (2 * h + s_) * NK:(2 * h + s_ + 1) * NK], wqk[:, n, :], keys[:, n, :],
                               start=True, stop=True)
            mm.then_inc(S("wk_mm"), 1)
            with pe.Fori(0, NB // 2) as pair:
                for r in range(2):
                    pe.wait_ge(S("x2_ready"), pair * 2 + (r + 1))
                    pe.wait_ge(S("x2_copied"), pair * 2 + (r + 1))
                    for q in range(TPB):
                        mm = pe.transpose(pb[r][:, q * P:(q + 1) * P], xst[:, r, q, :], ident)
                    mm.then_inc(S("x2_turned"), 1)
            pe.wait_ge(S("x2_copied"), NB + CREDIT)

            def attend(b, r):
                def scores(q):
                    pe.wait_ge(S("at_p"), b * TPB + (q + 1))
                    pe.matmul(pb[2 + q % 2][:, :], qk[:, r, 0, q * P:(q + 1) * P], qk[:, r, 1, :],
                              start=True, stop=True).then_inc(S("at_s"), 1)

                def turn(q):
                    pe.wait_ge(S("at_p"), b * TPB + (q + 1 + CREDIT))
                    pe.wait_ge(S("at_c"), b * TPB + (q + 1))
                    for n in range(TPB):
                        mm = pe.transpose(pb[4 + q % 2][:, n * P:(n + 1) * P], Pr[:, q % 2, n * P:(n + 1) * P], ident)
                    mm.then_inc(S("at_t"), 1)

                def values(q):
                    pe.wait_ge(S("at_c"), b * TPB + (q + 1 + CREDIT))
                    pe.wait_ge(S("at_o"), b * TPB + (q + 1))
                    if q == 0:
                        pe.wait_ge(S("xsum_ready"), b + 1)
                    for n in range(TPB):
                        mm = pe.matmul(pb[6 + q % 2][:, 0:D], PT[:, q % 2, n, :],
                                       xn2[:, bass.ds(b * TPB + n, 1), :].squeeze(1),
                                       start=(n == 0), stop=(n == TPB - 1))
                    mm.then_inc(S("at_v"), 1)

                pe.wait_ge(S("qk_ready"), 2 * b + 1)
                for k, wgt in enumerate((aWq, aWk)):
                    mm = pe.matmul(pb[k][:, :], wgt, xT[:, seq(b)], start=True, stop=True)
                mm.then_inc(S("pr_mm"), 1)
                pe.wait_ge(S("at_o"), b * TPB + 1)
                for n in range(TPB):
                    mm = pe.matmul(pb[6][:, 0:D], ones, xn2[:, bass.ds(b * TPB + n, 1), :].squeeze(1),
                                   start=(n == 0), stop=(n == TPB - 1))
                mm.then_inc(S("xsum_mm"), 1)
                pe.wait_ge(S("qk_ready"), 2 * b + 3)
                scores(0)
                scores(1)
                for q in range(TPB):
                    turn(q)
                    if q + 2 < TPB:
                        scores(q + 2)
                    if q >= 1:
                        values(q - 1)
                values(TPB - 1)
            with pe.Fori(0, NB // 2) as pair:
                attend(pair * 2, 0)
                attend(pair * 2 + 1, 1)

            pe.wait_ge(S("at_o"), NT + CREDIT)

            def scores_of(b, q, r):
                t = b * TPB + q
                pe.wait_ge(S("xb_ready"), b + 1)
                pe.wait_ge(S("sm_ready"), t + 1)
                pe.matmul(pb[0][:, :], xb[:, r, q * P:(q + 1) * P], WK, start=True, stop=True).then_inc(S("sm_mm"), 1)

            def hidden_of(b, es):
                for e in es:
                    pe.wait_ge(S("a_ready"), b * EB + (e + 1))
                    pe.matmul(pb[2 + e % 2][:, :], down[:, e * P:(e + 1) * P], xT[:, seq(b)],
                              start=True, stop=True).then_inc(S("a_mm"), 1)

            def output_of(b, q, r):
                t = b * TPB + q
                pe.wait_ge(S("wt_done"), 2 * t + 3)
                pe.wait_ge(S("o2_done"), t + 1)
                for e in range(EB):
                    mm = pe.matmul(pb[1][:, 0:D], Wt[:, q % 2, e, :], up[:, e, :],
                                   start=(e == 0), stop=(e == EB - 1))
                mm.then_inc(S("o2_mm"), 1)

            def tile(b, q, r, where):
                t = b * TPB + q
                if where != "last":
                    scores_of(*following(b, q, r))
                for h in range(PH):
                    pe.wait_ge(S("mk_done"), t * PH + (h + 1 + RING))
                    if h == 0 and where != "first":
                        pe.wait_ge(S("wt_done"), 2 * t - 1)
                    for e in range(EB):
                        mm = pe.matmul(pb[4 + 2 * (q % 2) + e // 4][:, (e % 4) * P:(e % 4 + 1) * P],
                                       MK[:, h % RING, e * P:(e + 1) * P],
                                       ident, start=(h == 0 and e % 4 == 0), stop=(h == PH - 1 and e % 4 == 3),
                                       is_transpose=True, skip_group_check=True)
                    mm.then_inc(S("tc"), 1)
                    if h == 2 and where != "first":
                        output_of(*preceding(b, q, r))
                    if h == 1 and not final(b):
                        hidden_of(b + 1, (2 * q, 2 * q + 1))
                if where == "last":
                    output_of(b, q, r)
            scores_of(0, 0, 0)
            hidden_of(0, range(EB))
            over_tiles(pe, tile)

        def scalar_layer1(act):
            act.sem_inc(S("x2_copied"), CREDIT)
            act.sem_inc(S("at_p"), CREDIT)
            act.sem_inc(S("qk_ready"), 1)
            act.sem_inc(S("sm_ready"), 1)
            act.sem_inc(S("at_c"), CREDIT)
            act.sem_inc(S("a_ready"), 2)
            act.sem_inc(S("o2_done"), 1)
            act.sem_inc(S("sg_done"), RING)
            act.wait_ge(S("sc_o"), NCH + 1)
            for dst, src in ((wqk, a["wqk"].rearrange("p s h d -> p (s h) d")), (keys, a["keys"].rearrange("p s h k -> p (s h) k")),
                             (down, a["down"]), (up, a["up"].rearrange("(e p) d -> p e d", p=P)),
                             (aWq, a["aWq"]), (aWk, a["aWk"])):
                act.dma_start(dst, src).then_inc(S("ld2"), 16)
            act.wait_ge(S("ln2_var"), 1)
            act.activation(rstd[:, :], lntmp[:, 1, :], ACT.Sqrt, bias=eps5).then_inc(S("ln2_std"), 1)
            act.wait_ge(S("wk_mm"), 1)
            act.activation(WK, pb[7][:, :], ACT.Copy).then_inc(S("wk_ready"), 1)
            with act.Fori(0, NB // 2) as pair:
                for r in range(2):
                    b = pair * 2 + r
                    act.wait_ge(S("x2_turned"), b + 1)
                    act.activation(xT[:, seq(b)], pb[r][:, :], ACT.Copy)
                    act.activation(xn2[:, bass.ds(b * TPB, TPB), :], xst[:, r], ACT.Copy).then_inc(S("x2_copied"), 1)
            act.wait_ge(S("bn_var"), 1)
            act.activation(bnc[:, 2:3], bnc[:, 1:2], ACT.Sqrt, bias=eps5).then_inc(S("bn_std"), 1)
            act.wait_ge(S("bq_ready"), 1)

            def attend(b, r):
                act.wait_ge(S("pr_mm"), b + 1 + CREDIT)
                act.wait_ge(S("at_t"), b * TPB + 1)
                act.activation(qk[:, r, 0, :], pb[0][:, :], ACT.Identity, scale=SCALE, bias=bqs).then_inc(S("qk_ready"), 1)
                act.activation(qk[:, r, 1, :], pb[1][:, :], ACT.Identity, bias=col("bk")).then_inc(S("qk_ready"), 1)
                act.wait_ge(S("xsum_mm"), b + 1)
                act.wait_ge(S("at_o"), b * TPB + 1)
                act.activation(xsum[:, r, :], pb[6][:, 0:D], ACT.Copy).then_inc(S("xsum_ready"), 1)

                def soft(q):
                    t = b * TPB + q
                    act.wait_ge(S("at_m"), t + 1)
                    act.wait_ge(S("at_t"), t + 1)
                    act.activation(Pr[:, q % 2, :], pb[2 + q % 2][:, :], ACT.Exp, bias=ac[:, q % 2, 0:1],
                                   accum_out=ac[:, q % 2, 1:2]).then_inc(S("at_p"), 1)

                def turned(q):
                    t = b * TPB + q
                    act.wait_ge(S("at_t"), t + 1 + CREDIT)
                    act.wait_ge(S("at_v"), t + 1)
                    act.activation(PT[:, q % 2].rearrange("p n s -> p (n s)"), pb[4 + q % 2][:, :],
                                   ACT.Copy).then_inc(S("at_c"), 1)
                soft(0)
                for q in range(1, TPB):
                    soft(q)
                    turned(q - 1)
                turned(TPB - 1)
            with act.Fori(0, NB // 2) as pair:
                attend(pair * 2, 0)
                attend(pair * 2 + 1, 1)

            act.wait_ge(S("at_o"), NT + CREDIT)

            def scores_in(b, q, r):
                t = b * TPB + q
                if not (isinstance(b, int) and t < 2):
                    act.wait_ge(S("z_pool"), t * ZP - (ZP - 1))
                    act.wait_ge(S("z_dve"), t * (PH - ZP) - (PH - ZP))
                act.wait_ge(S("sm_mm"), t + 1)
                act.activation(sim[:, q % 2].rearrange("p h s k -> p (h s k)"), pb[0][:, :],
                               ACT.Copy).then_inc(S("sm_ready"), 1)

            def hidden_in(b, r, es):
                for e in es:
                    act.wait_ge(S("a_mm"), b * EB + (e + 1))
                    act.activation(AB[r][:, e, :], pb[2 + e % 2][:, :], ACT.Gelu).then_inc(S("a_ready"), 1)

            def output(b, q, r):
                t = b * TPB + q
                act.wait_ge(S("o2_mm"), t + 3)
                act.activation(o2[:, bass.ds(t, 1), :].squeeze(1), pb[1][:, 0:D], ACT.Copy).then_inc(S("o2_done"), 1)

            def tile(b, q, r, where):
                t = b * TPB + q
                for h in range(PH):
                    if h < ZP:
                        act.wait_ge(S("z_pool"), t * ZP + (h + 2))
                    else:
                        act.wait_ge(S("z_dve"), t * (PH - ZP) + (h - ZP + 1))
                    act.wait_ge(S("mk_done"), t * PH + (h + 1))
                    act.activation(SG[:, h % RING, :], Z[:, h % RING, :], ACT.Sigmoid).then_inc(S("sg_done"), 1)
                    if h == 1 and where != "last":
                        scores_in(*following(b, q, r))
                    if h == 5 and where != "first":
                        output(*preceding(b, q, r))
                if not final(b):
                    if q == 0 and where != "first":
                        act.wait_ge(S("wt_done"), 2 * TPB * b + 1)
                    hidden_in(b + 1, 1 - r, (2 * q, 2 * q + 1))
                if where == "last":
                    output(b, q, r)
            scores_in(0, 0, 0)
            hidden_in(0, 0, range(EB))
            over_tiles(act, tile)
            act.wait_ge(S("o2_done"), NT + 1)
            with act.Fori(0, NB) as b:
                ob = o2[:, bass.ds(b * TPB, TPB), :]
                act.activation(ob, ob, ACT.Silu).then_inc(S("g2_ready"), 1)

        def vector_layer1(dve):
            dve.sem_inc(S("at_o"), CREDIT)
            dve.sem_inc(S("mk_done"), RING)
            dve.sem_inc(S("wt_done"), 1)
            dve.wait_ge(S("x1_done"), NB + 1)
            moments(dve, acc, ("ln2_v", "ln2_var", "ln2_std", "ln2_done"), None)
            with dve.Fori(0, NB // 2) as pair:
                for r in range(2):
                    b = pair * 2 + r
                    dve.wait_ge(S("x2_copied"), b + 1)
                    for q in range(TPB):
                        op = normed(dve, xst[:, r, q, :], acc, b * TPB + q)
                    op.then_inc(S("x2_ready"), 1)
            dve.wait_ge(S("x2_copied"), NB + CREDIT)
            with dve.Fori(0, NB) as b:
                dve.bn_stats(bnst[:, bass.ds(b * 6, 6)], xT[:, seq(b)]).then_inc(S("bn_v"), 1)
            dve.wait_ge(S("bn_v"), NB)
            dve.bn_aggr(bnc[:, 0:2], bnst).then_inc(S("bn_var"), 1)
            dve.wait_ge(S("bn_std"), 1)
            dve.reciprocal(bnc[:, 2:3], bnc[:, 2:3]).then_inc(S("bn_v"), 1)
            dve.tensor_scalar(bqs, col("bq"), SCALE, None, ALU.mult).then_inc(S("bq_ready"), 1)
            dve.wait_ge(S("bn_v"), NB + 1)
            dve.tensor_tensor(bnc[:, 2:3], bnc[:, 2:3], col("gamma"), ALU.mult).then_inc(S("bn_v"), 1)
            dve.wait_ge(S("bn_v"), NB + 2)
            dve.tensor_tensor(bnc[:, 3:4], bnc[:, 2:3], bnc[:, 0:1], ALU.mult).then_inc(S("bn_v"), 1)
            dve.wait_ge(S("bn_v"), NB + 3)
            dve.tensor_tensor(bnc[:, 3:4], col("bbeta"), bnc[:, 3:4], ALU.subtract).then_inc(S("bn_v"), 1)
            dve.wait_ge(S("bn_v"), NB + 4)

            def attend(b, r):
                def top(q):
                    t = b * TPB + q
                    dve.wait_ge(S("at_s"), t + 1 + CREDIT)
                    dve.wait_ge(S("at_o"), t + 1)
                    dve.tensor_reduce(ac[:, q % 2, 0:1], pb[2 + q % 2][:, :], AX.X, ALU.max,
                                      negate=True).then_inc(S("at_m"), 1)

                def rest(q):
                    t = b * TPB + q
                    z, rz, mz = (ac[:, q % 2, k:k + 1] for k in (1, 2, 3))
                    dve.wait_ge(S("at_p"), t + 1 + CREDIT)
                    dve.reciprocal(rz, z).then_inc(S("at_z"), 1)
                    dve.wait_ge(S("at_z"), 3 * t + 1)
                    dve.tensor_tensor(mz, z, rz, ALU.mult).then_inc(S("at_z"), 1)
                    dve.wait_ge(S("at_z"), 3 * t + 2)
                    dve.tensor_scalar(mz, mz, -1.0 / L, -1.0 / L, ALU.mult, ALU.add).then_inc(S("at_z"), 1)
                    dve.wait_ge(S("at_v"), t + 1 + CREDIT)
                    dve.scalar_tensor_tensor(atmp[:, q % 2, :], pb[6 + q % 2][:, 0:D], rz,
                                             xn2[:, bass.ds(t, 1), :].squeeze(1), ALU.mult, ALU.add).then_inc(S("at_x"), 1)
                    dve.wait_ge(S("at_z"), 3 * t + 3)
                    dve.wait_ge(S("at_x"), t + 1)
                    dve.wait_ge(S("xsum_ready"), b + 1)
                    dve.scalar_tensor_tensor(s1[:, bass.ds(t, 1), :].squeeze(1), xsum[:, r, :], mz,
                                             atmp[:, q % 2, :], ALU.mult, ALU.add).then_inc(S("at_o"), 1)
                top(0)
                top(1)
                for q in range(TPB):
                    rest(q)
                    if q + 2 < TPB:
                        top(q + 2)
            with dve.Fori(0, NB // 2) as pair:
                attend(pair * 2, 0)
                attend(pair * 2 + 1, 1)

            def bn_apply(b, r):
                dve.tensor_scalar(xb[:, r, :], xT[:, seq(b)], bnc[:, 2:3], bnc[:, 3:4], ALU.mult,
                                  ALU.add).then_inc(S("xb_ready"), 1)

            def picks(b, q):
                t = b * TPB + q
                dve.wait_ge(S("sm_ready"), t + 2)
                dve.sem_inc(S("picks_at"), 1)
                for h in range(PH):
                    for s_ in range(2):
                        op = dve.max(tv[:, q % 2, h, s_, :], sim[:, q % 2, h, s_, :])
                op.then_inc(S("tk_v"), 1)
                dve.wait_ge(S("tk_v"), 2 * t + 1)
                dve.tensor_tensor(cand, tv[:, q % 2, :, 0, :].unsqueeze(3).to_broadcast([P, PH, PK, PK]),
                                  tv[:, q % 2, :, 1, :].unsqueeze(2).to_broadcast([P, PH, PK, PK]),
                                  ALU.add).then_inc(S("tk_v"), 1)
                dve.wait_ge(S("tk_v"), 2 * t + 2)
                dve.sem_inc(S("picks_at"), 1)
                for h in range(PH):
                    op = dve.max(t8[:, q % 2, h, :], cand[:, h].rearrange("p a b -> p (a b)"))
                op.then_inc(S("tk_done"), 1)

            def weigh_hidden(b, q, r):
                t = b * TPB + q
                dve.wait_ge(S("tc"), (t + 1) * PH + RING)
                dve.wait_ge(S("a_ready"), (b + 1) * EB + 2)
                dve.wait_ge(S("o2_mm"), t + 1)
                for k in range(2):
                    dve.tensor_tensor(Wt[:, q % 2, 4 * k:4 * k + 4, :],
                                      pb[4 + 2 * (q % 2) + k][:, :].rearrange("p (e n) -> p e n", e=4),
                                      AB[r][:, 4 * k:4 * k + 4, q * P:(q + 1) * P], ALU.mult).then_inc(S("wt_done"), 1)

            def tile(b, q, r, where):
                t = b * TPB + q
                if q == 1 and not final(b):
                    bn_apply(b + 1, 1 - r)
                dve.wait_ge(S("tk_done"), t + 1)
                for h in range(PH):
                    k = t * PH + (h + 1)
                    dve.wait_ge(S("sg_done"), k + RING)
                    dve.wait_ge(S("tc"), k)
                    dve.scalar_tensor_tensor(MK[:, h % RING, :], Z[:, h % RING, :], t8[:, q % 2, h, 7:8],
                                             SG[:, h % RING, :], ALU.is_ge, ALU.mult).then_inc(S("mk_done"), 1)
                    if h == 1 and where != "first":
                        weigh_hidden(*preceding(b, q, r))
                    if h == 3:
                        for hz in range(ZP, PH):
                            dve.wait_ge(S("mk_done"), t * PH + (hz + 1))
                            dve.tensor_tensor(Z[:, hz % RING].rearrange("p (i j) -> p i j", i=NK),
                                              sim[:, q % 2, hz, 0, :].unsqueeze(2).to_broadcast([P, NK, NK]),
                                              sim[:, q % 2, hz, 1, :].unsqueeze(1).to_broadcast([P, NK, NK]),
                                              ALU.add).then_inc(S("z_dve"), 1)
                        if where != "last":
                            picks(*following(b, q, r)[0:2])
                if where == "last":
                    weigh_hidden(b, q, r)
            bn_apply(0, 0)
            picks(0, 0)
            over_tiles(dve, tile)
            with dve.Fori(0, NB) as b:
                bt = bass.ds(b * TPB, TPB)
                dve.wait_ge(S("g2_ready"), b + 1)
                dve.tensor_tensor(s1[:, bt, :], s1[:, bt, :], o2[:, bt, :], ALU.mult).then_inc(S("y_mul"), 1)
                dve.wait_ge(S("y_mul"), b + 1)
                dve.tensor_tensor(acc[:, bt, :], acc[:, bt, :], s1[:, bt, :], ALU.add).then_inc(S("y_done"), 1)

        @block.sync
        def _(sp):
            for dst, src in ((con[:, :], a["con"]), (small[:, :], a["small"]),
                             (rows[:, 0:16], a["bf2"].partition_broadcast(P)),
                             (rows[:, 16:20], a["tau"].partition_broadcast(P)),
                             (rows[:, 20:28], a["gb"].partition_broadcast(P))):
                sp.dma_start(dst, src).then_inc(S("ld_const"), 16)
            sp.dma_start(x_in, a["x"].rearrange("(t p) d -> p t d", p=P)).then_inc(S("ld_x"), 16)
            for dst, src in ((wproj[:, 0, :], a["Wq"]), (wproj[:, 1, :], a["Wk"]), (wproj[:, 2, :], a["Wv"]),
                             (wb[:, :], a["Wb"]), (gatew[:, :], a["gw"]), (wo[:, :], a["Wo"]),
                             (wf1[:, :, :], a["Wf1"].rearrange("(k p) n -> p k n", p=P)),
                             (wf2[:, :, :], a["Wf2"].rearrange("(k p) n -> p k n", p=P)),
                             (b2[0:E, :], a["b2"]), (b2[E:NX, :], a["bs2"])):
                sp.dma_start(dst, src).then_inc(S("ld_w"), 16)
            sp.wait_ge(S("beta_done"), NB + CREDIT)
            sp.dma_start(beta_d, beta_sb.rearrange("h (n c) -> h n c", c=C)).then_inc(S("beta_out"), 16)
            sp.wait_ge(S("beta_out"), 16)
            sp.dma_start(beta_it[:, :, :], beta_d.rearrange("h n c -> n h c")).then_inc(S("beta_in"), 16)
            sp.wait_ge(S("nrm_done"), NB + CREDIT)
            for dst, src in ((w1[:, 0:E, :], a["w1"].rearrange("e p n -> p e n")), (w1[:, E, :], a["ws1"]),
                             (w2[:, 0:E], a["w2"].rearrange("e (m p) d -> p e m d", p=P)),
                             (w2[:, E], a["ws2"].rearrange("(m p) d -> p m d", p=P))):
                sp.dma_start(dst, src).then_inc(S("ld_e"), 16)
            with sp.Fori(0, NB // 2) as pair:
                b0 = pair * 2
                for r in range(2):
                    sp.wait_ge(S("gram_v"), (b0 + (r + 1)) * TPB + TPB)
                    sp.wait_ge(S("v_turned"), (b0 + (r + 1)) * TPB + TPB)
                    sp.dma_start(gram_d[bass.ds((b0 + r) * NCH, NCH)].rearrange("n h j i -> (h j) n i"),
                                 cst[:, r, :, 0, :]).then_inc(S(f"cst_out{r}"), 16)
                    sp.dma_start(lv_d[:, bass.ds((b0 + r) * NCH, NCH)], cst[:, r, :, 1:3, :]).then_inc(S(f"cst_out{r}"), 16)
            for r in range(2):
                sp.wait_ge(S(f"cst_out{r}"), 16 * NB + 32)
            sp.dma_start(att[:, :, :, :], gram_d).then_inc(S("ld_att"), 16)
            sp.wait_ge(S("inv_ready"), 1)
            sp.dma_start(inv_d, att[:, :, :, :]).then_inc(S("inv_out"), 16)
            sp.wait_ge(S("inv_out"), 16)
            sp.wait_ge(S("scan_zero"), 2)

            inv_n = inv_d.rearrange("(b n) h j i -> n h j b i", b=NB)
            lv_n = lv_d.rearrange("p (b n) s c -> p b n s c", b=NB)
            with sp.Fori(0, NCH) as n:
                sp.wait_ge(S("sc_u"), n + 1)
                for h in range(H):
                    sp.dma_start(Gb[h * C:(h + 1) * C, :, h * C:(h + 1) * C],
                                 inv_n[bass.ds(n, 1), h].squeeze(0)).then_inc(S("ld_g"), 16)
                sp.wait_ge(S("sc_o"), n + 1)
                sp.dma_start(lv, lv_n[:, :, bass.ds(n, 1)].squeeze(2)).then_inc(S("ld_lv"), 16)
            sp.wait_ge(S("sc_o"), NCH + 1)
            sp.wait_ge(S("yb_mm"), NB * (NX - EA) + CREDIT)
            with sp.Fori(0, NB) as b:
                sp.wait_ge(S("x1_done"), b + 1)
                sp.dma_start(xr, x_d[bass.ds(b, 1)].squeeze(0)).then_inc(S("ld_xr"), 16)
            sync_layer1(sp)

        @block.gpsimd
        def _(pool):
            pool.memset(pads[:, 0, :, 0:3], 0.0).then_inc(S("zeros"), 1)
            pool.memset(pads[:, 1, :, 0:3], 0.0).then_inc(S("zeros"), 1)
            pool.memset(vT[:, :, 0:PADV], 0.0).then_inc(S("zeros"), 1)
            pool.memset(comb[:, :, E:NX], 1.0).then_inc(S("zeros"), 1)
            pool.wait_ge(S("ld_const"), 80)
            with pool.Fori(0, NB) as b:
                for q in range(TPB):
                    pool.wait_ge(S("nrm_done"), b + 1 + CREDIT)
                    if q == 0:
                        pool.wait_ge(S("sq_free"), 1)
                    pool.wait_ge(S("gram_mm"), b * TPB + (q + 1))
                    pool.tensor_tensor(
                        KX[:, q % 2].rearrange("p n (h c) -> p n h c", h=H),
                        kq[:, bass.ds(b * NCH + q * 4, 4), 0, :].unsqueeze(2).to_broadcast([P, 4, H, C]),
                        blocks4.unsqueeze(1).to_broadcast([P, 4, H, C]), ALU.mult).then_inc(S("kx_ready"), 1)
            pool.wait_ge(S("ld_att"), 16)
            pool.wait_ge(S("beta_in"), 16)
            pool.tensor_tensor(att, att, beta_it[:, :, :].unsqueeze(2).to_broadcast([P, H, C, C]),
                               ALU.mult).then_inc(S("subst"), 1)
            for j in range(1, C - 1):
                n = C - 1 - j
                prod = RP[:, 0:H * j * n].rearrange("p (h k i) -> p h k i", h=H, k=j)
                pool.wait_ge(S("subst"), 2 * j - 1)
                pool.tensor_tensor(prod, att[:, :, j, j + 1:C].unsqueeze(2).to_broadcast([P, H, j, n]),
                                   att[:, :, 0:j, j].unsqueeze(3).to_broadcast([P, H, j, n]),
                                   ALU.mult).then_inc(S("subst"), 1)
                pool.wait_ge(S("subst"), 2 * j)
                pool.tensor_tensor(att[:, :, 0:j, j + 1:C], att[:, :, 0:j, j + 1:C], prod,
                                   ALU.add).then_inc(S("subst"), 1)
            pool.wait_ge(S("subst"), 2 * C - 3)
            diag = RA[:, :].rearrange("p (h x) -> p h x", h=H)[:, :, 0:C * C:C + 1]
            pool.tensor_scalar(diag, diag, 1.0, None, ALU.add).then_inc(S("subst"), 1)
            pool.wait_ge(S("subst"), 2 * C - 2)
            pool.tensor_tensor(att, att, beta_it[:, :, :].unsqueeze(3).to_broadcast([P, H, C, C]),
                               ALU.mult).then_inc(S("inv_ready"), 1)
            pool.wait_ge(S("gram_a"), NB + CREDIT)
            pool.wait_ge(S("inv_ready"), 1)
            pool.wait_ge(S("y_mm"), YA * NB + CREDIT)
            pool.memset(Gb, 0.0).then_inc(S("scan_zero"), 1)
            pool.memset(zero, 0.0).then_inc(S("scan_zero"), 1)
            with pool.Fori(0, NCH) as n:
                pool.wait_ge(S("sc_s"), n + 1)
                pool.tensor_tensor(
                    Kb.rearrange("p b (h c) -> p b h c", h=H),
                    kq5[:, :, bass.ds(n, 1), 0, :].to_broadcast([P, NB, H, C]),
                    blocks4.unsqueeze(1).to_broadcast([P, NB, H, C]), ALU.mult).then_inc(S("sc_k"), 1)
            def fuse_sum(b, r):
                pool.wait_ge(S("fz_mul"), 4 * (b + 1) + 1)
                pool.wait_ge(S("fz_n"), b + 1)
                pool.tensor_tensor(mC[:, 0], mC[:, 0], mC[:, 1], ALU.add).then_inc(S("fz_add"), 1)
                pool.tensor_tensor(mC[:, 2], mC[:, 2], mC[:, 3], ALU.add).then_inc(S("fz_add"), 1)
                pool.wait_ge(S("fz_add"), 3 * b + 2 + 3)
                pool.tensor_tensor(oT[:, r], mC[:, 0], mC[:, 2], ALU.add).then_inc(S("fz_add"), 1)
            with pool.Fori(0, NB // 2) as pair:
                b0 = pair * 2
                for r in range(2):
                    fuse_sum(b0 + r, r)
            pool_layer1(pool)

        @block.tensor
        def _(pe):
            for n in ("xn_turned", "nrm_mm", "gram_mm", "y_mm", "yb_mm", "fl_mm", "fp_mm"):
                pe.sem_inc(S(n), CREDIT)
            for n in ("sc_u", "sc_s", "sc_o", "gate_mm", "fz_ms", "cs_turned", "fz_wo"):
                pe.sem_inc(S(n), 1)
            pe.wait_ge(S("ld_const"), 80)
            with pe.Fori(0, NB // 2) as pair:
                b0 = pair * 2
                for r in range(2):
                    pe.wait_ge(S("xn_ready"), b0 + (r + 1))
                    pe.wait_ge(S("xT_ready"), b0 + (r + 1))
                    for q in range(TPB):
                        mm = pe.transpose(pb[r][:, q * P:(q + 1) * P], xst[:, r, q, :], ident)
                    mm.then_inc(S("xn_turned"), 1)
            pe.wait_ge(S("ld_w"), 160)
            with pe.Fori(0, NB // 2) as pair:
                b0 = pair * 2
                for r in range(2):
                    b = b0 + r
                    pe.wait_ge(S("xs_ready"), b + 1)
                    pe.wait_ge(S("beta_done"), b + 1)
                    pe.wait_ge(S("gl_done"), b + 1)
                    pe.matmul(pb[2 + r][0:H, :], wb[:, :], xs[:, r, :], start=True, stop=True)
                    for q in range(TPB):
                        mm = pe.matmul(pb[4 + r][:, q * E:(q + 1) * E], xs[:, r, q * P:(q + 1) * P], gatew[:, :],
                                       start=True, stop=True)
                    mm.then_inc(S("gate_mm"), 1)
            pe.wait_ge(S("beta_done"), NB + CREDIT)
            pe.wait_ge(S("gl_done"), NB + CREDIT)
            with pe.Fori(0, NB // 2) as pair:
                b0 = pair * 2
                for r in range(2):
                    pe.wait_ge(S("conv_evac"), b0 + (r + 1))
                    for k in range(3):
                        mm = pe.matmul(pb[2 + 3 * r + k][:, :], wproj[:, k, :], xT[:, seq(b0 + r)],
                                       start=True, stop=True)
                    mm.then_inc(S("conv_mm"), 1)
            pe.wait_ge(S("xT_ready"), NB + CREDIT)
            pe.wait_ge(S("conv_evac"), NB + CREDIT)
            with pe.Fori(0, NB // 2) as pair:
                b0 = pair * 2
                for r in range(2):
                    b = b0 + r
                    pe.wait_ge(S("nrm_sq"), b + 1)
                    pe.wait_ge(S("nrm_rt"), b + 1)
                    for k in range(2):
                        mm = pe.matmul(pb[2 * r + k][:, :], blocks, sq[:, r, k * L:(k + 1) * L], start=True, stop=True)
                    mm.then_inc(S("nrm_mm"), 1)
            with pe.Fori(0, NB) as b:
                for q in range(TPB):
                    g1 = b * TPB + (q + 1)
                    pe.wait_ge(S("kx_ready"), g1)
                    pe.wait_ge(S("gram_v"), g1)
                    bank = pb[4 + q][:, 0:8 * C].rearrange("p (n c) -> p n c", n=4)
                    for i in range(4):
                        mm = pe.matmul(bank[:, i, 0:2 * C], KX[:, q % 2, i, :],
                                  kq[:, bass.ds(b * NCH + (q * 4 + i), 1), :, :].rearrange("p n s c -> p (n s c)"),
                                  start=True, stop=True)
                    mm.then_inc(S("gram_mm"), 1)
            pe.wait_ge(S("ld_e"), 64)
            pe.wait_ge(S("gram_v"), NB * TPB + TPB)
            with pe.Fori(0, NB) as b:
                def hidden(e):
                    for m in range(MB):
                        pe.wait_ge(S("h_ready"), (b * EA + e) * MB + (m + 1))
                        pe.matmul(pb[m][:, :], w1[:, e, m * P:(m + 1) * P], xT[:, seq(b)],
                                  start=True, stop=True).then_inc(S("h_mm"), 1)

                hidden(0)
                for e in range(EA):
                    if e + 1 < EA:
                        hidden(e + 1)
                    pe.wait_ge(S("h_ready"), (b * EA + (e + 1)) * MB + MB)
                    pe.wait_ge(S("y_added"), 4 * (b * YA + (e + 1)))
                    for q in range(TPB):
                        for m in range(MB):
                            mm = pe.matmul(pb[4 + e % 2][:, q * P:(q + 1) * P], hT[:, e % 2, m, q * P:(q + 1) * P],
                                           w2[:, e, m, :], start=(m == 0), stop=(m == MB - 1))
                    mm.then_inc(S("y_mm"), 1)
                    if e == 3:
                        pe.wait_ge(S("cs_ready"), b + 1)
                        pe.wait_ge(S("ct_ready"), b + 1)
                        for q in range(TPB):
                            mm = pe.transpose(pb[6][0:NX, q * P:(q + 1) * P], cs[:, q, :], ident)
                        mm.then_inc(S("cs_turned"), 1)
                pe.wait_ge(S("ct_ready"), b + 2)
                pe.wait_ge(S("y_added"), 4 * (b * YA + YA))
                for q in range(TPB):
                    mm = pe.matmul(pb[5][:, q * P:(q + 1) * P], cT[:, q * P:(q + 1) * P], b2[:, :],
                                   start=True, stop=True)
                mm.then_inc(S("y_mm"), 1)
            pe.wait_ge(S("scan_zero"), 2)
            pe.wait_ge(S("y_added"), 4 * YA * NB + ACCC)
            pe.wait_ge(S("h_ready"), EA * NB * MB + MB)
            pe.wait_ge(S("ct_ready"), NB + 1)
            pe.matmul(pb[7][:, 0:NB * C], blocks, zero, start=True, stop=False, skip_group_check=True)

            def expert_hidden(v, b, e, ms):
                for m in ms:
                    pe.wait_ge(S("hb_ready"), v * MB + (m + 1))
                    pe.matmul(pb[m % 2][:, :], w1[:, e, m * P:(m + 1) * P], xT[:, seq(b)],
                              start=True, stop=True).then_inc(S("hb_mm"), 1)

            def expert_out(v, e, r, half):
                if half == 0:
                    pe.wait_ge(S("hb_ready"), v * MB + (MB + 2))
                    pe.wait_ge(S("yb_added"), v * TPB + TPB)
                for q in (2 * half, 2 * half + 1):
                    for m in range(MB):
                        mm = pe.matmul(pb[4 + r][:, q * P:(q + 1) * P], hT[:, r, m, q * P:(q + 1) * P],
                                       w2[:, e, m, :], start=(m == 0), stop=(m == MB - 1))
                if half == 1:
                    mm.then_inc(S("yb_mm"), 1)

            def step_w(n, half):
                if half == 0:
                    pe.wait_ge(S("sc_k"), n + 1)
                    pe.wait_ge(S("ld_g"), n * 64 + 64)
                    pe.wait_ge(S("sc_wn"), n + 1)
                for b in range(4 * half, 4 * half + 4):
                    mm = pe.matmul(pb[2 + half][:, (b % 4) * P:(b % 4 + 1) * P], Kb[:, b, :], Gb[:, b, :],
                                   start=True, stop=True)
                if half == 1:
                    mm.then_inc(S("sc_w"), 1)

            def step_u(n, half):
                if half == 0:
                    pe.wait_ge(S("sc_wn"), n + 2)
                    pe.wait_ge(S("ld_lv"), n * 16 + 16)
                    pe.wait_ge(S("sc_s4"), n + 1)
                    pe.wait_ge(S("sc_oe"), n + 1)
                for b in range(4 * half, 4 * half + 4):
                    o = pb[6][:, b * C:(b + 1) * C]
                    pe.matmul(o, Gb[:, b, :], lv[:, b, 1, :], start=True, stop=False)
                    mm = pe.matmul(o, Wn[:, b, :], S4[:, b, :], start=False, stop=True)
                if half == 1:
                    mm.then_inc(S("sc_u"), 1)

            def step_s(n):
                pe.wait_ge(S("sc_u4"), n + 1)
                for b in range(NB):
                    mm = pe.matmul(pb[7][:, b * C:(b + 1) * C], Kb[:, b, :], U4[:, b, :],
                                   start=False, stop=False, skip_group_check=True)
                mm.then_inc(S("sc_s"), 1)

            def step_o(n, half):
                if half == 0:
                    pe.wait_ge(S("sc_ub"), n + 2)
                    pe.wait_ge(S("sc_sb"), n + 1)
                for b in range(4 * half, 4 * half + 4):
                    o = pb[6][:, b * C:(b + 1) * C]
                    pe.matmul(o, Sb[:, b, :], kq5[:, b, bass.ds(n, 1), 1, :].rearrange("p n c -> p (n c)"),
                              start=True, stop=False)
                    mm = pe.matmul(o, Ub[:, b, :], lv[:, b, 0, :], start=False, stop=True)
                if half == 1:
                    mm.then_inc(S("sc_o"), 1)

            def step(n, v, i, e):
                expert_hidden(v, i * 2, e, (0, 1))
                step_w(n, 0)
                expert_hidden(v, i * 2, e, (2, 3))
                step_w(n, 1)
                expert_out(v, e, 0, 0)
                step_u(n, 0)
                expert_out(v, e, 0, 1)
                step_u(n, 1)
                expert_hidden(v + 1, i * 2 + 1, e, (0, 1))
                step_s(n)
                expert_hidden(v + 1, i * 2 + 1, e, (2, 3))
                step_o(n, 0)
                expert_out(v + 1, e, 1, 0)
                step_o(n, 1)
                expert_out(v + 1, e, 1, 1)
            over_steps(pe, step)
            pe.wait_ge(S("sc_oe"), NCH + 1)
            pe.wait_ge(S("yb_added"), TPB * NB * (NX - EA) + ACCC)
            pe.wait_ge(S("hb_ready"), MB * NB * (NX - EA) + 2)

            def fuse_hidden(b, r):
                pe.wait_ge(S("fh_ready"), 2 * b + 2)
                srcs = [xT[:, seq(b)], firs[:, bass.ds(b, 1), :].squeeze(1), firl[:, bass.ds(b, 1), :].squeeze(1),
                        dT[:, bass.ds(b, 1), :].squeeze(1)]
                for m in range(2):
                    for k in range(4):
                        mm = pe.matmul(pb[2 * r + m][:, :], wf1[:, k, m * P:(m + 1) * P], srcs[k],
                                       start=(k == 0), stop=(k == 3))
                    mm.then_inc(S("fh_mm"), 1)

            def fuse_logits(b, r):
                pe.wait_ge(S("fh_ready"), 2 * b + 2 + 4)
                pe.wait_ge(S("fl_done"), b + 1)
                for q in range(TPB):
                    for m in range(2):
                        mm = pe.matmul(pb[4 + r][:, q * 16:(q + 1) * 16], hidT[:, r, m, q * P:(q + 1) * P],
                                       wf2[:, m, :], start=(m == 0), stop=(m == 1))
                mm.then_inc(S("fl_mm"), 1)
            staggered(pe, fuse_hidden, fuse_logits)

            def path_weights(b, r):
                pe.wait_ge(S("fp_ready"), b + 1)
                pe.wait_ge(S("fz_mul"), 4 * b + 1)
                for c in range(4):
                    for q in range(TPB):
                        mm = pe.transpose(pb[c][:, q * P:(q + 1) * P], Pst[:, r, q, c, :], ident)
                mm.then_inc(S("fp_mm"), 1)

            def project(b, r):
                pe.wait_ge(S("fz_sq"), b + 1)
                pe.wait_ge(S("fz_rt"), b + 1)
                pe.matmul(pb[4][:, :], blocks, sqo, start=True, stop=True).then_inc(S("fz_ms"), 1)
                pe.wait_ge(S("fz_n"), b + 1 + CREDIT)
                pe.wait_ge(S("fz_sg"), b + 1)
                for q in range(TPB):
                    mm = pe.matmul(pb[5][:, q * P:(q + 1) * P], oN[:, q * P:(q + 1) * P], wo[:, :],
                                   start=True, stop=True)
                mm.then_inc(S("fz_wo"), 1)
            pe.wait_ge(S("fl_done"), NB + CREDIT)
            pe.wait_ge(S("fh_ready"), 2 * NB + 4)
            staggered(pe, path_weights, project)
            tensor_layer1(pe)

        @block.scalar
        def _(act):
            act.sem_inc(S("xT_ready"), CREDIT)
            act.sem_inc(S("beta_done"), CREDIT)
            act.sem_inc(S("conv_evac"), CREDIT)
            act.sem_inc(S("silu_done"), CREDIT)
            act.sem_inc(S("nrm_rt"), CREDIT)
            act.sem_inc(S("gram_a"), CREDIT)
            act.sem_inc(S("h_ready"), MB)
            act.sem_inc(S("ct_ready"), 1)
            act.sem_inc(S("sc_wn"), 1)
            act.sem_inc(S("sc_oe"), 1)
            act.sem_inc(S("hb_ready"), 2)
            act.sem_inc(S("fh_ready"), 4)
            act.sem_inc(S("fz_rt"), 1)
            act.wait_ge(S("ld_const"), 80)
            act.wait_ge(S("ln_var"), 1)
            act.activation(rstd[:, :], lntmp[:, 1, :], ACT.Sqrt, bias=eps5).then_inc(S("ln_std"), 1)
            with act.Fori(0, NB // 2) as pair:
                b0 = pair * 2
                for r in range(2):
                    act.wait_ge(S("xn_turned"), b0 + (r + 1 + CREDIT))
                    act.activation(xT[:, seq(b0 + r)], pb[r][:, :], ACT.Copy).then_inc(S("xT_ready"), 1)

            def gate_in(b, r):
                act.wait_ge(S("xT_ready"), b + 1 + CREDIT)
                act.wait_ge(S("gate_mm"), b + 1)
                act.activation(xs[:, r, :], xT[:, seq(b)], ACT.Copy).then_inc(S("xs_ready"), 1)

            def gate_beta(b, r):
                act.wait_ge(S("gate_mm"), b + 2)
                act.activation(beta_sb[:, seq(b)], pb[2 + r][0:H, :], ACT.Sigmoid).then_inc(S("beta_done"), 1)
            with act.Fori(0, NB // 2) as pair:
                b0 = pair * 2
                for r in range(2):
                    gate_in(b0 + r, r)
                    gate_beta(b0 + r, r)

            def conv_in(b, r):
                act.wait_ge(S("conv_mm"), b + 1)
                act.wait_ge(S("conv_tap"), 12 * (b + 1))
                for k in range(3):
                    op = act.activation(pads[:, r, k, 3:CW], pb[2 + 3 * r + k][:, :], ACT.Copy)
                op.then_inc(S("conv_evac"), 1)

            def conv_out(b, r):
                act.wait_ge(S("conv_tap"), 12 * (b + 1) + CONVC)
                items = bass.ds(b * NCH, NCH)
                v3 = [cacc[r][:, k, :].rearrange("p (n c) -> p n c", n=NCH) for k in range(2)]
                act.activation(kq[:, items, 1, :], v3[0], ACT.Silu)
                act.activation(kq[:, items, 0, :], v3[1], ACT.Silu)
                act.activation(vtok[:, bass.ds(b, 1), :].squeeze(1), cacc[r][:, 2, :],
                               ACT.Silu).then_inc(S("silu_done"), 1)
            act.wait_ge(S("zeros"), 4)
            staggered(act, conv_in, conv_out)

            def nrm_square(b, r):
                act.wait_ge(S("nrm_mm"), b + 1)
                act.activation(sq[:, r, :], RK[:, seq(b, 2 * L)], ACT.Square).then_inc(S("nrm_sq"), 1)

            def nrm_root(b, r):
                act.wait_ge(S("nrm_mm"), b + 1 + CREDIT)
                act.wait_ge(S("nrm_done"), b + 1)
                for k in range(2):
                    op = act.activation(rn[:, r, k * L:(k + 1) * L], pb[2 * r + k][:, :], ACT.Sqrt, bias=eps6)
                op.then_inc(S("nrm_rt"), 1)
            act.wait_ge(S("silu_done"), NB + CREDIT)
            staggered(act, nrm_square, nrm_root)
            act.wait_ge(S("nrm_mm"), NB + CREDIT)
            act.sem_inc(S("sq_free"), 1)
            def kv_copy(b, r):
                act.wait_ge(S("k_turned"), b + 1)
                act.activation(kv_in[:, r, 0], kq[:, bass.ds(b * NCH, NCH), 0, :], ACT.Copy)
                act.activation(kv_in[:, r, 1].rearrange("p n c -> p (n c)"), vtok[:, bass.ds(b, 1), :].squeeze(1),
                               ACT.Copy).then_inc(S("kv_in"), 1)

            def keys_back(b, r):
                act.wait_ge(S("gram_mm"), (b + 1) * TPB + CREDIT)
                act.wait_ge(S("k_turned"), b + 1 + CREDIT)
                act.sem_inc(S("keys_at"), 1)
                act.activation(kq[:, bass.ds(b * NCH, NCH), 0, :], kt[:, r], ACT.Copy).then_inc(S("gram_a"), 1)
            act.wait_ge(S("nrm_done"), NB + CREDIT)
            staggered(act, kv_copy, keys_back)
            act.wait_ge(S("topk"), 10)
            act.activation(tw[:, 2, :], tw[:, 2, :], ACT.Exp).then_inc(S("top_e"), 1)
            act.wait_ge(S("top_all"), 1)
            with act.Fori(0, NB) as b:
                for e in range(EA):
                    for m in range(MB):
                        act.wait_ge(S("h_mm"), (b * EA + e) * MB + (m + 1))
                        if m == 0:
                            act.wait_ge(S("y_mm"), b * YA + (e + 1 if e >= 2 else 1))
                        act.activation(hT[:, e % 2, m, :], pb[m][:, :], ACT.Gelu,
                                       bias=col("b1", e * MB + m)).then_inc(S("h_ready"), 1)
                    if e == EA - 1:
                        act.wait_ge(S("cs_turned"), b + 2)
                        act.wait_ge(S("y_mm"), b * YA + CREDIT)
                        act.activation(cT, pb[6][0:NX, :], ACT.Copy).then_inc(S("ct_ready"), 1)
            act.wait_ge(S("inv_out"), 16)
            act.wait_ge(S("y_mm"), YA * NB + CREDIT)

            def expert_hidden(v, e, r):
                act.wait_ge(S("yb_mm"), v + 1)
                for m in range(MB):
                    act.wait_ge(S("hb_mm"), v * MB + (m + 1))
                    act.activation(hT[:, r, m, :], pb[m % 2][:, :], ACT.Gelu,
                                   bias=col("b1", e * MB + m)).then_inc(S("hb_ready"), 1)

            def step(n, v, i, e):
                expert_hidden(v, e, 0)
                act.wait_ge(S("sc_w"), n + 1)
                act.wait_ge(S("sc_u"), n + 1)
                for k in range(2):
                    op = act.activation(Wn[:, 4 * k:4 * k + 4, :].rearrange("p b c -> p (b c)"), pb[2 + k][:, :],
                                        ACT.Copy, scale=-1.0)
                op.then_inc(S("sc_wn"), 1)
                act.wait_ge(S("sc_u"), n + 2)
                act.wait_ge(S("sc_s"), n + 1)
                act.wait_ge(S("sc_ub"), n + 1)
                act.activation(U4.rearrange("p b c -> p (b c)"), pb[6][:, 0:NB * C], ACT.Copy).then_inc(S("sc_u4"), 1)
                expert_hidden(v + 1, e, 1)
                act.wait_ge(S("sc_s"), n + 2)
                act.wait_ge(S("sc_sb"), n + 1)
                act.activation(S4.rearrange("p b c -> p (b c)"), pb[7][:, 0:NB * C], ACT.Copy).then_inc(S("sc_s4"), 1)
                act.wait_ge(S("sc_o"), n + 2)
                act.activation(dT[:, :, bass.ds(n * C, C)], pb[6][:, 0:NB * C].rearrange("p (b c) -> p b c", b=NB),
                               ACT.Copy).then_inc(S("sc_oe"), 1)
            over_steps(act, step)
            act.wait_ge(S("yb_added"), TPB * NB * (NX - EA) + ACCC)
            act.activation(acc[:, :, :], acc[:, :, :], ACT.Silu).then_inc(S("g_ready"), 1)
            act.wait_ge(S("yb_mm"), NB * (NX - EA) + CREDIT)
            act.wait_ge(S("sc_sb"), NCH + 1)
            with act.Fori(0, NB // 2) as pair:
                b0 = pair * 2
                for r in range(2):
                    b = b0 + r
                    for m in range(2):
                        act.wait_ge(S("fh_mm"), 2 * b + (m + 1))
                        if m == 0:
                            act.wait_ge(S("fl_mm"), b + 1)
                        act.activation(hidT[:, r, m, :], pb[2 * r + m][:, :], ACT.Gelu,
                                       bias=col("bf1", m)).then_inc(S("fh_ready"), 1)
            act.activation(itau, rows[:, 16:20], ACT.Exp, scale=-1.0).then_inc(S("itau"), 1)
            act.wait_ge(S("fg"), 3)
            act.activation(ft3(2), ft3(2), ACT.Exp).then_inc(S("fg_e"), 1)
            act.activation(ftx(1), lg[:, :, :, 3], ACT.Exp, scale=-1.0).then_inc(S("fg_e"), 1)
            act.wait_ge(S("pg_ready"), 2)

            def path_spread(b, r):
                act.wait_ge(S("fp_mm"), b + 1)
                act.activation(
                    Pst[:, r].rearrange("p q c (h d) -> p (q c h) d", h=H),
                    PG[:, bass.ds(b * TPB, TPB)].rearrange("p t c h -> p (t c h)").unsqueeze(2).to_broadcast([P, 64, DK]),
                    ACT.Copy).then_inc(S("fp_ready"), 1)

            def rms(b, r):
                act.wait_ge(S("fz_add"), 3 * (b + 1) + 3)
                act.wait_ge(S("fz_ms"), b + 1)
                act.activation(sqo, oT[:, r], ACT.Square).then_inc(S("fz_sq"), 1)
                act.wait_ge(S("fz_ms"), b + 2)
                act.wait_ge(S("fz_n"), b + 2)
                act.activation(rr, pb[4][:, :], ACT.Sqrt, scale=1.0 / DK, bias=eps5).then_inc(S("fz_rt"), 1)
            staggered(act, path_spread, rms)
            scalar_layer1(act)

        @block.vector
        def _(dve):
            dve.sem_inc(S("gl_done"), CREDIT)
            dve.sem_inc(S("conv_tap"), CONVC)
            dve.sem_inc(S("nrm_done"), CREDIT)
            dve.sem_inc(S("gram_v"), TPB)
            dve.sem_inc(S("v_turned"), TPB)
            dve.sem_inc(S("k_turned"), CREDIT)
            dve.sem_inc(S("cst_out0"), 32)
            dve.sem_inc(S("cst_out1"), 32)
            dve.sem_inc(S("y_added"), ACCC)
            dve.sem_inc(S("sc_ub"), 1)
            dve.sem_inc(S("yb_added"), ACCC)
            dve.sem_inc(S("fl_done"), CREDIT)
            dve.sem_inc(S("fz_n"), CREDIT)
            dve.sem_inc(S("fz_add"), 3)
            dve.sem_inc(S("fz_sg"), 1)
            dve.sem_inc(S("x1_done"), 1)
            dve.sem_inc(S("fz_mul"), 1)

            moments(dve, x_in, ("ln_v", "ln_var", "ln_std", "ln_done"), "ld_x")
            with dve.Fori(0, NB // 2) as pair:
                b0 = pair * 2
                for r in range(2):
                    dve.wait_ge(S("xn_turned"), b0 + (r + 1))
                    for q in range(TPB):
                        op = normed(dve, xst[:, r, q, :], x_in, (b0 + r) * TPB + q)
                    op.then_inc(S("xn_ready"), 1)
            gate_b = rows[:, 20:28]
            with dve.Fori(0, NB // 2) as pair:
                b0 = pair * 2
                for r in range(2):
                    dve.wait_ge(S("gate_mm"), b0 + (r + 2))
                    dve.tensor_tensor(gl[:, bass.ds((b0 + r) * TPB, TPB), :],
                                      pb[4 + r][:, 0:TPB * E].rearrange("p (q e) -> p q e", q=TPB),
                                      gate_b.unsqueeze(1).to_broadcast([P, TPB, E]), ALU.add).then_inc(S("gl_done"), 1)
            with dve.Fori(0, NB // 2) as pair:
                b0 = pair * 2
                for r in range(2):
                    b = b0 + r
                    dve.wait_ge(S("conv_evac"), b + 1 + CREDIT)
                    dve.wait_ge(S("silu_done"), b + 1)
                    for k in range(4):
                        for c3 in range(3):
                            tap, src, dst = col("cw", c3 * 4 + k), pads[:, r, c3, k:k + L], cacc[r][:, c3, :]
                            if k == 0:
                                op = dve.tensor_scalar(dst, src, tap, None, ALU.mult)
                            else:
                                dve.wait_ge(S("conv_tap"), 12 * b + (3 * (k - 1) + c3 + 1 + CONVC))
                                op = dve.scalar_tensor_tensor(dst, src, tap, dst, ALU.mult, ALU.add)
                            op.then_inc(S("conv_tap"), 1)
            with dve.Fori(0, NB // 2) as pair:
                b0 = pair * 2
                for r in range(2):
                    b = b0 + r
                    dve.wait_ge(S("nrm_rt"), b + 1 + CREDIT)
                    dve.reciprocal(rn[:, r, :], rn[:, r, :]).then_inc(S("nrm_rec"), 1)
                    dve.wait_ge(S("nrm_rec"), b + 1)
                    dve.tensor_tensor(RK[:, seq(b, 2 * L)], RK[:, seq(b, 2 * L)], rn[:, r, :],
                                      ALU.mult).then_inc(S("nrm_done"), 1)
            masks = con[:, O_GRAM:O_GRAM + 2 * C]

            def products(b, r):
                dve.wait_ge(S(f"cst_out{r}"), 16 * b + (32 - 16 * r))
                dve.wait_ge(S("kv_in"), b + 1)
                dve.transpose(cst[:, r, :, 2, :], kv_in[:, r, 1]).then_inc(S("v_turned"), TPB)
                dve.wait_ge(S("gram_a"), b + 1)
                dve.transpose(kt[:, r], kv_in[:, r, 0]).then_inc(S("k_turned"), 1)
                for q in range(TPB):
                    dve.wait_ge(S("gram_mm"), b * TPB + (q + 1 + CREDIT))
                    bank = pb[4 + q][:, 0:8 * C].rearrange("p (n c) -> p n c", n=4)
                    dve.tensor_tensor(cst[:, r, q * 4:q * 4 + 4, 0:2, :].rearrange("p n s c -> p n (s c)"),
                                      bank[:, :, 0:2 * C], masks.unsqueeze(1).to_broadcast([P, 4, 2 * C]),
                                      ALU.mult).then_inc(S("gram_v"), 1)
            with dve.Fori(0, NB // 2) as pair:
                b0 = pair * 2
                for r in range(2):
                    products(b0 + r, r)
            n_top = 0

            def t_inc(op):
                op.then_inc(S("topk"), 1)

            bc = [P, NT, E]
            io = iota_e.unsqueeze(1).to_broadcast(bc)
            t8 = [top[:, k, 0:NT * E].rearrange("p (t e) -> p t e", e=E) for k in range(4)]
            m1, m2, df, i1 = (tw[:, k, :] for k in range(4))
            dve.wait_ge(S("gl_done"), NB + CREDIT)

            def best(src, m, oh, k0):
                dve.tensor_reduce(m, src, AX.X, ALU.max).then_inc(S("topk"), 1)
                dve.wait_ge(S("topk"), k0 + 1)
                dve.tensor_tensor(oh, src, m.unsqueeze(2).to_broadcast(bc), ALU.is_equal).then_inc(S("topk"), 1)
                dve.wait_ge(S("topk"), k0 + 2)
                dve.tensor_tensor(oh, oh, io, ALU.mult).then_inc(S("topk"), 1)
                dve.wait_ge(S("topk"), k0 + 3)
                dve.tensor_reduce(i1, oh, AX.X, ALU.min).then_inc(S("topk"), 1)
                dve.wait_ge(S("topk"), k0 + 4)
                dve.tensor_tensor(oh, io, i1.unsqueeze(2).to_broadcast(bc), ALU.is_equal).then_inc(S("topk"), 1)
                dve.wait_ge(S("topk"), k0 + 5)
            dve.wait_ge(S("silu_done"), NB + CREDIT)
            best(gl[:, :, :], m1, t8[0], 0)
            dve.scalar_tensor_tensor(t8[1].rearrange("p t e -> p (t e)"), t8[0].rearrange("p t e -> p (t e)"), -3e38,
                                     gl[:, :, :].rearrange("p t e -> p (t e)"), ALU.mult, ALU.add).then_inc(S("top_x"), 1)
            dve.wait_ge(S("top_x"), 1)
            dve.tensor_reduce(m2, t8[1], AX.X, ALU.max).then_inc(S("topk"), 1)
            dve.wait_ge(S("topk"), 6)
            dve.tensor_tensor(df, m2, m1, ALU.subtract).then_inc(S("topk"), 1)
            dve.tensor_tensor(t8[2], t8[1], m2.unsqueeze(2).to_broadcast(bc), ALU.is_equal).then_inc(S("topk"), 1)
            dve.wait_ge(S("topk"), 8)
            dve.tensor_tensor(t8[2], t8[2], io, ALU.mult).then_inc(S("topk"), 1)
            dve.wait_ge(S("topk"), 9)
            dve.tensor_reduce(i1, t8[2], AX.X, ALU.min).then_inc(S("topk"), 1)
            dve.wait_ge(S("topk"), 10)
            dve.tensor_tensor(t8[2], io, i1.unsqueeze(2).to_broadcast(bc), ALU.is_equal).then_inc(S("topk"), 1)
            dve.wait_ge(S("top_e"), 1)
            dve.wait_ge(S("topk"), 11)
            dve.tensor_scalar(m1, df, 1.0, None, ALU.add).then_inc(S("topk"), 1)
            dve.wait_ge(S("topk"), 12)
            dve.reciprocal(m1, m1).then_inc(S("topk"), 1)
            dve.wait_ge(S("topk"), 13)
            dve.tensor_tensor(m2, df, m1, ALU.mult).then_inc(S("topk"), 1)
            dve.tensor_tensor(t8[0], t8[0], m1.unsqueeze(2).to_broadcast(bc), ALU.mult).then_inc(S("topk"), 1)
            dve.wait_ge(S("topk"), 15)
            dve.tensor_tensor(t8[2], t8[2], m2.unsqueeze(2).to_broadcast(bc), ALU.mult).then_inc(S("topk"), 1)
            dve.wait_ge(S("topk"), 16)
            dve.wait_ge(S("zeros"), 4)
            dve.tensor_tensor(comb[:, :, 0:E], t8[0], t8[2], ALU.add).then_inc(S("top_all"), 1)
            dve.wait_ge(S("top_all"), 1)
            for r in range(2):
                dve.wait_ge(S(f"cst_out{r}"), 16 * NB + 32)
            dve.wait_ge(S("beta_out"), 16)
            with dve.Fori(0, NB) as b:
                done = 0
                at = {}

                def filters(n):
                    nonlocal done
                    for _ in range(n):
                        if done == FA:
                            return
                        kind, k = FIRS[done]
                        dst = (firs if kind == "s" else firl)[:, bass.ds(b, 1), :].squeeze(1)
                        off = PADV - 2 + k if kind == "s" else k
                        src = vT[:, bass.ds(b, 1), off:off + L].squeeze(1)
                        tap = col("fs" if kind == "s" else "fl", k)
                        if k == 0:
                            op = dve.tensor_scalar(dst, src, tap, None, ALU.mult)
                        else:
                            dve.wait_ge(S("fir"), b * FA + (at[kind] + 1))
                            op = dve.scalar_tensor_tensor(dst, src, tap, dst, ALU.mult, ALU.add)
                        op.then_inc(S("fir"), 1)
                        at[kind] = done
                        done += 1
                dve.wait_ge(S("cs_turned"), b + 1)
                dve.tensor_copy(cs, comb[:, bass.ds(b * TPB, TPB), :]).then_inc(S("cs_ready"), 1)
                for e in range(EA):
                    dve.wait_ge(S("y_mm"), b * YA + (e + 1 + CREDIT))
                    for q in range(TPB):
                        y = pb[4 + e % 2][:, q * P:(q + 1) * P]
                        t = b * TPB + q
                        dst = acc[:, bass.ds(t, 1), :].squeeze(1)
                        weight = comb[:, bass.ds(t, 1), e:e + 1].squeeze(1)
                        if e == 0:
                            op = dve.tensor_scalar(dst, y, weight, None, ALU.mult)
                        else:
                            dve.wait_ge(S("y_added"), b * (TPB * YA) + (TPB * (e - 1) + q + 1 + ACCC))
                            op = dve.scalar_tensor_tensor(dst, y, weight, dst, ALU.mult, ALU.add)
                        op.then_inc(S("y_added"), 1)
                    filters(-(-FA // EA))
                dve.wait_ge(S("y_mm"), b * YA + (YA + CREDIT))
                dve.wait_ge(S("y_added"), b * (TPB * YA) + (TPB * EA + ACCC))
                dst = acc[:, bass.ds(b * TPB, TPB), :]
                dve.tensor_tensor(dst, dst, pb[5][:, :].rearrange("p (q d) -> p q d", q=TPB),
                                  ALU.add).then_inc(S("y_added"), 4)
                assert done == FA
            dve.wait_ge(S("y_mm"), YA * NB + CREDIT)
            dve.wait_ge(S("y_added"), 4 * YA * NB + ACCC)
            dve.wait_ge(S("inv_ready"), 1)
            dve.memset(S4, 0.0).then_inc(S("sc_s4"), 1)
            dve.memset(Sb, 0.0).then_inc(S("sc_sb"), 1)

            def spread(dst, src):
                return dve.tensor_tensor(dst.rearrange("p b (h c) -> p b h c", h=H),
                                         src.unsqueeze(2).to_broadcast([P, NB, H, C]),
                                         blocks4.unsqueeze(1).to_broadcast([P, NB, H, C]), ALU.mult)

            def add_expert(v, b, e, r):
                dve.wait_ge(S("yb_mm"), v + 1 + CREDIT)
                if e > EA:
                    dve.wait_ge(S("yb_added"), v * TPB - (TPB * (NB - 1) - ACCC))
                for q in range(TPB):
                    dst = acc[:, bass.ds(b * TPB + q, 1), :].squeeze(1)
                    dve.scalar_tensor_tensor(dst, pb[4 + r][:, q * P:(q + 1) * P], comb[:, bass.ds(b * TPB + q, 1), e:e + 1].squeeze(1),
                                             dst, ALU.mult, ALU.add).then_inc(S("yb_added"), 1)

            def add_taps(v, b, e):
                dst = firl[:, bass.ds(b, 1), :].squeeze(1)
                for j in range(FB):
                    if j > 0:
                        dve.wait_ge(S("firb"), v * FB + j)
                    elif e > EA:
                        dve.wait_ge(S("firb"), v * FB - FB * (NB - 1))
                    k = FIRS[FA + (e - EA) * FB + j][1]
                    dve.scalar_tensor_tensor(dst, vT[:, bass.ds(b, 1), k:k + L].squeeze(1), col("fl", k), dst,
                                             ALU.mult, ALU.add).then_inc(S("firb"), 1)

            def step(n, v, i, e):
                add_expert(v, i * 2, e, 0)
                dve.wait_ge(S("sc_u4"), n + 1)
                dve.wait_ge(S("sc_o"), n + 1)
                spread(Ub, U4).then_inc(S("sc_ub"), 1)
                add_taps(v, i * 2, e)
                add_expert(v + 1, i * 2 + 1, e, 1)
                dve.wait_ge(S("sc_s4"), n + 2)
                dve.wait_ge(S("sc_o"), n + 2)
                spread(Sb, S4).then_inc(S("sc_sb"), 1)
                add_taps(v + 1, i * 2 + 1, e)
            dve.wait_ge(S("fir"), FA * NB)
            over_steps(dve, step)
            with dve.Fori(0, NB // 2) as pair:
                b0 = pair * 2
                for r in range(2):
                    b = b0 + r
                    dve.wait_ge(S("fl_mm"), b + 1 + CREDIT)
                    dve.tensor_tensor(lg[:, bass.ds(b * TPB, TPB)].rearrange("p t h c -> p t (h c)"),
                                      pb[4 + r][:, 0:64].rearrange("p (q n) -> p q n", q=TPB),
                                      rows[:, 0:16].unsqueeze(1).to_broadcast([P, TPB, 16]),
                                      ALU.add).then_inc(S("fl_done"), 1)
            dve.wait_ge(S("fl_done"), NB + CREDIT)
            dve.wait_ge(S("itau"), 1)
            b3 = [P, NT, H, 3]
            dve.tensor_tensor(ft3(2), lg[:, :, :, 0:3],
                              itau.unsqueeze(1).unsqueeze(3).to_broadcast(b3), ALU.mult).then_inc(S("fg"), 1)
            dve.wait_ge(S("fg"), 1)
            dve.tensor_reduce(ftx(0), ft3(2), AX.X, ALU.max).then_inc(S("fg"), 1)
            dve.wait_ge(S("fg"), 2)
            dve.tensor_tensor(ft3(2), ft3(2), ftx(0).unsqueeze(3).to_broadcast(b3), ALU.subtract).then_inc(S("fg"), 1)
            dve.wait_ge(S("fg_e"), 2)
            dve.tensor_reduce(ftx(0), ft3(2), AX.X, ALU.add).then_inc(S("fg"), 1)
            dve.tensor_scalar(ftx(1), ftx(1), 1.0, None, ALU.add).then_inc(S("fg"), 1)
            dve.wait_ge(S("fg"), 5)
            dve.reciprocal(ftx(0), ftx(0)).then_inc(S("fg"), 1)
            dve.reciprocal(ftx(1), ftx(1)).then_inc(S("fg"), 1)
            dve.wait_ge(S("fg"), 7)
            dve.tensor_scalar(ftx(5), ftx(1), MAX_FLOOR - MIN_FLOOR, 1.0 - MAX_FLOOR, ALU.mult, ALU.add).then_inc(S("fg"), 1)
            dve.wait_ge(S("fg"), 8)
            pv = PG[:, :, 3, :]
            dve.tensor_tensor(pv, ftx(5), ftx(1), ALU.mult).then_inc(S("fg"), 1)
            dve.wait_ge(S("fg"), 9)
            dve.tensor_scalar(ftx(5), pv, -1.0, 1.0, ALU.mult, ALU.add).then_inc(S("fg"), 1)
            dve.wait_ge(S("fg"), 10)
            dve.tensor_tensor(ftx(5), ftx(5), ftx(0), ALU.mult).then_inc(S("pg_ready"), 1)
            dve.wait_ge(S("pg_ready"), 1)
            dve.tensor_tensor(PG[:, :, 0:3, :], ft3(2).rearrange("p t h c -> p t c h"),
                              ftx(5).unsqueeze(2).to_broadcast([P, NT, 3, H]), ALU.mult).then_inc(S("pg_ready"), 1)
            paths = [firs, firl, dT, vtok]

            def weigh(b, r):
                dve.wait_ge(S("fp_mm"), b + 1 + CREDIT)
                dve.wait_ge(S("fz_add"), 3 * (b + 1))
                for c in range(4):
                    dve.tensor_tensor(mC[:, c], pb[c][:, :], paths[c][:, bass.ds(b, 1), :].squeeze(1),
                                      ALU.mult).then_inc(S("fz_mul"), 1)

            def gated(b, r):
                dve.wait_ge(S("fz_rt"), b + 2)
                dve.reciprocal(rr, rr).then_inc(S("fz_rec"), 1)
                dve.wait_ge(S("fz_rec"), b + 1)
                dve.wait_ge(S("fz_wo"), b + 1)
                dve.scalar_tensor_tensor(oN, oT[:, r], col("nw"), rr, ALU.mult, ALU.mult).then_inc(S("fz_n"), 1)
                dve.wait_ge(S("fz_wo"), b + 2)
                dve.wait_ge(S("x1_done"), b + 1)
                ga = acc[:, bass.ds(b * TPB, TPB), :]
                dve.tensor_tensor(sgt, pb[5][:, :].rearrange("p (q d) -> p q d", q=TPB), ga,
                                  ALU.mult).then_inc(S("fz_sg"), 1)
                dve.wait_ge(S("fz_sg"), b + 2)
                dve.wait_ge(S("ld_xr"), (b + 1) * 16)
                dve.tensor_tensor(ga, sgt, xr, ALU.add).then_inc(S("x1_done"), 1)
            dve.wait_ge(S("g_ready"), 1)
            staggered(dve, weigh, gated)
            vector_layer1(dve)


def kernel(**inputs):
    import concourse.bacc as bacc
    from concourse.bass_utils import run_bass_kernel_spmd

    g = {k: np.asarray(v) for k, v in inputs.items()}
    A, F, A1, F1 = "L0_attn_", "L0_ffn_", "L1_attn_", "L1_ffn_"
    b1 = np.concatenate([g[F + "b1"], g[F + "bs1"][None]], 0)
    small = np.concatenate([
        g[A + "conv_w_q"], g[A + "conv_w_k"], g[A + "conv_w_v"],
        g[A + "fir_short_w"].reshape(P, 3), g[A + "fir_long_w"].reshape(P, 31),
        g[A + "b_fuse1"].reshape(2, P).T, np.tile(g[A + "norm_w"], H)[:, None],
        b1.reshape(NX * MB, P).T, g[A1 + "bq"][:, None], g[A1 + "bk"][:, None],
        g[F1 + "bn_gamma"][:, None], g[F1 + "bn_beta"][:, None]], 1)
    laid = {
        "x": g[A + "hidden_states"].reshape(TOK, D), "con": shape_constants(), "small": small,
        "bf2": g[A + "b_fuse2"], "tau": g[A + "others_log_tau"], "gb": g[F + "gate_b"],
        "Wq": g[A + "W_q"], "Wk": g[A + "W_k"], "Wv": g[A + "W_v"], "Wb": g[A + "W_b"], "gw": g[F + "gate_w"],
        "Wo": g[A + "W_o"], "Wf1": g[A + "W_fuse1"], "Wf2": g[A + "W_fuse2"],
        "b2": g[F + "b2"], "bs2": g[F + "bs2"][None], "w1": g[F + "w1"], "ws1": g[F + "ws1"],
        "w2": g[F + "w2"], "ws2": g[F + "ws2"],
        "aWq": g[A1 + "Wq"].T, "aWk": g[A1 + "Wk"].T,
        "wqk": g[F1 + "w_q"].reshape(2, PH, P, D).transpose(2, 0, 1, 3),
        "keys": g[F1 + "keys_p"].transpose(3, 2, 0, 1),
        "down": g[F1 + "down"][:NE].T, "up": g[F1 + "up"][:NE],
    }
    laid = {"in_" + k: np.ascontiguousarray(v) for k, v in laid.items()}
    nc = bacc.Bacc("TRN2", target_bir_lowering=False, num_devices=1)
    aps = {k[3:]: nc.dram_tensor(k, v.shape, F32, kind="ExternalInput").ap() for k, v in laid.items()}
    out = nc.dram_tensor("out", (TOK, D), F32, kind="ExternalOutput").ap()
    gated_two_layer_kernel(nc, aps, out)
    r = run_bass_kernel_spmd(nc, [laid], core_ids=[0])
    return r.results[0]["out"].reshape(NB, L, D)
```

```python
from contextlib import ExitStack

import numpy as np

import concourse.bass as bass
from concourse import mybir

F32 = mybir.dt.float32
ALU = mybir.AluOpType
ACT = mybir.ActivationFunctionType
AX = mybir.AxisListType

NB, L, D = 8, 512, 128
TOK = NB * L
P = 128
TPB = L // P
NT = TOK // P
H, DK = 4, 32
C = 32
NCH = L // C
ITEMS = NB * NCH
PADV = 30
VW = PADV + L
E, HID = 8, 512
NX = E + 1
MB = HID // P
E1 = 3
EA = 5
E2 = EA - E1
SPE = NB // 2
PH, NK, PK = 8, 32, 8
NE = NK * NK
EB = NE // P
EPS = 1e-5
MIN_FLOOR, MAX_FLOOR = 0.01, 0.1
CREDIT = 2


def shape_constants():
    p = np.arange(P)[:, None]
    c = np.arange(P)[None, :]
    i = np.arange(C)[None, :]
    parts = [
        p == c,
        p // C == c // C,
        np.ones((P, P)),
        -1.0 * (i > p % C),
        i >= p % C,
        np.broadcast_to(np.arange(E)[None, :] - E, (P, E)),
        np.full((P, 1), 1e-6), np.full((P, 1), EPS),
    ]
    return np.ascontiguousarray(np.concatenate([np.asarray(x, np.float32) for x in parts], 1))


O_ID, O_BLK, O_ONE, O_GRAM, O_LOC = 0, P, 2 * P, 3 * P, 3 * P + C
O_IOTA = O_LOC + C
O_E6, O_E5, NCONST = O_IOTA + E, O_IOTA + E + 1, O_IOTA + E + 2

SMALLS, SMALL = {}, 0
for _n, _w in (("cw", 12), ("fs", 3), ("fl", 31), ("bf1", 2), ("nw", 1), ("b1", NX * MB), ("bq", 1), ("bk", 1),
               ("gamma", 1), ("bbeta", 1)):
    SMALLS[_n] = (SMALL, _w)
    SMALL += _w


def gated_two_layer_kernel(nc, a, out):
    ctx = ExitStack()
    with ctx:
        def sb(name, shape):
            return ctx.enter_context(nc.sbuf_tensor(name, shape, F32))

        def sem(name):
            return ctx.enter_context(nc.semaphore(name))

        con = sb("con", [P, NCONST])
        small = sb("small", [P, SMALL])
        rows = sb("rows", [P, 16 + H + E])
        xT = sb("xT", [P, TOK])
        stats = sb("stats", [P, NT, 6])
        mean = sb("mean", [P, NT])
        rstd = sb("rstd", [P, NT])
        lntmp = sb("lntmp", [P, 3, NT])
        wproj = sb("wproj", [P, 3, D])
        wo = sb("wo", [P, D])
        wb = sb("wb", [P, H])
        wf1 = sb("wf1", [P, 4, 2 * D])
        wf2 = sb("wf2", [P, 2, 16])
        gatew = sb("gatew", [P, E])
        b2 = sb("b2", [NX, D])
        acc = sb("acc", [P, NT, D])
        bnc_t = sb("bnc", [P, 4])
        scal = sb("scal", [P, 4 * NT + TPB * NX + H])
        ctT = sb("ctT", [NX, L])
        RA = sb("RA", [P, NT * D])
        RK = sb("RK", [P, ITEMS * 2 * C])
        RV = sb("RV", [P, NB * VW])
        RF = sb("RF", [P, 2 * TOK])
        RW = sb("RW", [P, 2 * NX * HID])
        RH = sb("RH", [P, 2 * MB * L])
        RP = sb("RP", [P, H * 16 * 16])
        RT = sb("RT", [P, 2 * L])
        RS = sb("RS", [P, 3 * NB * C])
        beta_it = sb("beta_it", [P, H, C])
        gl = sb("gl", [P, NT, E])
        comb = sb("comb", [P, NT, NX])

        pb = [ctx.enter_context(nc.psum_tensor(f"bank{i}", [P, 512], F32)) for i in range(8)]

        ident = con[:, O_ID:O_ID + P]
        blocks = con[:, O_BLK:O_BLK + P]
        ones = con[:, O_ONE:O_ONE + P]
        iota_e = con[:, O_IOTA:O_IOTA + E]
        eps6 = con[:, O_E6:O_E6 + 1]
        eps5 = con[:, O_E5:O_E5 + 1]

        def col(name, n=None):
            o, w = SMALLS[name]
            return small[:, o:o + w] if n is None else small[:, o + n:o + n + 1]

        x_in = RA[:, :].rearrange("p (t d) -> p t d", d=D)
        att = RA[:, :].rearrange("p (h j i) -> p h j i", h=H, j=C)
        dT = RA[:, :].rearrange("p (b l) -> p b l", b=NB)
        kq = RK[:, :].rearrange("p (n s c) -> p n s c", s=2, c=C)
        vT = RV[:, :].rearrange("p (b l) -> p b l", b=NB)
        firs = RF[:, 0:TOK].rearrange("p (b l) -> p b l", b=NB)
        firl = RF[:, TOK:2 * TOK].rearrange("p (b l) -> p b l", b=NB)
        w1 = RW[:, 0:NX * HID].rearrange("p (e n) -> p e n", e=NX)
        w2 = RW[:, NX * HID:].rearrange("p (e m d) -> p e m d", e=NX, m=MB)
        hT = RH[:, :].rearrange("p (r m l) -> p r m l", r=2, m=MB)

        beta_d = nc.dram_tensor("beta_d", (H, ITEMS, C), F32, kind="Internal").ap()
        gram_d = nc.dram_tensor("gram_d", (ITEMS, H, C, C), F32, kind="Internal").ap()
        inv_d = nc.dram_tensor("inv_d", (ITEMS, H, C, C), F32, kind="Internal").ap()
        lv_d = nc.dram_tensor("lv_d", (P, ITEMS, 2, C), F32, kind="Internal").ap()

        s = {}

        def S(name):
            if name not in s:
                s[name] = sem(name)
            return s[name]

        block = ctx.enter_context(nc.Block())
        x_d = a["x"].rearrange("(b q p) d -> b p q d", p=P, q=TPB)
        out_d = out.rearrange("(b q p) d -> b p q d", p=P, q=TPB)

        def seq(b, n=L):
            return bass.ds(b * n, n)

        def staggered(eng, lead, follow):
            lead(0, 0)
            with eng.Fori(0, (NB - 2) // 2) as pair:
                b = pair * 2
                for r in range(2):
                    lead(b + (r + 1), 1 - r)
                    follow(b + r, r)
            lead(NB - 1, 1)
            follow(NB - 2, 0)
            follow(NB - 1, 1)

        xst = RH[:, 0:2 * L].rearrange("p (r q d) -> p r q d", r=2, q=TPB)
        xs = RH[:, 2 * L:4 * L].rearrange("p (r l) -> p r l", r=2)
        top = RT[:, :].rearrange("p (n x) -> p n x", n=4)
        beta_sb = acc[0:H, :, :].rearrange("p t d -> p (t d)")
        CW = 3 + L
        pads = RF[:, 0:6 * CW].rearrange("p (r s l) -> p r s l", r=2, s=3)
        cacc = RF[:, 6 * CW:6 * CW + 6 * L].rearrange("p (r s l) -> p r s l", r=2, s=3)
        rn = RW[:, EA * HID:EA * HID + 4 * L].rearrange("p (r l) -> p r l", r=2)
        sq = RW[:, (NX + EA) * HID:(NX + EA) * HID + 4 * L].rearrange("p (r l) -> p r l", r=2)
        KX = RP[:, 0:2 * L].rearrange("p (r n c) -> p r n c", r=2, n=4)
        kv_in = [x.rearrange("p (s n c) -> p s n c", s=2, n=NCH)
                 for x in (RA[:, 6 * L:8 * L], RF[:, 6 * CW + 6 * L:6 * CW + 8 * L])]
        kt = RT[:, :].rearrange("p (r n c) -> p r n c", r=2, n=NCH)
        cst = RA[:, 0:2 * NCH * 3 * C].rearrange("p (r n s c) -> p r n s c", r=2, n=NCH, s=3)
        blocks4 = blocks.rearrange("p (h c) -> p h c", h=H)
        vtok = vT[:, :, PADV:VW]
        tw = scal[:, 0:4 * NT].rearrange("p (n t) -> p n t", n=4)
        cs = scal[:, 4 * NT:4 * NT + TPB * NX].rearrange("p (q e) -> p q e", q=TPB)
        itau = scal[:, 4 * NT + TPB * NX:4 * NT + TPB * NX + H]
        cT = ctT[:, :]
        SW = NB * P
        assert E1 == 3 and SW + 2 * NB * C <= E1 * HID and 2 * SW <= EA * HID
        Kb = RW[:, 0:SW].rearrange("p (b c) -> p b c", b=NB)
        Gb = RT[:, :].rearrange("p (b c) -> p b c", b=NB)
        lv = RW[:, SW:SW + 2 * NB * C].rearrange("p (b s c) -> p b s c", b=NB, s=2)
        Wn = RW[:, NX * HID:NX * HID + SW].rearrange("p (b c) -> p b c", b=NB)
        Ub = RW[:, NX * HID + SW:NX * HID + 2 * SW].rearrange("p (b c) -> p b c", b=NB)
        Sb = RP[:, 0:SW].rearrange("p (b c) -> p b c", b=NB)
        U4 = RS[:, 0:NB * C].rearrange("p (b c) -> p b c", b=NB)
        S4 = RS[:, NB * C:2 * NB * C].rearrange("p (b c) -> p b c", b=NB)
        kq5 = RK[:, :].rearrange("p (b n s c) -> p b n s c", b=NB, n=NCH, s=2)
        zero = RS[:, 2 * NB * C:]
        hidT = RH[:, 0:4 * L].rearrange("p (r m l) -> p r m l", r=2, m=2)
        lg = RH[:, 4 * L:5 * L].rearrange("p (t h c) -> p t h c", t=NT, h=H)
        PG = RH[:, 5 * L:6 * L].rearrange("p (t c h) -> p t c h", t=NT, c=4)
        TH = TPB * H
        others = RH[:, 6 * L:6 * L + 3 * TH].rearrange("p (t h c) -> p t h c", h=H, c=3)
        osum, pval, pscale = (RH[:, 6 * L + k * TH:6 * L + (k + 1) * TH].rearrange("p (t h) -> p t h", h=H)
                              for k in (3, 4, 5))
        FG = 11
        Pst = RW[:, 0:8 * L].rearrange("p (r q c d) -> p r q c d", r=2, q=TPB, c=4)
        mC = RW[:, 8 * L:12 * L].rearrange("p (c l) -> p c l", c=4)
        oT = RW[:, 12 * L:14 * L].rearrange("p (r l) -> p r l", r=2)
        sqo = RW[:, 14 * L:15 * L]
        rr = RW[:, 15 * L:16 * L]
        oN = RW[:, 16 * L:17 * L]
        xr = RW[:, 17 * L:18 * L].rearrange("p (q d) -> p q d", q=TPB)
        sgt = RP[:, 0:L].rearrange("p (q d) -> p q d", q=TPB)

        CONVC = 2 * 12
        ACCC = 2 * TPB
        FIRS = [("s", 0), ("l", 0), ("s", 1), ("l", 1), ("s", 2)] + [("l", k) for k in range(2, 31)]
        FB = 7
        FA = len(FIRS) - FB * (NX - EA)

        def over_stages(eng, body):
            body(0, 0, True, False, False, True)
            body(1, 1, True, True, False, True)
            with eng.Fori(1, NB // 2) as pair:
                for r in range(2):
                    body(pair * 2 + r, r, True, True, True, True)
            body(NB, 0, False, True, True, False)
            body(NB + 1, 1, False, False, True, False)

        def over_steps(eng, step):
            for e in range(EA, NX):
                with eng.Fori(0, SPE) as i:
                    n = i + (e - EA) * SPE
                    step(n, 2 * n, i, e)

        def moments(dve, x, sems, loaded):
            v, var, std, done = sems
            parts = len(loaded)
            for k in range(parts):
                dve.wait_ge(S(loaded[k]), 16)
                with dve.Fori(k * NB // parts, (k + 1) * NB // parts) as b:
                    for q in range(TPB):
                        op = dve.bn_stats(stats[:, bass.ds(b * TPB + q, 1), :].squeeze(1),
                                          x[:, bass.ds(b * TPB + q, 1), :].squeeze(1))
                    op.then_inc(S(v), 1)
            dve.wait_ge(S(v), NB)
            me, mo, se, so = (stats[:, :, k] for k in (1, 4, 2, 5))
            t0, t1, t2 = (lntmp[:, k, :] for k in range(3))
            dve.tensor_tensor(t0, me, mo, ALU.add).then_inc(S(v), 1)
            dve.tensor_tensor(t1, me, mo, ALU.subtract).then_inc(S(v), 1)
            dve.tensor_tensor(t2, se, so, ALU.add).then_inc(S(v), 1)
            dve.wait_ge(S(v), NB + 3)
            dve.tensor_scalar(mean[:, :], t0, 0.5, None, ALU.mult).then_inc(S(v), 1)
            dve.scalar_tensor_tensor(t1, t1, 0.25, t1, ALU.mult, ALU.mult).then_inc(S(v), 1)
            dve.wait_ge(S(v), NB + 5)
            dve.scalar_tensor_tensor(t1, t2, 1.0 / D, t1, ALU.mult, ALU.add).then_inc(S(var), 1)
            dve.wait_ge(S(std), 1)
            dve.reciprocal(rstd[:, :], rstd[:, :]).then_inc(S(done), 1)
            dve.wait_ge(S(done), 1)

        def normed(dve, dst, x, t):
            return dve.tensor_scalar(dst, x[:, bass.ds(t, 1), :].squeeze(1), mean[:, bass.ds(t, 1)],
                                     rstd[:, bass.ds(t, 1)], ALU.subtract, ALU.mult)


        xn2 = RA[:, :].rearrange("p (t d) -> p t d", d=D)
        s1 = RF[:, 0:TOK].rearrange("p (t d) -> p t d", d=D)
        o2 = RF[:, TOK:2 * TOK].rearrange("p (t d) -> p t d", d=D)
        wqk = RK[:, 0:2048].rearrange("p (n d) -> p n d", n=2 * PH)
        Wt = RK[:, 0:2048].rearrange("p (r e n) -> p r e n", r=2, e=EB)
        keys = RK[:, 2048:2560].rearrange("p (n k) -> p n k", n=2 * PH)
        down = RK[:, 2560:3584]
        up = RK[:, 3584:4608].rearrange("p (e d) -> p e d", e=EB)
        aWq = RK[:, 4608:4736]
        aWk = RK[:, 4736:4864]
        WK = RK[:, 5120:5632]
        xb = RK[:, 6144:7168].rearrange("p (r l) -> p r l", r=2)
        qk = RW[:, 0:2048].rearrange("p (r s l) -> p r s l", r=2, s=2)
        Pr = RW[:, 2048:3072].rearrange("p (r l) -> p r l", r=2)
        PT = RW[:, 3072:4096].rearrange("p (r n s) -> p r n s", r=2, n=TPB)
        xsum = RW[:, 5120:6144].rearrange("p (b d) -> p b d", b=NB)
        atmp = RW[:, 4352:4608].rearrange("p (r d) -> p r d", r=2)
        ac = RW[:, 4608:4640].rearrange("p (r n) -> p r n", r=TPB)
        bqs = lntmp[:, 0, 0:1]
        bnst = lntmp[:, 1:3, :].rearrange("p a b -> p (a b)")[:, 0:6 * NB]
        bnc = bnc_t[:, :]
        RING = 4
        Z = RW[:, 0:PH * NE].rearrange("p (k e) -> p k e", k=PH)
        SG = RV[:, 0:RING * NE].rearrange("p (k e) -> p k e", k=RING)
        sim = RW[:, 8192:9216].rearrange("p (r h s k) -> p r h s k", r=2, h=PH, s=2)
        cand = RP[:, 0:512].rearrange("p (h a b) -> p h a b", h=PH, a=PK)
        tv = RP[:, 512:768].rearrange("p (r h s k) -> p r h s k", r=2, h=PH, s=2)
        t8 = RP[:, 768:896].rearrange("p (r h k) -> p r h k", r=2, h=PH)
        AB = [RH[:, :].rearrange("p (e l) -> p e l", e=EB), RA[:, :].rearrange("p (e l) -> p e l", e=EB)]
        SCALE = float(D) ** -0.5

        def following(b, q, r):
            return (b, q + 1, r) if q + 1 < TPB else (b + 1, 0, 1 - r)

        def preceding(b, q, r):
            return (b, q - 1, r) if q > 0 else (b - 1, TPB - 1, 1 - r)

        def exists(b, q, ahead):
            return not isinstance(b, int) or b * TPB + q + ahead < NT

        def over_tiles(eng, tile):
            tile(0, 0, 0, "first")
            with eng.Fori(0, NB // 2 - 1) as pair:
                for r in range(2):
                    b = pair * 2 + r
                    for q in range(1, TPB):
                        tile(b, q, r, "")
                    tile(b + 1, 0, 1 - r, "")
            for b in (NB - 2, NB - 1):
                for q in range(1, TPB):
                    tile(b, q, b % 2, "last" if (b, q) == (NB - 1, TPB - 1) else "")
                if b == NB - 2:
                    tile(b + 1, 0, 1 - b % 2, "")

        def final(b):
            return isinstance(b, int) and b == NB - 1

        def sync_layer1(sp):
            with sp.Fori(0, NB) as b:
                sp.wait_ge(S("y_done"), b + 1)
                sp.dma_start(out_d[bass.ds(b, 1)].squeeze(0), acc[:, bass.ds(b * TPB, TPB), :]).then_inc(S("out_done"), 16)
            sp.wait_ge(S("out_done"), 16 * NB)

        def pool_layer1(pool):
            pool.sem_inc(S("z_pool"), 1)

            def tile(b, q, r, last):
                t = b * TPB + q
                pool.wait_ge(S("sm_ready"), t + 2)
                for h in range(PH):
                    pool.wait_ge(S("tc"), t * PH + (h + 1))
                    pool.tensor_tensor(Z[:, h].rearrange("p (i j) -> p i j", i=NK),
                                       sim[:, q % 2, h, 0, :].unsqueeze(2).to_broadcast([P, NK, NK]),
                                       sim[:, q % 2, h, 1, :].unsqueeze(1).to_broadcast([P, NK, NK]),
                                       ALU.add).then_inc(S("z_pool"), 1)
            with pool.Fori(0, NB) as b:
                for q in range(TPB):
                    tile(b, q, 0, False)
            with pool.Fori(0, NB) as b:
                bt = bass.ds(b * TPB, TPB)
                pool.wait_ge(S("y_mul"), b + 1)
                pool.tensor_tensor(acc[:, bt, :], acc[:, bt, :], s1[:, bt, :], ALU.add).then_inc(S("y_done"), 1)

        def tensor_layer1(pe):
            pe.sem_inc(S("at_s"), CREDIT)
            pe.sem_inc(S("at_t"), CREDIT)
            pe.sem_inc(S("at_v"), CREDIT)
            pe.sem_inc(S("tc"), PH)
            pe.sem_inc(S("pr_mm"), CREDIT)
            pe.sem_inc(S("o2_mm"), CREDIT)
            pe.wait_ge(S("ld2"), 96)
            pe.wait_ge(S("x1_done"), NB + 1)
            for n in range(2 * PH):
                s_, h = n // PH, n % PH
                mm = pe.matmul(pb[7][:, (2 * h + s_) * NK:(2 * h + s_ + 1) * NK], wqk[:, n, :], keys[:, n, :],
                               start=True, stop=True)
            mm.then_inc(S("wk_mm"), 1)
            with pe.Fori(0, NB // 2) as pair:
                for r in range(2):
                    pe.wait_ge(S("x2_ready"), pair * 2 + (r + 1))
                    pe.wait_ge(S("x2_copied"), pair * 2 + (r + 1))
                    for q in range(TPB):
                        mm = pe.transpose(pb[r][:, q * P:(q + 1) * P], xst[:, r, q, :], ident)
                    for q in range(TPB):
                        mm = pe.matmul(pb[2 + r][:, 0:D], ones, xst[:, r, q, :], start=(q == 0), stop=(q == TPB - 1))
                    mm.then_inc(S("x2_turned"), 1)
            pe.wait_ge(S("x2_copied"), NB + CREDIT)

            def project(b):
                pe.wait_ge(S("qk_ready"), 2 * b + 1)
                for k, wgt in enumerate((aWq, aWk)):
                    mm = pe.matmul(pb[k][:, :], wgt, xT[:, seq(b)], start=True, stop=True)
                mm.then_inc(S("pr_mm"), 1)

            def scores(b, q, r):
                if q == 0:
                    pe.wait_ge(S("qk_ready"), 2 * b + 3)
                pe.wait_ge(S("at_p"), b * TPB + (q + 1))
                pe.matmul(pb[2 + q % 2][:, :], qk[:, r, 0, q * P:(q + 1) * P], qk[:, r, 1, :],
                          start=True, stop=True).then_inc(S("at_s"), 1)

            def turn(b, q):
                pe.wait_ge(S("at_p"), b * TPB + (q + 1 + CREDIT))
                pe.wait_ge(S("at_c"), b * TPB + (q + 1))
                for n in range(TPB):
                    mm = pe.transpose(pb[4 + q % 2][:, n * P:(n + 1) * P], Pr[:, q % 2, n * P:(n + 1) * P], ident)
                mm.then_inc(S("at_t"), 1)

            def values(b, q):
                pe.wait_ge(S("at_c"), b * TPB + (q + 1 + CREDIT))
                pe.wait_ge(S("at_o"), b * TPB + (q + 1))
                for n in range(TPB):
                    mm = pe.matmul(pb[6 + q % 2][:, 0:D], PT[:, q % 2, n, :],
                                   xn2[:, bass.ds(b * TPB + n, 1), :].squeeze(1),
                                   start=(n == 0), stop=(n == TPB - 1))
                mm.then_inc(S("at_v"), 1)

            def tile(b, q, r, where):
                turn(b, q)
                if exists(b, q, 2):
                    scores(*following(*following(b, q, r)))
                if q == 0 and not final(b):
                    project(b + 1)
                if where != "first":
                    values(*preceding(b, q, r)[0:2])
            project(0)
            scores(0, 0, 0)
            scores(0, 1, 0)
            over_tiles(pe, tile)
            values(NB - 1, TPB - 1)

            pe.wait_ge(S("at_o"), NT + CREDIT)

            def scores_of(b, q, r):
                t = b * TPB + q
                pe.wait_ge(S("xb_ready"), b + 1)
                pe.wait_ge(S("sm_ready"), t + 1)
                pe.matmul(pb[0][:, :], xb[:, r, q * P:(q + 1) * P], WK, start=True, stop=True).then_inc(S("sm_mm"), 1)

            def hidden_of(b, es):
                for e in es:
                    pe.wait_ge(S("a_ready"), b * EB + (e + 1))
                    pe.matmul(pb[2 + e % 2][:, :], down[:, e * P:(e + 1) * P], xT[:, seq(b)],
                              start=True, stop=True).then_inc(S("a_mm"), 1)

            def output_of(b, q, r):
                t = b * TPB + q
                pe.wait_ge(S("wt_done"), 2 * t + 3)
                pe.wait_ge(S("o2_done"), t + 1)
                for e in range(EB):
                    mm = pe.matmul(pb[1][:, 0:D], Wt[:, q % 2, e, :], up[:, e, :],
                                   start=(e == 0), stop=(e == EB - 1))
                mm.then_inc(S("o2_mm"), 1)

            def tile(b, q, r, where):
                t = b * TPB + q
                if where != "last":
                    scores_of(*following(b, q, r))
                for h in range(PH):
                    pe.wait_ge(S("mk_done"), t * PH + (h + 1 + RING))
                    if h == 0 and where != "first":
                        pe.wait_ge(S("wt_done"), 2 * t - 1)
                    for e in range(EB):
                        mm = pe.matmul(pb[4 + 2 * (q % 2) + e // 4][:, (e % 4) * P:(e % 4 + 1) * P],
                                       Z[:, h, e * P:(e + 1) * P],
                                       ident, start=(h == 0 and e % 4 == 0), stop=(h == PH - 1 and e % 4 == 3),
                                       is_transpose=True, skip_group_check=True)
                    mm.then_inc(S("tc"), 1)
                    if h == 2 and where != "first":
                        output_of(*preceding(b, q, r))
                    if h == 1 and not final(b):
                        hidden_of(b + 1, (2 * q, 2 * q + 1))
                if where == "last":
                    output_of(b, q, r)
            scores_of(0, 0, 0)
            hidden_of(0, range(EB))
            over_tiles(pe, tile)

        def scalar_layer1(act):
            act.sem_inc(S("x2_copied"), CREDIT)
            act.sem_inc(S("at_p"), CREDIT)
            act.sem_inc(S("qk_ready"), 1)
            act.sem_inc(S("sm_ready"), 1)
            act.sem_inc(S("at_c"), CREDIT)
            act.sem_inc(S("a_ready"), 2)
            act.sem_inc(S("o2_done"), 1)
            act.sem_inc(S("sg_done"), RING)
            act.wait_ge(S("sc_o"), NCH + 1)
            for dst, src in ((wqk, a["wqk"].rearrange("p s h d -> p (s h) d")),
                             (keys, a["keys"].rearrange("p s h k -> p (s h) k")),
                             (down, a["down"]), (up, a["up"].rearrange("(e p) d -> p e d", p=P)),
                             (aWq, a["aWq"]), (aWk, a["aWk"])):
                act.dma_start(dst, src).then_inc(S("ld2"), 16)
            act.wait_ge(S("ln2_var"), 1)
            act.activation(rstd[:, :], lntmp[:, 1, :], ACT.Sqrt, bias=eps5).then_inc(S("ln2_std"), 1)
            act.wait_ge(S("wk_mm"), 1)
            act.activation(WK, pb[7][:, :], ACT.Copy).then_inc(S("wk_ready"), 1)
            with act.Fori(0, NB // 2) as pair:
                for r in range(2):
                    b = pair * 2 + r
                    act.wait_ge(S("x2_turned"), b + 1)
                    act.activation(xT[:, seq(b)], pb[r][:, :], ACT.Copy)
                    act.activation(xsum[:, bass.ds(b, 1), :].squeeze(1), pb[2 + r][:, 0:D], ACT.Copy)
                    act.activation(xn2[:, bass.ds(b * TPB, TPB), :], xst[:, r], ACT.Copy).then_inc(S("x2_copied"), 1)
            act.wait_ge(S("bn_var"), 1)
            act.activation(bnc[:, 2:3], bnc[:, 1:2], ACT.Sqrt, bias=eps5).then_inc(S("bn_std"), 1)
            act.wait_ge(S("bq_ready"), 1)

            def projected(b, r):
                act.wait_ge(S("pr_mm"), b + 1 + CREDIT)
                act.activation(qk[:, r, 0, :], pb[0][:, :], ACT.Identity, scale=SCALE, bias=bqs).then_inc(S("qk_ready"), 1)
                act.activation(qk[:, r, 1, :], pb[1][:, :], ACT.Identity, bias=col("bk")).then_inc(S("qk_ready"), 1)

            def soft(b, q):
                t = b * TPB + q
                act.wait_ge(S("at_m"), t + 1)
                act.wait_ge(S("at_t"), t + 1)
                act.activation(Pr[:, q % 2, :], pb[2 + q % 2][:, :], ACT.Exp, bias=ac[:, q, 0:1],
                               accum_out=ac[:, q, 1:2]).then_inc(S("at_p"), 1)

            def turned(b, q):
                t = b * TPB + q
                act.wait_ge(S("at_t"), t + 1 + CREDIT)
                act.wait_ge(S("at_v"), t + 1)
                act.activation(PT[:, q % 2].rearrange("p n s -> p (n s)"), pb[4 + q % 2][:, :],
                               ACT.Copy).then_inc(S("at_c"), 1)

            def tile(b, q, r, where):
                soft(b, q)
                if where != "first":
                    turned(*preceding(b, q, r)[0:2])
                if q == 0 and not final(b):
                    act.wait_ge(S("at_t"), b * TPB + CREDIT)
                    projected(b + 1, 1 - r)
            projected(0, 0)
            over_tiles(act, tile)
            turned(NB - 1, TPB - 1)

            act.wait_ge(S("at_o"), NT + CREDIT)

            def scores_in(b, q, r):
                t = b * TPB + q
                if not (isinstance(b, int) and t < 2):
                    act.wait_ge(S("z_pool"), t * PH - (PH - 1))
                act.wait_ge(S("sm_mm"), t + 1)
                act.activation(sim[:, q % 2].rearrange("p h s k -> p (h s k)"), pb[0][:, :],
                               ACT.Copy).then_inc(S("sm_ready"), 1)

            def hidden_in(b, r, es):
                for e in es:
                    act.wait_ge(S("a_mm"), b * EB + (e + 1))
                    act.activation(AB[r][:, e, :], pb[2 + e % 2][:, :], ACT.Gelu).then_inc(S("a_ready"), 1)

            def output(b, q, r):
                t = b * TPB + q
                act.wait_ge(S("o2_mm"), t + 3)
                act.activation(o2[:, bass.ds(t, 1), :].squeeze(1), pb[1][:, 0:D], ACT.Copy).then_inc(S("o2_done"), 1)

            def tile(b, q, r, where):
                t = b * TPB + q
                for h in range(PH):
                    act.wait_ge(S("z_pool"), t * PH + (h + 2))
                    act.wait_ge(S("mk_done"), t * PH + (h + 1))
                    act.activation(SG[:, h % RING, :], Z[:, h, :], ACT.Sigmoid).then_inc(S("sg_done"), 1)
                    if h == 1 and where != "last":
                        scores_in(*following(b, q, r))
                    if h == 5 and where != "first":
                        output(*preceding(b, q, r))
                if not final(b):
                    if q == 0 and where != "first":
                        act.wait_ge(S("wt_done"), 2 * TPB * b + 1)
                    hidden_in(b + 1, 1 - r, (2 * q, 2 * q + 1))
                if where == "last":
                    output(b, q, r)
            scores_in(0, 0, 0)
            hidden_in(0, 0, range(EB))
            over_tiles(act, tile)
            act.wait_ge(S("o2_done"), NT + 1)

            def gate_out(b):
                ob = o2[:, bass.ds(b * TPB, TPB), :]
                act.activation(ob, ob, ACT.Silu).then_inc(S("g2_ready"), 1)
            gate_out(0)
            with act.Fori(1, NB) as b:
                gate_out(b)

        def vector_layer1(dve):
            dve.sem_inc(S("at_o"), CREDIT)
            dve.sem_inc(S("mk_done"), RING)
            dve.sem_inc(S("wt_done"), 1)
            dve.wait_ge(S("x1_done"), NB + 1)
            moments(dve, acc, ("ln2_v", "ln2_var", "ln2_std", "ln2_done"), [])

            def renormed(b, r):
                dve.wait_ge(S("x2_copied"), b + 1)
                for q in range(TPB):
                    op = normed(dve, xst[:, r, q, :], acc, b * TPB + q)
                op.then_inc(S("x2_ready"), 1)

            def feature_sums(b):
                dve.bn_stats(bnst[:, bass.ds(b * 6, 6)], xT[:, seq(b)]).then_inc(S("bn_v"), 1)
            renormed(0, 0)
            renormed(1, 1)
            with dve.Fori(1, NB // 2) as pair:
                for r in range(2):
                    renormed(pair * 2 + r, r)
                    feature_sums(pair * 2 + (r - 2))
            dve.wait_ge(S("x2_copied"), NB + CREDIT)
            feature_sums(NB - 2)
            feature_sums(NB - 1)
            dve.wait_ge(S("bn_v"), NB)
            dve.bn_aggr(bnc[:, 0:2], bnst).then_inc(S("bn_var"), 1)
            dve.wait_ge(S("bn_std"), 1)
            dve.reciprocal(bnc[:, 2:3], bnc[:, 2:3]).then_inc(S("bn_v"), 1)
            dve.tensor_scalar(bqs, col("bq"), SCALE, None, ALU.mult).then_inc(S("bq_ready"), 1)
            dve.wait_ge(S("bn_v"), NB + 1)
            dve.tensor_tensor(bnc[:, 2:3], bnc[:, 2:3], col("gamma"), ALU.mult).then_inc(S("bn_v"), 1)
            dve.wait_ge(S("bn_v"), NB + 2)
            dve.tensor_tensor(bnc[:, 3:4], bnc[:, 2:3], bnc[:, 0:1], ALU.mult).then_inc(S("bn_v"), 1)
            dve.wait_ge(S("bn_v"), NB + 3)
            dve.tensor_tensor(bnc[:, 3:4], col("bbeta"), bnc[:, 3:4], ALU.subtract).then_inc(S("bn_v"), 1)
            dve.wait_ge(S("bn_v"), NB + 4)

            def top(b, q):
                dve.wait_ge(S("at_s"), b * TPB + (q + 1 + CREDIT))
                dve.tensor_reduce(ac[:, q, 0:1], pb[2 + q % 2][:, :], AX.X, ALU.max, negate=True).then_inc(S("at_m"), 1)

            def tile(b, q, r, where):
                t = b * TPB + q
                if exists(b, q, 2):
                    top(*following(*following(b, q, r))[0:2])
                z, rz, mz = (ac[:, q, k:k + 1] for k in (1, 2, 3))
                dve.wait_ge(S("at_p"), t + 1 + CREDIT)
                dve.reciprocal(rz, z).then_inc(S("at_z"), 1)
                dve.wait_ge(S("at_z"), 3 * t + 1)
                dve.tensor_tensor(mz, z, rz, ALU.mult).then_inc(S("at_z"), 1)
                dve.wait_ge(S("at_z"), 3 * t + 2)
                dve.tensor_scalar(mz, mz, -1.0 / L, -1.0 / L, ALU.mult, ALU.add).then_inc(S("at_z"), 1)
                dve.wait_ge(S("at_v"), t + 1 + CREDIT)
                dve.scalar_tensor_tensor(atmp[:, q % 2, :], pb[6 + q % 2][:, 0:D], rz,
                                         xn2[:, bass.ds(t, 1), :].squeeze(1), ALU.mult, ALU.add).then_inc(S("at_x"), 1)
                dve.wait_ge(S("at_z"), 3 * t + 3)
                dve.wait_ge(S("at_x"), t + 1)
                dve.scalar_tensor_tensor(s1[:, bass.ds(t, 1), :].squeeze(1), xsum[:, bass.ds(b, 1), :].squeeze(1), mz,
                                         atmp[:, q % 2, :], ALU.mult, ALU.add).then_inc(S("at_o"), 1)
            top(0, 0)
            top(0, 1)
            over_tiles(dve, tile)

            def bn_apply(b, r):
                dve.tensor_scalar(xb[:, r, :], xT[:, seq(b)], bnc[:, 2:3], bnc[:, 3:4], ALU.mult,
                                  ALU.add).then_inc(S("xb_ready"), 1)

            def picks(b, q):
                t = b * TPB + q
                dve.wait_ge(S("sm_ready"), t + 2)
                dve.sem_inc(S("picks_at"), 1)
                for h in range(PH):
                    for s_ in range(2):
                        op = dve.max(tv[:, q % 2, h, s_, :], sim[:, q % 2, h, s_, :])
                op.then_inc(S("tk_v"), 1)
                dve.wait_ge(S("tk_v"), 2 * t + 1)
                dve.tensor_tensor(cand, tv[:, q % 2, :, 0, :].unsqueeze(3).to_broadcast([P, PH, PK, PK]),
                                  tv[:, q % 2, :, 1, :].unsqueeze(2).to_broadcast([P, PH, PK, PK]),
                                  ALU.add).then_inc(S("tk_v"), 1)
                dve.wait_ge(S("tk_v"), 2 * t + 2)
                dve.sem_inc(S("picks_at"), 1)
                for h in range(PH):
                    op = dve.max(t8[:, q % 2, h, :], cand[:, h].rearrange("p a b -> p (a b)"))
                op.then_inc(S("tk_done"), 1)

            def weigh_hidden(b, q, r):
                t = b * TPB + q
                dve.wait_ge(S("tc"), (t + 2) * PH)
                dve.wait_ge(S("a_ready"), (b + 1) * EB + 2)
                dve.wait_ge(S("o2_mm"), t + 1)
                for k in range(2):
                    dve.tensor_tensor(Wt[:, q % 2, 4 * k:4 * k + 4, :],
                                      pb[4 + 2 * (q % 2) + k][:, :].rearrange("p (e n) -> p e n", e=4),
                                      AB[r][:, 4 * k:4 * k + 4, q * P:(q + 1) * P], ALU.mult).then_inc(S("wt_done"), 1)

            def tile(b, q, r, where):
                t = b * TPB + q
                if q == 1 and not final(b):
                    bn_apply(b + 1, 1 - r)
                dve.wait_ge(S("tk_done"), t + 1)
                for h in range(PH):
                    k = t * PH + (h + 1)
                    dve.wait_ge(S("sg_done"), k + RING)
                    dve.scalar_tensor_tensor(Z[:, h, :], Z[:, h, :], t8[:, q % 2, h, 7:8],
                                             SG[:, h % RING, :], ALU.is_ge, ALU.mult).then_inc(S("mk_done"), 1)
                    if h == 1 and where != "first":
                        weigh_hidden(*preceding(b, q, r))
                    if h == 3:
                        if where != "last":
                            picks(*following(b, q, r)[0:2])
                if where == "last":
                    weigh_hidden(b, q, r)
            bn_apply(0, 0)
            picks(0, 0)
            over_tiles(dve, tile)
            with dve.Fori(0, NB) as b:
                bt = bass.ds(b * TPB, TPB)
                dve.wait_ge(S("g2_ready"), b + 1)
                dve.tensor_tensor(s1[:, bt, :], s1[:, bt, :], o2[:, bt, :], ALU.mult).then_inc(S("y_mul"), 1)

        @block.sync
        def _(sp):
            for k in range(4):
                sp.dma_start(x_in[:, k * (NT // 4):(k + 1) * (NT // 4), :],
                             a["x"].rearrange("(k t p) d -> k p t d", k=4, p=P)[k]).then_inc(S(f"ld_x{k}"), 16)
            for dst, src in ((con[:, :], a["con"]), (small[:, :], a["small"]),
                             (rows[:, 0:16], a["bf2"].partition_broadcast(P)),
                             (rows[:, 16:20], a["tau"].partition_broadcast(P)),
                             (rows[:, 20:28], a["gb"].partition_broadcast(P))):
                sp.dma_start(dst, src).then_inc(S("ld_const"), 16)
            for dst, src in ((wproj[:, 0, :], a["Wq"]), (wproj[:, 1, :], a["Wk"]), (wproj[:, 2, :], a["Wv"]),
                             (wb[:, :], a["Wb"]), (gatew[:, :], a["gw"]), (wo[:, :], a["Wo"]),
                             (wf1[:, :, :], a["Wf1"].rearrange("(k p) n -> p k n", p=P)),
                             (wf2[:, :, :], a["Wf2"].rearrange("(k p) n -> p k n", p=P)),
                             (b2[0:E, :], a["b2"]), (b2[E:NX, :], a["bs2"])):
                sp.dma_start(dst, src).then_inc(S("ld_w"), 16)
            for dst, src in ((w1[:, 0:EA, :], a["w1"][0:EA].rearrange("e p n -> p e n")),
                             (w2[:, 0:EA], a["w2"][0:EA].rearrange("e (m p) d -> p e m d", p=P))):
                sp.dma_start(dst, src).then_inc(S("ld_ea"), 16)
            sp.wait_ge(S("beta_done"), NB + CREDIT)
            sp.dma_start(beta_d, beta_sb.rearrange("h (n c) -> h n c", c=C)).then_inc(S("beta_out"), 16)
            sp.wait_ge(S("beta_out"), 16)
            sp.dma_start(beta_it[:, :, :], beta_d.rearrange("h n c -> n h c")).then_inc(S("beta_in"), 16)
            with sp.Fori(0, NB // 2) as pair:
                b0 = pair * 2
                for r in range(2):
                    sp.wait_ge(S("gram_v"), (b0 + (r + 1)) * TPB + TPB)
                    sp.wait_ge(S("v_turned"), (b0 + (r + 1)) * TPB + TPB)
                    sp.dma_start(gram_d[bass.ds((b0 + r) * NCH, NCH)].rearrange("n h j i -> (h j) n i"),
                                 cst[:, r, :, 0, :]).then_inc(S(f"cst_out{r}"), 16)
                    sp.dma_start(lv_d[:, bass.ds((b0 + r) * NCH, NCH)], cst[:, r, :, 1:3, :]).then_inc(S(f"cst_out{r}"), 16)
            for r in range(2):
                sp.wait_ge(S(f"cst_out{r}"), 16 * NB + 32)
            sp.wait_ge(S("k_turned"), NB + CREDIT)
            sp.dma_start(att[:, :, :, :], gram_d).then_inc(S("ld_att"), 16)
            sp.wait_ge(S("nrm_done"), NB + CREDIT)
            sp.wait_ge(S("nrm_half"), 2 * NB + 2 * CREDIT)
            for dst, src in ((w1[:, EA:E, :], a["w1"][EA:E].rearrange("e p n -> p e n")), (w1[:, E, :], a["ws1"]),
                             (w2[:, EA:E], a["w2"][EA:E].rearrange("e (m p) d -> p e m d", p=P)),
                             (w2[:, E], a["ws2"].rearrange("(m p) d -> p m d", p=P))):
                sp.dma_start(dst, src).then_inc(S("ld_eb"), 16)
            sp.wait_ge(S("inv_ready"), 1)
            sp.dma_start(inv_d, att[:, :, :, :]).then_inc(S("inv_out"), 16)
            sp.wait_ge(S("inv_out"), 16)
            sp.wait_ge(S("scan_zero"), 2)

            inv_n = inv_d.rearrange("(b n) h j i -> n h j b i", b=NB)
            lv_n = lv_d.rearrange("p (b n) s c -> p b n s c", b=NB)
            with sp.Fori(0, NCH) as n:
                sp.wait_ge(S("sc_u"), n + 1)
                for h in range(H):
                    sp.dma_start(Gb[h * C:(h + 1) * C, :, h * C:(h + 1) * C],
                                 inv_n[bass.ds(n, 1), h].squeeze(0)).then_inc(S("ld_g"), 16)
                sp.wait_ge(S("sc_o"), n + 1)
                sp.dma_start(lv, lv_n[:, :, bass.ds(n, 1)].squeeze(2)).then_inc(S("ld_lv"), 16)
            sp.wait_ge(S("sc_o"), NCH + 1)
            sp.wait_ge(S("yb_mm"), NB * (NX - EA) + CREDIT)
            with sp.Fori(0, NB) as b:
                sp.wait_ge(S("x1_done"), b + 1)
                sp.dma_start(xr, x_d[bass.ds(b, 1)].squeeze(0)).then_inc(S("ld_xr"), 16)
            sync_layer1(sp)

        @block.gpsimd
        def _(pool):
            pool.memset(pads[:, 0, :, 0:3], 0.0).then_inc(S("zeros"), 1)
            pool.memset(pads[:, 1, :, 0:3], 0.0).then_inc(S("zeros"), 1)
            pool.memset(vT[:, :, 0:PADV], 0.0).then_inc(S("zeros"), 1)
            pool.memset(comb[:, :, E:NX], 1.0).then_inc(S("zeros"), 1)
            pool.wait_ge(S("ld_const"), 80)
            with pool.Fori(0, NB) as b:
                for q in range(TPB):
                    pool.wait_ge(S("nrm_done"), b + 1 + CREDIT)
                    pool.wait_ge(S("gram_mm"), b * TPB + (q + 1))
                    pool.tensor_tensor(
                        KX[:, q % 2].rearrange("p n (h c) -> p n h c", h=H),
                        kq[:, bass.ds(b * NCH + q * 4, 4), 0, :].unsqueeze(2).to_broadcast([P, 4, H, C]),
                        blocks4.unsqueeze(1).to_broadcast([P, 4, H, C]), ALU.mult).then_inc(S("kx_ready"), 1)
            pool.wait_ge(S("ld_att"), 16)
            pool.wait_ge(S("beta_in"), 16)
            pool.tensor_tensor(att, att, beta_it[:, :, :].unsqueeze(2).to_broadcast([P, H, C, C]),
                               ALU.mult).then_inc(S("subst"), 1)
            for j in range(1, C - 1):
                n = C - 1 - j
                prod = RP[:, 0:H * j * n].rearrange("p (h k i) -> p h k i", h=H, k=j)
                pool.wait_ge(S("subst"), 2 * j - 1)
                pool.tensor_tensor(prod, att[:, :, j, j + 1:C].unsqueeze(2).to_broadcast([P, H, j, n]),
                                   att[:, :, 0:j, j].unsqueeze(3).to_broadcast([P, H, j, n]),
                                   ALU.mult).then_inc(S("subst"), 1)
                pool.wait_ge(S("subst"), 2 * j)
                pool.tensor_tensor(att[:, :, 0:j, j + 1:C], att[:, :, 0:j, j + 1:C], prod,
                                   ALU.add).then_inc(S("subst"), 1)
            pool.wait_ge(S("subst"), 2 * C - 3)
            diag = RA[:, :].rearrange("p (h x) -> p h x", h=H)[:, :, 0:C * C:C + 1]
            pool.tensor_scalar(diag, diag, 1.0, None, ALU.add).then_inc(S("subst"), 1)
            pool.wait_ge(S("subst"), 2 * C - 2)
            pool.tensor_tensor(att, att, beta_it[:, :, :].unsqueeze(3).to_broadcast([P, H, C, C]),
                               ALU.mult).then_inc(S("inv_ready"), 1)
            pool.wait_ge(S("gram_a"), NB + CREDIT)
            pool.wait_ge(S("inv_ready"), 1)
            pool.wait_ge(S("ya_mm"), E1 * NB + CREDIT)
            pool.memset(Gb, 0.0).then_inc(S("scan_zero"), 1)
            pool.memset(zero, 0.0).then_inc(S("scan_zero"), 1)
            with pool.Fori(0, NCH) as n:
                pool.wait_ge(S("sc_s"), n + 1)
                pool.tensor_tensor(
                    Kb.rearrange("p b (h c) -> p b h c", h=H),
                    kq5[:, :, bass.ds(n, 1), 0, :].to_broadcast([P, NB, H, C]),
                    blocks4.unsqueeze(1).to_broadcast([P, NB, H, C]), ALU.mult).then_inc(S("sc_k"), 1)
            def fuse_sum(b, r):
                pool.wait_ge(S("fz_mul"), 4 * (b + 1) + 1)
                pool.wait_ge(S("fz_n"), b + 1)
                pool.tensor_tensor(mC[:, 0], mC[:, 0], mC[:, 1], ALU.add).then_inc(S("fz_add"), 1)
                pool.tensor_tensor(mC[:, 2], mC[:, 2], mC[:, 3], ALU.add).then_inc(S("fz_add"), 1)
                pool.wait_ge(S("fz_add"), 3 * b + 2 + 3)
                pool.tensor_tensor(oT[:, r], mC[:, 0], mC[:, 2], ALU.add).then_inc(S("fz_add"), 1)
            with pool.Fori(0, NB // 2) as pair:
                b0 = pair * 2
                for r in range(2):
                    fuse_sum(b0 + r, r)
            pool_layer1(pool)

        @block.tensor
        def _(pe):
            for n in ("xn_turned", "gate_mm", "gram_mm", "ya_mm", "y_mm", "bias_mm", "yb_mm", "fl_mm", "fp_mm"):
                pe.sem_inc(S(n), CREDIT)
            for n in ("sc_u", "sc_s", "sc_o", "fz_ms", "cs_turned", "fz_wo"):
                pe.sem_inc(S(n), 1)
            pe.sem_inc(S("nrm_half"), 2 * CREDIT)
            pe.wait_ge(S("ld_const"), 80)
            with pe.Fori(0, NB // 2) as pair:
                b0 = pair * 2
                for r in range(2):
                    pe.wait_ge(S("xn_ready"), b0 + (r + 1))
                    pe.wait_ge(S("xT_ready"), b0 + (r + 1))
                    for q in range(TPB):
                        mm = pe.transpose(pb[r][:, q * P:(q + 1) * P], xst[:, r, q, :], ident)
                    mm.then_inc(S("xn_turned"), 1)
            pe.wait_ge(S("ld_w"), 160)
            with pe.Fori(0, NB // 2) as pair:
                b0 = pair * 2
                for r in range(2):
                    b = b0 + r
                    pe.wait_ge(S("xs_ready"), b + 1)
                    pe.wait_ge(S("beta_done"), b + 1)
                    pe.wait_ge(S("gl_done"), b + 1)
                    pe.matmul(pb[2 + r][0:H, :], wb[:, :], xs[:, r, :], start=True, stop=True)
                    for q in range(TPB):
                        mm = pe.matmul(pb[4 + r][:, q * E:(q + 1) * E], xs[:, r, q * P:(q + 1) * P], gatew[:, :],
                                       start=True, stop=True)
                    mm.then_inc(S("gate_mm"), 1)
            pe.wait_ge(S("beta_done"), NB + CREDIT)
            pe.wait_ge(S("gl_done"), NB + CREDIT)
            pe.wait_ge(S("xT_ready"), NB + CREDIT)
            pe.wait_ge(S("ld_ea"), 32)

            def conv(b, k):
                pe.matmul(pb[(2, 3, 6)[k]][:, :], wproj[:, k, :], xT[:, seq(b)], start=True, stop=True).then_inc(S("conv_mm"), 1)

            def norm(b, r, k):
                pe.matmul(pb[(7, 2)[k]][:, :], blocks, sq[:, r, k * L:(k + 1) * L], start=True,
                          stop=True).then_inc(S("nrm_half"), 1)

            def products(b, r, q):
                pe.wait_ge(S("kx_ready"), b * TPB + (q + 1))
                bank = pb[(3, 6, 7, 2)[q]][:, 0:8 * C].rearrange("p (n c) -> p n c", n=4)
                for i in range(4):
                    mm = pe.matmul(bank[:, i, 0:2 * C], KX[:, q % 2, i, :],
                                   kq[:, bass.ds(b * NCH + (q * 4 + i), 1), :, :].rearrange("p n s c -> p (n s c)"),
                                   start=True, stop=True)
                mm.then_inc(S("gram_mm"), 1)

            def hidden(u, b, e, ms):
                for m in ms:
                    pe.wait_ge(S("ha_ready"), u * MB + (m + 1))
                    pe.matmul(pb[m % 2][:, :], w1[:, e, m * P:(m + 1) * P], xT[:, seq(b)],
                              start=True, stop=True).then_inc(S("ha_mm"), 1)

            def out_half(u, e, r, half):
                if half == 0:
                    pe.wait_ge(S("ha_ready"), u * MB + (MB + 2))
                    pe.wait_ge(S("ya_added"), u * TPB + TPB)
                for q in (2 * half, 2 * half + 1):
                    for m in range(MB):
                        mm = pe.matmul(pb[4 + r][:, q * P:(q + 1) * P], hT[:, r, m, q * P:(q + 1) * P],
                                       w2[:, e, m, :], start=(m == 0), stop=(m == MB - 1))
                if half == 1:
                    mm.then_inc(S("ya_mm"), 1)

            def norm_first(b, r):
                pe.wait_ge(S("nrm_sq"), b + 1)
                norm(b, r, 0)

            def norm_second(b, r, conv_on):
                if conv_on:
                    pe.wait_ge(S("conv_evac"), b + 2 + CREDIT)
                norm(b, r, 1)

            def products_first(b, r, conv_on):
                if conv_on:
                    pe.wait_ge(S("conv_evac"), b + 3 + CREDIT)
                products(b, r, 0)

            def products_third(b, r, norm_on):
                pe.wait_ge(S("nrm_rt"), b + (2 if norm_on else 1) + CREDIT)
                products(b, r, 2)

            def body(b, r, conv_on, norm_on, products_on, experts_on):
                u = b * E1
                if products_on:
                    pe.wait_ge(S("gram_v"), b * TPB - TPB)
                if norm_on:
                    pe.wait_ge(S("nrm_rt"), b + 1)
                if conv_on:
                    pe.wait_ge(S("conv_evac"), b + CREDIT)
                if experts_on:
                    hidden(u, b, 0, (0, 1))
                if conv_on:
                    conv(b, 0)
                if experts_on:
                    hidden(u, b, 0, (2, 3))
                if conv_on:
                    conv(b, 1)
                if experts_on:
                    out_half(u, 0, r, 0)
                if conv_on:
                    conv(b, 2)
                if experts_on:
                    out_half(u, 0, r, 1)
                    hidden(u + 1, b, 1, (0, 1))
                if norm_on:
                    norm_first(b - 1, 1 - r)
                if experts_on:
                    hidden(u + 1, b, 1, (2, 3))
                if norm_on:
                    norm_second(b - 1, 1 - r, conv_on)
                if experts_on:
                    out_half(u + 1, 1, 1 - r, 0)
                    out_half(u + 1, 1, 1 - r, 1)
                    hidden(u + 2, b, 2, (0, 1))
                if products_on:
                    products_first(b - 2, r, conv_on)
                if experts_on:
                    hidden(u + 2, b, 2, (2, 3))
                if products_on:
                    products(b - 2, r, 1)
                if experts_on:
                    out_half(u + 2, 2, r, 0)
                if products_on:
                    products_third(b - 2, r, norm_on)
                if experts_on:
                    out_half(u + 2, 2, r, 1)
                if products_on:
                    products(b - 2, r, 3)
            over_stages(pe, body)
            pe.wait_ge(S("gram_v"), NB * TPB + TPB)
            pe.wait_ge(S("ha_ready"), E1 * NB * MB + 2)
            pe.wait_ge(S("ya_added"), E1 * NB * TPB + ACCC)
            with pe.Fori(0, NB) as b:
                def hidden_next(j):
                    for m in range(MB):
                        pe.wait_ge(S("h_ready"), (b * E2 + j) * MB + (m + 1))
                        pe.matmul(pb[m][:, :], w1[:, E1 + j, m * P:(m + 1) * P], xT[:, seq(b)],
                                  start=True, stop=True).then_inc(S("h_mm"), 1)

                hidden_next(0)
                for j in range(E2):
                    if j + 1 < E2:
                        hidden_next(j + 1)
                    pe.wait_ge(S("h_ready"), (b * E2 + (j + 1)) * MB + MB)
                    pe.wait_ge(S("y_added"), 4 * (b * E2 + (j + 1)))
                    for q in range(TPB):
                        for m in range(MB):
                            mm = pe.matmul(pb[4 + j % 2][:, q * P:(q + 1) * P], hT[:, j % 2, m, q * P:(q + 1) * P],
                                           w2[:, E1 + j, m, :], start=(m == 0), stop=(m == MB - 1))
                    mm.then_inc(S("y_mm"), 1)
                    if j == 0:
                        pe.wait_ge(S("cs_ready"), b + 1)
                        pe.wait_ge(S("ct_ready"), b + 1)
                        for q in range(TPB):
                            mm = pe.transpose(pb[6][0:NX, q * P:(q + 1) * P], cs[:, q, :], ident)
                        mm.then_inc(S("cs_turned"), 1)
                pe.wait_ge(S("ct_ready"), b + 2)
                pe.wait_ge(S("bias_added"), b + 1)
                for q in range(TPB):
                    mm = pe.matmul(pb[7][:, q * P:(q + 1) * P], cT[:, q * P:(q + 1) * P], b2[:, :],
                                   start=True, stop=True)
                mm.then_inc(S("bias_mm"), 1)
            pe.wait_ge(S("scan_zero"), 2)
            pe.wait_ge(S("y_added"), 4 * E2 * NB + ACCC)
            pe.wait_ge(S("bias_added"), NB + 1)
            pe.wait_ge(S("h_ready"), E2 * NB * MB + MB)
            pe.wait_ge(S("ld_eb"), 64)
            pe.wait_ge(S("ct_ready"), NB + 1)
            pe.matmul(pb[7][:, 0:NB * C], blocks, zero, start=True, stop=False, skip_group_check=True)

            def expert_hidden(v, b, e, ms):
                for m in ms:
                    pe.wait_ge(S("hb_ready"), v * MB + (m + 1))
                    pe.matmul(pb[m % 2][:, :], w1[:, e, m * P:(m + 1) * P], xT[:, seq(b)],
                              start=True, stop=True).then_inc(S("hb_mm"), 1)

            def expert_out(v, e, r, half):
                if half == 0:
                    pe.wait_ge(S("hb_ready"), v * MB + (MB + 2))
                    pe.wait_ge(S("yb_added"), v * TPB + TPB)
                for q in (2 * half, 2 * half + 1):
                    for m in range(MB):
                        mm = pe.matmul(pb[4 + r][:, q * P:(q + 1) * P], hT[:, r, m, q * P:(q + 1) * P],
                                       w2[:, e, m, :], start=(m == 0), stop=(m == MB - 1))
                if half == 1:
                    mm.then_inc(S("yb_mm"), 1)

            def step_w(n, half):
                if half == 0:
                    pe.wait_ge(S("sc_k"), n + 1)
                    pe.wait_ge(S("ld_g"), n * 64 + 64)
                    pe.wait_ge(S("sc_wn"), n + 1)
                for b in range(4 * half, 4 * half + 4):
                    mm = pe.matmul(pb[2 + half][:, (b % 4) * P:(b % 4 + 1) * P], Kb[:, b, :], Gb[:, b, :],
                                   start=True, stop=True)
                if half == 1:
                    mm.then_inc(S("sc_w"), 1)

            def step_u(n, half):
                if half == 0:
                    pe.wait_ge(S("sc_wn"), n + 2)
                    pe.wait_ge(S("ld_lv"), n * 16 + 16)
                    pe.wait_ge(S("sc_s4"), n + 1)
                    pe.wait_ge(S("sc_oe"), n + 1)
                for b in range(4 * half, 4 * half + 4):
                    o = pb[6][:, b * C:(b + 1) * C]
                    pe.matmul(o, Gb[:, b, :], lv[:, b, 1, :], start=True, stop=False)
                    mm = pe.matmul(o, Wn[:, b, :], S4[:, b, :], start=False, stop=True)
                if half == 1:
                    mm.then_inc(S("sc_u"), 1)

            def step_s(n):
                pe.wait_ge(S("sc_u4"), n + 1)
                for b in range(NB):
                    mm = pe.matmul(pb[7][:, b * C:(b + 1) * C], Kb[:, b, :], U4[:, b, :],
                                   start=False, stop=False, skip_group_check=True)
                mm.then_inc(S("sc_s"), 1)

            def step_o(n, half):
                if half == 0:
                    pe.wait_ge(S("sc_ub"), n + 2)
                    pe.wait_ge(S("sc_sb"), n + 1)
                for b in range(4 * half, 4 * half + 4):
                    o = pb[6][:, b * C:(b + 1) * C]
                    pe.matmul(o, Sb[:, b, :], kq5[:, b, bass.ds(n, 1), 1, :].rearrange("p n c -> p (n c)"),
                              start=True, stop=False)
                    mm = pe.matmul(o, Ub[:, b, :], lv[:, b, 0, :], start=False, stop=True)
                if half == 1:
                    mm.then_inc(S("sc_o"), 1)

            def step(n, v, i, e):
                expert_hidden(v, i * 2, e, (0, 1))
                step_w(n, 0)
                expert_hidden(v, i * 2, e, (2, 3))
                step_w(n, 1)
                expert_out(v, e, 0, 0)
                step_u(n, 0)
                expert_out(v, e, 0, 1)
                step_u(n, 1)
                expert_hidden(v + 1, i * 2 + 1, e, (0, 1))
                step_s(n)
                expert_hidden(v + 1, i * 2 + 1, e, (2, 3))
                step_o(n, 0)
                expert_out(v + 1, e, 1, 0)
                step_o(n, 1)
                expert_out(v + 1, e, 1, 1)
            over_steps(pe, step)
            pe.wait_ge(S("sc_oe"), NCH + 1)
            pe.wait_ge(S("yb_added"), TPB * NB * (NX - EA) + ACCC)
            pe.wait_ge(S("hb_ready"), MB * NB * (NX - EA) + 2)

            def fuse_hidden(b, m):
                pe.wait_ge(S("fh_ready"), 2 * b + (m + 1))
                srcs = [xT[:, seq(b)], firs[:, bass.ds(b, 1), :].squeeze(1), firl[:, bass.ds(b, 1), :].squeeze(1),
                        dT[:, bass.ds(b, 1), :].squeeze(1)]
                for k in range(4):
                    mm = pe.matmul(pb[m][:, :], wf1[:, k, m * P:(m + 1) * P], srcs[k], start=(k == 0), stop=(k == 3))
                mm.then_inc(S("fh_mm"), 1)

            def fuse_logits(b, r):
                pe.wait_ge(S("fh_ready"), 2 * b + 2 + CREDIT)
                pe.wait_ge(S("fl_done"), b + 1)
                for q in range(TPB):
                    for m in range(2):
                        mm = pe.matmul(pb[2][:, q * 16:(q + 1) * 16], hidT[:, r, m, q * P:(q + 1) * P],
                                       wf2[:, m, :], start=(m == 0), stop=(m == 1))
                mm.then_inc(S("fl_mm"), 1)

            def path_weights(b, r):
                pe.wait_ge(S("fp_ready"), b + 1)
                pe.wait_ge(S("fz_mul"), 4 * b + 1)
                for c in range(4):
                    for q in range(TPB):
                        mm = pe.transpose(pb[3 + c][:, q * P:(q + 1) * P], Pst[:, r, q, c, :], ident)
                mm.then_inc(S("fp_mm"), 1)

            def mean_square(b):
                pe.wait_ge(S("fz_sq"), b + 1)
                pe.wait_ge(S("fz_sg"), b + 1)
                pe.matmul(pb[7][:, :], blocks, sqo, start=True, stop=True).then_inc(S("fz_ms"), 1)

            def project_out(b):
                pe.wait_ge(S("fz_n"), b + 1 + CREDIT)
                pe.wait_ge(S("fz_rt"), b + 2)
                for q in range(TPB):
                    mm = pe.matmul(pb[7][:, q * P:(q + 1) * P], oN[:, q * P:(q + 1) * P], wo[:, :],
                                   start=True, stop=True)
                mm.then_inc(S("fz_wo"), 1)

            def body(b, r, gate, paths_on, out_on, _):
                if gate:
                    fuse_hidden(b, 0)
                if out_on:
                    mean_square(b - 2)
                if gate:
                    fuse_hidden(b, 1)
                if paths_on:
                    path_weights(b - 1, 1 - r)
                if gate:
                    fuse_logits(b, r)
                if out_on:
                    project_out(b - 2)
            pe.wait_ge(S("sc_s4"), NCH + 1)
            over_stages(pe, body)
            tensor_layer1(pe)

        @block.scalar
        def _(act):
            act.sem_inc(S("xT_ready"), CREDIT)
            act.sem_inc(S("beta_done"), CREDIT)
            act.sem_inc(S("conv_evac"), CREDIT)
            act.sem_inc(S("silu_done"), CREDIT)
            act.sem_inc(S("nrm_rt"), CREDIT)
            act.sem_inc(S("gram_a"), CREDIT)
            act.sem_inc(S("h_ready"), MB)
            act.sem_inc(S("ct_ready"), 1)
            act.sem_inc(S("sc_wn"), 1)
            act.sem_inc(S("sc_oe"), 1)
            act.sem_inc(S("hb_ready"), 2)
            act.sem_inc(S("ha_ready"), 2)
            act.sem_inc(S("fh_ready"), CREDIT)
            act.sem_inc(S("fz_rt"), 1)
            act.wait_ge(S("ld_const"), 80)
            act.wait_ge(S("ln_var"), 1)
            act.activation(rstd[:, :], lntmp[:, 1, :], ACT.Sqrt, bias=eps5).then_inc(S("ln_std"), 1)
            with act.Fori(0, NB // 2) as pair:
                b0 = pair * 2
                for r in range(2):
                    act.wait_ge(S("xn_turned"), b0 + (r + 1 + CREDIT))
                    act.activation(xT[:, seq(b0 + r)], pb[r][:, :], ACT.Copy).then_inc(S("xT_ready"), 1)

            def gate_in(b, r):
                act.wait_ge(S("xT_ready"), b + 1 + CREDIT)
                act.wait_ge(S("gate_mm"), b + 1)
                act.activation(xs[:, r, :], xT[:, seq(b)], ACT.Copy).then_inc(S("xs_ready"), 1)

            def gate_beta(b, r):
                act.wait_ge(S("gate_mm"), b + 1 + CREDIT)
                act.activation(beta_sb[:, seq(b)], pb[2 + r][0:H, :], ACT.Sigmoid).then_inc(S("beta_done"), 1)
            staggered(act, gate_in, gate_beta)

            act.wait_ge(S("zeros"), 4)
            act.wait_ge(S("gate_mm"), NB + CREDIT)

            def hidden(u, e, r):
                act.wait_ge(S("ya_mm"), u + 1)
                for m in range(MB):
                    act.wait_ge(S("ha_mm"), u * MB + (m + 1))
                    act.activation(hT[:, r, m, :], pb[m % 2][:, :], ACT.Gelu,
                                   bias=col("b1", e * MB + m)).then_inc(S("ha_ready"), 1)

            def conv_in(b, r):
                act.wait_ge(S("conv_tap"), 12 * (b + 1))
                for k in range(3):
                    act.wait_ge(S("conv_mm"), 3 * b + (k + 1))
                    op = act.activation(pads[:, r, k, 3:CW], pb[(2, 3, 6)[k]][:, :], ACT.Copy)
                op.then_inc(S("conv_evac"), 1)

            def conv_out(b, r):
                act.wait_ge(S("conv_tap"), 12 * (b + 1) + CONVC)
                items = bass.ds(b * NCH, NCH)
                v3 = [cacc[:, r, k, :].rearrange("p (n c) -> p n c", n=NCH) for k in range(2)]
                act.activation(kq[:, items, 1, :], v3[0], ACT.Silu)
                act.activation(kq[:, items, 0, :], v3[1], ACT.Silu)
                act.activation(vtok[:, bass.ds(b, 1), :].squeeze(1), cacc[:, r, 2, :],
                               ACT.Silu).then_inc(S("silu_done"), 1)
                act.wait_ge(S("silu_done"), b + 1 + CREDIT)
                act.wait_ge(S("nrm_half"), 2 * b + 2)
                act.activation(sq[:, r, :], RK[:, seq(b, 2 * L)], ACT.Square).then_inc(S("nrm_sq"), 1)

            def nrm_root(b, r):
                act.wait_ge(S("nrm_done"), b + 1)
                for k in range(2):
                    act.wait_ge(S("nrm_half"), 2 * b + (k + 1 + 2 * CREDIT))
                    op = act.activation(rn[:, r, k * L:(k + 1) * L], pb[(7, 2)[k]][:, :], ACT.Sqrt, bias=eps6)
                op.then_inc(S("nrm_rt"), 1)

            def kv_copy(b, r):
                act.wait_ge(S("k_turned"), b + 1)
                act.wait_ge(S("nrm_done"), b + 1 + CREDIT)
                act.sem_inc(S("keys_at"), 1)
                act.activation(kv_in[r][:, 0], kq[:, bass.ds(b * NCH, NCH), 0, :], ACT.Copy)
                act.activation(kv_in[r][:, 1].rearrange("p n c -> p (n c)"), vtok[:, bass.ds(b, 1), :].squeeze(1),
                               ACT.Copy).then_inc(S("kv_in"), 1)

            def keys_back(b, r):
                act.wait_ge(S("gram_mm"), (b + 1) * TPB + CREDIT)
                act.wait_ge(S("k_turned"), b + 1 + CREDIT)
                act.sem_inc(S("keys_at"), 1)
                act.activation(kq[:, bass.ds(b * NCH, NCH), 0, :], kt[:, r], ACT.Copy).then_inc(S("gram_a"), 1)

            def body(b, r, conv_on, norm_on, products_on, experts_on):
                u = b * E1
                if experts_on:
                    hidden(u, 0, r)
                if products_on:
                    kv_copy(b - 2, r)
                if conv_on:
                    conv_in(b, r)
                if isinstance(b, int) and b == 0:
                    act.wait_ge(S("topk"), 10)
                    act.activation(tw[:, 2, :], tw[:, 2, :], ACT.Exp).then_inc(S("top_e"), 1)
                if experts_on:
                    hidden(u + 1, 1, 1 - r)
                if norm_on:
                    nrm_root(b - 1, 1 - r)
                if experts_on:
                    hidden(u + 2, 2, r)
                if conv_on:
                    conv_out(b, r)
                if products_on:
                    keys_back(b - 2, r)
            over_stages(act, body)
            act.wait_ge(S("ya_mm"), E1 * NB + CREDIT)
            with act.Fori(0, NB) as b:
                for j in range(E2):
                    for m in range(MB):
                        act.wait_ge(S("h_mm"), (b * E2 + j) * MB + (m + 1))
                        if m == 0:
                            act.wait_ge(S("y_mm"), b * E2 + (j + 1))
                        act.activation(hT[:, j % 2, m, :], pb[m][:, :], ACT.Gelu,
                                       bias=col("b1", (E1 + j) * MB + m)).then_inc(S("h_ready"), 1)
                    if j == E2 - 1:
                        act.wait_ge(S("cs_turned"), b + 2)
                        act.wait_ge(S("bias_mm"), b + CREDIT)
                        act.activation(cT, pb[6][0:NX, :], ACT.Copy).then_inc(S("ct_ready"), 1)
            act.wait_ge(S("inv_out"), 16)
            act.wait_ge(S("y_mm"), E2 * NB + CREDIT)

            def expert_hidden(v, e, r):
                act.wait_ge(S("yb_mm"), v + 1)
                for m in range(MB):
                    act.wait_ge(S("hb_mm"), v * MB + (m + 1))
                    act.activation(hT[:, r, m, :], pb[m % 2][:, :], ACT.Gelu,
                                   bias=col("b1", e * MB + m)).then_inc(S("hb_ready"), 1)

            def step(n, v, i, e):
                expert_hidden(v, e, 0)
                act.wait_ge(S("sc_w"), n + 1)
                act.wait_ge(S("sc_u"), n + 1)
                for k in range(2):
                    op = act.activation(Wn[:, 4 * k:4 * k + 4, :].rearrange("p b c -> p (b c)"), pb[2 + k][:, :],
                                        ACT.Copy, scale=-1.0)
                op.then_inc(S("sc_wn"), 1)
                act.wait_ge(S("sc_u"), n + 2)
                act.wait_ge(S("sc_s"), n + 1)
                act.wait_ge(S("sc_ub"), n + 1)
                act.activation(U4.rearrange("p b c -> p (b c)"), pb[6][:, 0:NB * C], ACT.Copy).then_inc(S("sc_u4"), 1)
                expert_hidden(v + 1, e, 1)
                act.wait_ge(S("sc_s"), n + 2)
                act.wait_ge(S("sc_sb"), n + 1)
                act.activation(S4.rearrange("p b c -> p (b c)"), pb[7][:, 0:NB * C], ACT.Copy).then_inc(S("sc_s4"), 1)
                act.wait_ge(S("sc_o"), n + 2)
                act.activation(dT[:, :, bass.ds(n * C, C)], pb[6][:, 0:NB * C].rearrange("p (b c) -> p b c", b=NB),
                               ACT.Copy).then_inc(S("sc_oe"), 1)
            over_steps(act, step)
            act.wait_ge(S("yb_added"), TPB * NB * (NX - EA) + ACCC)
            act.activation(acc[:, :, :], acc[:, :, :], ACT.Silu).then_inc(S("g_ready"), 1)
            act.wait_ge(S("yb_mm"), NB * (NX - EA) + CREDIT)
            act.wait_ge(S("sc_sb"), NCH + 1)
            act.activation(itau, rows[:, 16:20], ACT.Exp, scale=-1.0).then_inc(S("itau"), 1)

            def fuse_gelu(b, r, m):
                act.wait_ge(S("fh_mm"), 2 * b + (m + 1))
                if m == 0:
                    act.wait_ge(S("fl_mm"), b + 1)
                act.activation(hidT[:, r, m, :], pb[m][:, :], ACT.Gelu, bias=col("bf1", m)).then_inc(S("fh_ready"), 1)

            def exponentials(b):
                act.wait_ge(S("fg"), b * FG + 3)
                act.activation(others, others, ACT.Exp).then_inc(S("fg_e"), 1)
                act.activation(pval, lg[:, bass.ds(b * TPB, TPB), :, 3], ACT.Exp, scale=-1.0).then_inc(S("fg_e"), 1)

            def path_spread(b, r):
                act.wait_ge(S("pg_ready"), b + 1)
                act.wait_ge(S("fp_mm"), b + 1)
                act.activation(
                    Pst[:, r].rearrange("p q c (h d) -> p (q c h) d", h=H),
                    PG[:, bass.ds(b * TPB, TPB)].rearrange("p t c h -> p (t c h)").unsqueeze(2).to_broadcast([P, 64, DK]),
                    ACT.Copy).then_inc(S("fp_ready"), 1)

            def squares(b, r):
                act.wait_ge(S("fz_add"), 3 * (b + 1) + 3)
                act.wait_ge(S("fz_ms"), b + 1)
                act.activation(sqo, oT[:, r], ACT.Square).then_inc(S("fz_sq"), 1)

            def root(b):
                act.wait_ge(S("fz_ms"), b + 2)
                act.wait_ge(S("fz_n"), b + 2)
                act.activation(rr, pb[7][:, :], ACT.Sqrt, scale=1.0 / DK, bias=eps5).then_inc(S("fz_rt"), 1)

            def body(b, r, gate, paths_on, out_on, _):
                if paths_on:
                    exponentials(b - 1)
                if out_on:
                    squares(b - 2, r)
                if gate:
                    fuse_gelu(b, r, 0)
                if out_on:
                    root(b - 2)
                if paths_on:
                    path_spread(b - 1, 1 - r)
                if gate:
                    fuse_gelu(b, r, 1)
            over_stages(act, body)
            scalar_layer1(act)

        @block.vector
        def _(dve):
            dve.sem_inc(S("gl_done"), CREDIT)
            dve.sem_inc(S("conv_tap"), CONVC)
            dve.sem_inc(S("nrm_done"), CREDIT)
            dve.sem_inc(S("gram_v"), TPB)
            dve.sem_inc(S("v_turned"), TPB)
            dve.sem_inc(S("k_turned"), CREDIT)
            dve.sem_inc(S("cst_out0"), 32)
            dve.sem_inc(S("cst_out1"), 32)
            dve.sem_inc(S("y_added"), ACCC)
            dve.sem_inc(S("sc_ub"), 1)
            dve.sem_inc(S("yb_added"), ACCC)
            dve.sem_inc(S("ya_added"), ACCC)
            dve.sem_inc(S("bias_added"), 1)
            dve.sem_inc(S("fl_done"), 1)
            dve.sem_inc(S("fz_n"), CREDIT)
            dve.sem_inc(S("fz_add"), 3)
            dve.sem_inc(S("fz_sg"), 1)
            dve.sem_inc(S("x1_done"), 1)
            dve.sem_inc(S("fz_mul"), 1)

            moments(dve, x_in, ("ln_v", "ln_var", "ln_std", "ln_done"), [f"ld_x{k}" for k in range(4)])
            with dve.Fori(0, NB // 2) as pair:
                b0 = pair * 2
                for r in range(2):
                    dve.wait_ge(S("xn_turned"), b0 + (r + 1))
                    for q in range(TPB):
                        op = normed(dve, xst[:, r, q, :], x_in, (b0 + r) * TPB + q)
                    op.then_inc(S("xn_ready"), 1)
            gate_b = rows[:, 20:28]
            with dve.Fori(0, NB // 2) as pair:
                b0 = pair * 2
                for r in range(2):
                    dve.wait_ge(S("gate_mm"), b0 + (r + 1 + CREDIT))
                    dve.tensor_tensor(gl[:, bass.ds((b0 + r) * TPB, TPB), :],
                                      pb[4 + r][:, 0:TPB * E].rearrange("p (q e) -> p q e", q=TPB),
                                      gate_b.unsqueeze(1).to_broadcast([P, TPB, E]), ALU.add).then_inc(S("gl_done"), 1)
            n_top = 0

            def t_inc(op):
                op.then_inc(S("topk"), 1)

            bc = [P, NT, E]
            io = iota_e.unsqueeze(1).to_broadcast(bc)
            t8 = [top[:, k, 0:NT * E].rearrange("p (t e) -> p t e", e=E) for k in range(4)]
            m1, m2, df, i1 = (tw[:, k, :] for k in range(4))
            dve.wait_ge(S("gl_done"), NB + CREDIT)

            def best(src, m, oh, k0):
                dve.tensor_reduce(m, src, AX.X, ALU.max).then_inc(S("topk"), 1)
                dve.wait_ge(S("topk"), k0 + 1)
                dve.tensor_tensor(oh, src, m.unsqueeze(2).to_broadcast(bc), ALU.is_equal).then_inc(S("topk"), 1)
                dve.wait_ge(S("topk"), k0 + 2)
                dve.tensor_tensor(oh, oh, io, ALU.mult).then_inc(S("topk"), 1)
                dve.wait_ge(S("topk"), k0 + 3)
                dve.tensor_reduce(i1, oh, AX.X, ALU.min).then_inc(S("topk"), 1)
                dve.wait_ge(S("topk"), k0 + 4)
                dve.tensor_tensor(oh, io, i1.unsqueeze(2).to_broadcast(bc), ALU.is_equal).then_inc(S("topk"), 1)
                dve.wait_ge(S("topk"), k0 + 5)
            best(gl[:, :, :], m1, t8[0], 0)
            dve.scalar_tensor_tensor(t8[1].rearrange("p t e -> p (t e)"), t8[0].rearrange("p t e -> p (t e)"), -3e38,
                                     gl[:, :, :].rearrange("p t e -> p (t e)"), ALU.mult, ALU.add).then_inc(S("top_x"), 1)
            dve.wait_ge(S("top_x"), 1)
            dve.tensor_reduce(m2, t8[1], AX.X, ALU.max).then_inc(S("topk"), 1)
            dve.wait_ge(S("topk"), 6)
            dve.tensor_tensor(df, m2, m1, ALU.subtract).then_inc(S("topk"), 1)
            dve.tensor_tensor(t8[2], t8[1], m2.unsqueeze(2).to_broadcast(bc), ALU.is_equal).then_inc(S("topk"), 1)
            dve.wait_ge(S("topk"), 8)
            dve.tensor_tensor(t8[2], t8[2], io, ALU.mult).then_inc(S("topk"), 1)
            dve.wait_ge(S("topk"), 9)
            dve.tensor_reduce(i1, t8[2], AX.X, ALU.min).then_inc(S("topk"), 1)
            dve.wait_ge(S("topk"), 10)
            dve.tensor_tensor(t8[2], io, i1.unsqueeze(2).to_broadcast(bc), ALU.is_equal).then_inc(S("topk"), 1)
            dve.wait_ge(S("top_e"), 1)
            dve.wait_ge(S("topk"), 11)
            dve.tensor_scalar(m1, df, 1.0, None, ALU.add).then_inc(S("topk"), 1)
            dve.wait_ge(S("topk"), 12)
            dve.reciprocal(m1, m1).then_inc(S("topk"), 1)
            dve.wait_ge(S("topk"), 13)
            dve.tensor_tensor(m2, df, m1, ALU.mult).then_inc(S("topk"), 1)
            dve.tensor_tensor(t8[0], t8[0], m1.unsqueeze(2).to_broadcast(bc), ALU.mult).then_inc(S("topk"), 1)
            dve.wait_ge(S("topk"), 15)
            dve.tensor_tensor(t8[2], t8[2], m2.unsqueeze(2).to_broadcast(bc), ALU.mult).then_inc(S("topk"), 1)
            dve.wait_ge(S("topk"), 16)
            dve.wait_ge(S("zeros"), 4)
            dve.tensor_tensor(comb[:, :, 0:E], t8[0], t8[2], ALU.add).then_inc(S("top_all"), 1)
            dve.wait_ge(S("top_all"), 1)
            dve.wait_ge(S("beta_out"), 16)
            masks = con[:, O_GRAM:O_GRAM + 2 * C]

            def taps(b, r):
                dve.wait_ge(S("conv_evac"), b + 1 + CREDIT)
                dve.wait_ge(S("silu_done"), b + 1)
                for k in range(4):
                    for c3 in range(3):
                        tap, src, dst = col("cw", c3 * 4 + k), pads[:, r, c3, k:k + L], cacc[:, r, c3, :]
                        if k == 0:
                            op = dve.tensor_scalar(dst, src, tap, None, ALU.mult)
                        else:
                            dve.wait_ge(S("conv_tap"), 12 * b + (3 * (k - 1) + c3 + 1 + CONVC))
                            op = dve.scalar_tensor_tensor(dst, src, tap, dst, ALU.mult, ALU.add)
                        op.then_inc(S("conv_tap"), 1)

            def nrm_apply(b, r):
                dve.wait_ge(S("nrm_rt"), b + 1 + CREDIT)
                dve.reciprocal(rn[:, r, :], rn[:, r, :]).then_inc(S("nrm_rec"), 1)
                dve.wait_ge(S("nrm_rec"), b + 1)
                dve.tensor_tensor(RK[:, seq(b, 2 * L)], RK[:, seq(b, 2 * L)], rn[:, r, :],
                                  ALU.mult).then_inc(S("nrm_done"), 1)

            def turn(b, r):
                dve.wait_ge(S(f"cst_out{r}"), 16 * b + (32 - 16 * r))
                dve.wait_ge(S("kv_in"), b + 1)
                dve.transpose(cst[:, r, :, 2, :], kv_in[r][:, 1]).then_inc(S("v_turned"), TPB)
                dve.wait_ge(S("gram_a"), b + 1)
                dve.transpose(kt[:, r], kv_in[r][:, 0]).then_inc(S("k_turned"), 1)

            def mask_products(b, r):
                for q in range(TPB):
                    dve.wait_ge(S("gram_mm"), b * TPB + (q + 1 + CREDIT))
                    bank = pb[(3, 6, 7, 2)[q]][:, 0:8 * C].rearrange("p (n c) -> p n c", n=4)
                    dve.tensor_tensor(cst[:, r, q * 4:q * 4 + 4, 0:2, :].rearrange("p n s c -> p n (s c)"),
                                      bank[:, :, 0:2 * C], masks.unsqueeze(1).to_broadcast([P, 4, 2 * C]),
                                      ALU.mult).then_inc(S("gram_v"), 1)

            def add_first(u, b, e, r):
                dve.wait_ge(S("ya_mm"), u + 1 + CREDIT)
                for q in range(TPB):
                    y = pb[4 + r][:, q * P:(q + 1) * P]
                    dst = acc[:, bass.ds(b * TPB + q, 1), :].squeeze(1)
                    weight = comb[:, bass.ds(b * TPB + q, 1), e:e + 1].squeeze(1)
                    if e == 0:
                        op = dve.tensor_scalar(dst, y, weight, None, ALU.mult)
                    else:
                        dve.wait_ge(S("ya_added"), u * TPB + (q + 1 + ACCC - TPB))
                        op = dve.scalar_tensor_tensor(dst, y, weight, dst, ALU.mult, ALU.add)
                    op.then_inc(S("ya_added"), 1)

            def body(b, r, conv_on, norm_on, products_on, experts_on):
                u = b * E1
                if products_on:
                    turn(b - 2, r)
                if experts_on:
                    add_first(u, b, 0, r)
                if conv_on:
                    taps(b, r)
                if experts_on:
                    add_first(u + 1, b, 1, 1 - r)
                if norm_on:
                    nrm_apply(b - 1, 1 - r)
                if products_on:
                    mask_products(b - 2, r)
                if experts_on:
                    add_first(u + 2, b, 2, r)
            over_stages(dve, body)
            dve.wait_ge(S("ya_added"), E1 * NB * TPB + ACCC)
            dve.wait_ge(S("silu_done"), NB + CREDIT)
            dve.wait_ge(S("conv_tap"), 12 * NB + CONVC)
            with dve.Fori(0, NB) as b:
                done = 0
                at = {}

                def filters(n):
                    nonlocal done
                    for _ in range(n):
                        if done == FA:
                            return
                        kind, k = FIRS[done]
                        dst = (firs if kind == "s" else firl)[:, bass.ds(b, 1), :].squeeze(1)
                        off = PADV - 2 + k if kind == "s" else k
                        src = vT[:, bass.ds(b, 1), off:off + L].squeeze(1)
                        tap = col("fs" if kind == "s" else "fl", k)
                        if k == 0:
                            op = dve.tensor_scalar(dst, src, tap, None, ALU.mult)
                        else:
                            dve.wait_ge(S("fir"), b * FA + (at[kind] + 1))
                            op = dve.scalar_tensor_tensor(dst, src, tap, dst, ALU.mult, ALU.add)
                        op.then_inc(S("fir"), 1)
                        at[kind] = done
                        done += 1
                dve.wait_ge(S("cs_turned"), b + 1)
                dve.tensor_copy(cs, comb[:, bass.ds(b * TPB, TPB), :]).then_inc(S("cs_ready"), 1)
                for j in range(E2):
                    dve.wait_ge(S("y_mm"), b * E2 + (j + 1 + CREDIT))
                    for q in range(TPB):
                        dst = acc[:, bass.ds(b * TPB + q, 1), :].squeeze(1)
                        weight = comb[:, bass.ds(b * TPB + q, 1), E1 + j:E1 + j + 1].squeeze(1)
                        if j > 0:
                            dve.wait_ge(S("y_added"), b * (TPB * E2) + (TPB * (j - 1) + q + 1 + ACCC))
                        dve.scalar_tensor_tensor(dst, pb[4 + j % 2][:, q * P:(q + 1) * P], weight, dst,
                                                 ALU.mult, ALU.add).then_inc(S("y_added"), 1)
                    filters(-(-FA // E2))
                dve.wait_ge(S("bias_mm"), b + (1 + CREDIT))
                dve.wait_ge(S("y_added"), b * (TPB * E2) + (TPB * E2 + ACCC))
                dst = acc[:, bass.ds(b * TPB, TPB), :]
                dve.tensor_tensor(dst, dst, pb[7][:, :].rearrange("p (q d) -> p q d", q=TPB),
                                  ALU.add).then_inc(S("bias_added"), 1)
                assert done == FA
            dve.wait_ge(S("y_mm"), E2 * NB + CREDIT)
            dve.wait_ge(S("bias_added"), NB + 1)
            dve.wait_ge(S("inv_ready"), 1)
            dve.memset(S4, 0.0).then_inc(S("sc_s4"), 1)
            dve.memset(Sb, 0.0).then_inc(S("sc_sb"), 1)

            def spread(dst, src):
                return dve.tensor_tensor(dst.rearrange("p b (h c) -> p b h c", h=H),
                                         src.unsqueeze(2).to_broadcast([P, NB, H, C]),
                                         blocks4.unsqueeze(1).to_broadcast([P, NB, H, C]), ALU.mult)

            def add_expert(v, b, e, r):
                dve.wait_ge(S("yb_mm"), v + 1 + CREDIT)
                if e > EA:
                    dve.wait_ge(S("yb_added"), v * TPB - (TPB * (NB - 1) - ACCC))
                for q in range(TPB):
                    dst = acc[:, bass.ds(b * TPB + q, 1), :].squeeze(1)
                    weight = comb[:, bass.ds(b * TPB + q, 1), e:e + 1].squeeze(1)
                    dve.scalar_tensor_tensor(dst, pb[4 + r][:, q * P:(q + 1) * P], weight, dst,
                                             ALU.mult, ALU.add).then_inc(S("yb_added"), 1)

            def add_taps(v, b, e):
                dst = firl[:, bass.ds(b, 1), :].squeeze(1)
                for j in range(FB):
                    if j > 0:
                        dve.wait_ge(S("firb"), v * FB + j)
                    elif e > EA:
                        dve.wait_ge(S("firb"), v * FB - FB * (NB - 1))
                    k = FIRS[FA + (e - EA) * FB + j][1]
                    dve.scalar_tensor_tensor(dst, vT[:, bass.ds(b, 1), k:k + L].squeeze(1), col("fl", k), dst,
                                             ALU.mult, ALU.add).then_inc(S("firb"), 1)

            def step(n, v, i, e):
                add_expert(v, i * 2, e, 0)
                dve.wait_ge(S("sc_u4"), n + 1)
                dve.wait_ge(S("sc_o"), n + 1)
                spread(Ub, U4).then_inc(S("sc_ub"), 1)
                add_taps(v, i * 2, e)
                add_expert(v + 1, i * 2 + 1, e, 1)
                dve.wait_ge(S("sc_s4"), n + 2)
                dve.wait_ge(S("sc_o"), n + 2)
                spread(Sb, S4).then_inc(S("sc_sb"), 1)
                add_taps(v + 1, i * 2 + 1, e)
            dve.wait_ge(S("fir"), FA * NB)
            over_steps(dve, step)
            paths = [firs, firl, dT, vtok]
            b3 = [P, TPB, H, 3]

            def gate_logits(b):
                tiles = bass.ds(b * TPB, TPB)
                dve.wait_ge(S("fl_mm"), b + 1 + CREDIT)
                dve.tensor_tensor(lg[:, tiles].rearrange("p t h c -> p t (h c)"),
                                  pb[2][:, 0:64].rearrange("p (q n) -> p q n", q=TPB),
                                  rows[:, 0:16].unsqueeze(1).to_broadcast([P, TPB, 16]),
                                  ALU.add).then_inc(S("fl_done"), 1)
                dve.wait_ge(S("fl_done"), b + 2)
                dve.tensor_tensor(others, lg[:, tiles, :, 0:3],
                                  itau.unsqueeze(1).unsqueeze(3).to_broadcast(b3), ALU.mult).then_inc(S("fg"), 1)
                dve.wait_ge(S("fg"), b * FG + 1)
                dve.tensor_reduce(osum, others, AX.X, ALU.max).then_inc(S("fg"), 1)
                dve.wait_ge(S("fg"), b * FG + 2)
                dve.tensor_tensor(others, others, osum.unsqueeze(3).to_broadcast(b3), ALU.subtract).then_inc(S("fg"), 1)

            def gate_weights(b):
                tiles = bass.ds(b * TPB, TPB)
                dve.wait_ge(S("fg_e"), 2 * b + 2)
                dve.tensor_reduce(osum, others, AX.X, ALU.add).then_inc(S("fg"), 1)
                dve.tensor_scalar(pval, pval, 1.0, None, ALU.add).then_inc(S("fg"), 1)
                dve.wait_ge(S("fg"), b * FG + 5)
                dve.reciprocal(osum, osum).then_inc(S("fg"), 1)
                dve.reciprocal(pval, pval).then_inc(S("fg"), 1)
                dve.wait_ge(S("fg"), b * FG + 7)
                dve.tensor_scalar(pscale, pval, MAX_FLOOR - MIN_FLOOR, 1.0 - MAX_FLOOR, ALU.mult,
                                  ALU.add).then_inc(S("fg"), 1)
                dve.wait_ge(S("fg"), b * FG + 8)
                pv = PG[:, tiles, 3, :]
                dve.tensor_tensor(pv, pscale, pval, ALU.mult).then_inc(S("fg"), 1)
                dve.wait_ge(S("fg"), b * FG + 9)
                dve.tensor_scalar(pscale, pv, -1.0, 1.0, ALU.mult, ALU.add).then_inc(S("fg"), 1)
                dve.wait_ge(S("fg"), b * FG + 10)
                dve.tensor_tensor(pscale, pscale, osum, ALU.mult).then_inc(S("fg"), 1)
                dve.wait_ge(S("fg"), b * FG + 11)
                dve.tensor_tensor(PG[:, tiles, 0:3, :], others.rearrange("p t h c -> p t c h"),
                                  pscale.unsqueeze(2).to_broadcast([P, TPB, 3, H]), ALU.mult).then_inc(S("pg_ready"), 1)

            def weigh(b):
                dve.wait_ge(S("fp_mm"), b + 1 + CREDIT)
                dve.wait_ge(S("fz_add"), 3 * (b + 1))
                for c in range(4):
                    dve.tensor_tensor(mC[:, c], pb[3 + c][:, :], paths[c][:, bass.ds(b, 1), :].squeeze(1),
                                      ALU.mult).then_inc(S("fz_mul"), 1)

            def rms_norm(b, r):
                dve.wait_ge(S("fz_rt"), b + 2)
                dve.reciprocal(rr, rr).then_inc(S("fz_rec"), 1)
                dve.wait_ge(S("fz_rec"), b + 1)
                dve.wait_ge(S("fz_wo"), b + 1)
                dve.scalar_tensor_tensor(oN, oT[:, r], col("nw"), rr, ALU.mult, ALU.mult).then_inc(S("fz_n"), 1)

            def gated_residual(b):
                dve.wait_ge(S("fz_wo"), b + 2)
                dve.wait_ge(S("x1_done"), b + 1)
                ga = acc[:, bass.ds(b * TPB, TPB), :]
                dve.tensor_tensor(sgt, pb[7][:, :].rearrange("p (q d) -> p q d", q=TPB), ga,
                                  ALU.mult).then_inc(S("fz_sg"), 1)
                dve.wait_ge(S("fz_sg"), b + 2)
                dve.wait_ge(S("ld_xr"), (b + 1) * 16)
                dve.tensor_tensor(ga, sgt, xr, ALU.add).then_inc(S("x1_done"), 1)
                dve.wait_ge(S("x1_done"), b + 2)
                for q in range(TPB):
                    op = dve.bn_stats(stats[:, bass.ds(b * TPB + q, 1), :].squeeze(1),
                                      acc[:, bass.ds(b * TPB + q, 1), :].squeeze(1))
                op.then_inc(S("ln2_v"), 1)

            def body(b, r, gate, paths_on, out_on, _):
                if paths_on:
                    gate_weights(b - 1)
                if out_on:
                    rms_norm(b - 2, r)
                if paths_on:
                    weigh(b - 1)
                if gate:
                    gate_logits(b)
                if out_on:
                    gated_residual(b - 2)
            dve.wait_ge(S("itau"), 1)
            dve.wait_ge(S("g_ready"), 1)
            over_stages(dve, body)
            vector_layer1(dve)


def kernel(**inputs):
    import concourse.bacc as bacc
    from concourse.bass_utils import run_bass_kernel_spmd

    g = {k: np.asarray(v) for k, v in inputs.items()}
    A, F, A1, F1 = "L0_attn_", "L0_ffn_", "L1_attn_", "L1_ffn_"
    b1 = np.concatenate([g[F + "b1"], g[F + "bs1"][None]], 0)
    small = np.concatenate([
        g[A + "conv_w_q"], g[A + "conv_w_k"], g[A + "conv_w_v"],
        g[A + "fir_short_w"].reshape(P, 3), g[A + "fir_long_w"].reshape(P, 31),
        g[A + "b_fuse1"].reshape(2, P).T, np.tile(g[A + "norm_w"], H)[:, None],
        b1.reshape(NX * MB, P).T, g[A1 + "bq"][:, None], g[A1 + "bk"][:, None],
        g[F1 + "bn_gamma"][:, None], g[F1 + "bn_beta"][:, None]], 1)
    laid = {
        "x": g[A + "hidden_states"].reshape(TOK, D), "con": shape_constants(), "small": small,
        "bf2": g[A + "b_fuse2"], "tau": g[A + "others_log_tau"], "gb": g[F + "gate_b"],
        "Wq": g[A + "W_q"], "Wk": g[A + "W_k"], "Wv": g[A + "W_v"], "Wb": g[A + "W_b"], "gw": g[F + "gate_w"],
        "Wo": g[A + "W_o"], "Wf1": g[A + "W_fuse1"], "Wf2": g[A + "W_fuse2"],
        "b2": g[F + "b2"], "bs2": g[F + "bs2"][None], "w1": g[F + "w1"], "ws1": g[F + "ws1"],
        "w2": g[F + "w2"], "ws2": g[F + "ws2"],
        "aWq": g[A1 + "Wq"].T, "aWk": g[A1 + "Wk"].T,
        "wqk": g[F1 + "w_q"].reshape(2, PH, P, D).transpose(2, 0, 1, 3),
        "keys": g[F1 + "keys_p"].transpose(3, 2, 0, 1),
        "down": g[F1 + "down"][:NE].T, "up": g[F1 + "up"][:NE],
    }
    laid = {"in_" + k: np.ascontiguousarray(v) for k, v in laid.items()}
    nc = bacc.Bacc("TRN2", target_bir_lowering=False, num_devices=1)
    aps = {k[3:]: nc.dram_tensor(k, v.shape, F32, kind="ExternalInput").ap() for k, v in laid.items()}
    out = nc.dram_tensor("out", (TOK, D), F32, kind="ExternalOutput").ap()
    gated_two_layer_kernel(nc, aps, out)
    r = run_bass_kernel_spmd(nc, [laid], core_ids=[0])
    return r.results[0]["out"].reshape(NB, L, D)
```
